# Optimizing a Trainium2 kernel written in Bass

```python
import numpy as np
import jax
import jax.numpy as jnp

def _softmax(x, axis=-1):
    return jax.nn.softmax(x, axis=axis)

def _gelu(x):
    return jax.nn.gelu(x, approximate=True)

def _silu(x):
    return jax.nn.silu(x)

def _sigmoid(x):
    return jax.nn.sigmoid(x)

def _layernorm(x, axis=-1, eps=1e-05):
    m = jnp.mean(x, axis=axis, keepdims=True)
    v = jnp.var(x, axis=axis, keepdims=True)
    return (x - m) / jnp.sqrt(v + eps)

def _scatter_add(tgt, idx, src, axis=0):
    return tgt.at[idx].add(src)

def _segment_sum(src, seg, n):
    return jax.ops.segment_sum(src, seg, n)
kernel_name = 'mk_adaln_d2_jaxref_r8_d2183a'

def setup_inputs(seed: int=0):
    np.random.seed(seed)
    _w = jnp.asarray

    def _L0_attn_setup():
        import jax, jax.numpy as jnp
        import numpy as np
        B, L, D_MODEL = (2, 512, 128)
        D_STATE, D_CONV, EXPAND, HEADDIM = (128, 4, 2, 64)
        D_INNER = EXPAND * D_MODEL
        NHEADS = D_INNER // HEADDIM
        CONV_DIM = D_INNER + 2 * D_STATE
        D_IN_PROJ = 2 * D_INNER + 2 * D_STATE + NHEADS
        CHUNK = 128
        EPS = 1e-05

        def _segsum(a):
            T = a.shape[-1]
            cs = jnp.cumsum(a, axis=-1)
            seg = cs[..., :, None] - cs[..., None, :]
            mask = jnp.tril(jnp.ones((T, T), dtype=bool))
            return jnp.where(mask, seg, -jnp.inf)

        def _forward(x, norm_w, norm_b, in_proj_w, conv_w, conv_b, dt_bias, A_log, D, rms_w, out_proj_w):
            b, l, _ = x.shape
            mu = jnp.mean(x, -1, keepdims=True)
            var = jnp.mean(jnp.square(x - mu), -1, keepdims=True)
            xn = (x - mu) * jax.lax.rsqrt(var + EPS) * norm_w + norm_b
            zxbcdt = xn @ in_proj_w.T
            z = zxbcdt[..., :D_INNER]
            xBC = zxbcdt[..., D_INNER:D_INNER + CONV_DIM]
            dt = jax.nn.softplus(zxbcdt[..., -NHEADS:] + dt_bias)
            xc = jnp.pad(xBC.transpose(0, 2, 1), ((0, 0), (0, 0), (D_CONV - 1, 0)))
            xc = jax.lax.conv_general_dilated(xc, conv_w[:, None, :], (1,), 'VALID', feature_group_count=CONV_DIM, dimension_numbers=('NCH', 'OIH', 'NCH'))
            xBC = jax.nn.silu(xc + conv_b[None, :, None]).transpose(0, 2, 1)
            xs = xBC[..., :D_INNER].reshape(b, l, NHEADS, HEADDIM)
            Bm = xBC[..., D_INNER:D_INNER + D_STATE]
            Cm = xBC[..., D_INNER + D_STATE:]
            A = -jnp.exp(A_log)
            a = dt * A
            X = xs * dt[..., None]
            c = l // CHUNK
            a_c = a.reshape(b, c, CHUNK, NHEADS).transpose(0, 3, 1, 2)
            a_cum = jnp.cumsum(a_c, -1)
            Lmat = jnp.exp(_segsum(a_c))
            Xc = X.reshape(b, c, CHUNK, NHEADS, HEADDIM)
            Bc = Bm.reshape(b, c, CHUNK, D_STATE)
            Cc = Cm.reshape(b, c, CHUNK, D_STATE)
            Y_diag = jnp.einsum('bcln,bcsn,bhcls,bcshp->bclhp', Cc, Bc, Lmat, Xc)
            decay_states = jnp.exp(a_cum[..., -1:] - a_cum)
            states = jnp.einsum('bcln,bhcl,bclhp->bchpn', Bc, decay_states, Xc)
            states = jnp.concatenate([jnp.zeros_like(states[:, :1]), states], axis=1)
            chunk_decay = jnp.exp(_segsum(jnp.pad(a_cum[..., -1], ((0, 0), (0, 0), (1, 0)))))
            prev = jnp.einsum('bhzc,bchpn->bzhpn', chunk_decay, states)[:, :-1]
            Y_off = jnp.einsum('bcln,bchpn,bhcl->bclhp', Cc, prev, jnp.exp(a_cum))
            y = (Y_diag + Y_off).reshape(b, l, NHEADS, HEADDIM) + D[None, None, :, None] * xs
            y = y.reshape(b, l, D_INNER)
            y = y * jax.nn.silu(z)
            y = y * jax.lax.rsqrt(jnp.mean(jnp.square(y), -1, keepdims=True) + EPS) * rms_w
            return x + y @ out_proj_w.T
        key = jax.random.key(seed)
        ks = jax.random.split(key, 8)
        return {'x': jax.random.normal(ks[0], (B, L, D_MODEL), jnp.float32), 'norm_w': jnp.ones((D_MODEL,), jnp.float32), 'norm_b': jnp.zeros((D_MODEL,), jnp.float32), 'in_proj_w': 0.02 * jax.random.normal(ks[1], (D_IN_PROJ, D_MODEL), jnp.float32), 'conv_w': 0.2 * jax.random.normal(ks[2], (CONV_DIM, D_CONV), jnp.float32), 'conv_b': jnp.zeros((CONV_DIM,), jnp.float32), 'dt_bias': jax.random.uniform(ks[3], (NHEADS,), jnp.float32, -4.0, 0.0), 'A_log': jnp.log(jax.random.uniform(ks[4], (NHEADS,), jnp.float32, 1.0, 16.0)), 'D': jnp.ones((NHEADS,), jnp.float32), 'rms_w': jnp.ones((D_INNER,), jnp.float32), 'out_proj_w': 0.02 * jax.random.normal(ks[5], (D_MODEL, D_INNER), jnp.float32)}
    _L0_attn_in = _L0_attn_setup()

    def _L0_ffn_setup():
        import jax, jax.numpy as jnp
        import numpy as np
        D = 128
        H = 128
        E = 8
        K = 2
        I = 2 * 128
        ROUTE_SCALE = 1.0
        key = jax.random.key(seed)
        ks = jax.random.split(key, 12)
        s = lambda *sh: 1.0 / np.sqrt(sh[-1])
        return {'x': jax.random.normal(ks[0], (1, 256, D), jnp.float32), 'gate_w': jax.random.normal(ks[1], (E, D), jnp.float32) * s(E, D), 'w1': jax.random.normal(ks[2], (E, H, D), jnp.float32) * s(H, D), 'b1': jax.random.normal(ks[3], (E, H), jnp.float32) * 0.01, 'w2': jax.random.normal(ks[4], (E, D, H), jnp.float32) * s(D, H), 'b2': jax.random.normal(ks[5], (E, D), jnp.float32) * 0.01, 'w3': jax.random.normal(ks[6], (E, H, D), jnp.float32) * s(H, D), 'b3': jax.random.normal(ks[7], (E, H), jnp.float32) * 0.01, 'sw1': jax.random.normal(ks[8], (I, D), jnp.float32) * s(I, D), 'sw2': jax.random.normal(ks[9], (I, D), jnp.float32) * s(I, D), 'sw3': jax.random.normal(ks[10], (D, I), jnp.float32) * s(D, I)}
    _L0_ffn_in = _L0_ffn_setup()
    _L0_c = _w((lambda *s: np.random.randn(*s).astype(np.float32) * 0.05)(4, 128))
    _L0_wmod = _w((lambda *s: np.random.randn(*s).astype(np.float32) * 0.05)(128, 6 * 128) * 128 ** (-0.5))

    def _L1_attn_setup():
        import jax, jax.numpy as jnp
        import numpy as np
        D_MODEL = 128
        NUM_HEADS = 16
        D_K = D_MODEL // NUM_HEADS
        ROPE_THETA = 10000.0

        def apply_rope(x, theta=ROPE_THETA):
            S, d = (x.shape[-2], x.shape[-1])
            pos = jnp.arange(S, dtype=x.dtype)
            inv_freq = theta ** (-jnp.arange(0, d, 2, dtype=x.dtype) / d)
            ang = pos[:, None] * inv_freq[None, :]
            cos, sin = (jnp.cos(ang), jnp.sin(ang))
            x1, x2 = (x[..., 0::2], x[..., 1::2])
            o1 = x1 * cos - x2 * sin
            o2 = x1 * sin + x2 * cos
            return jnp.stack([o1, o2], axis=-1).reshape(x.shape)
        key = jax.random.key(seed)
        ks = jax.random.split(key, 5)
        B, S, D = (2, 256, D_MODEL)
        x = jax.random.normal(ks[0], (B, S, D), dtype=jnp.float32)
        scale = 0.02
        W_q = jax.random.normal(ks[1], (D, D), dtype=jnp.float32) * scale
        W_k = jax.random.normal(ks[2], (D, D), dtype=jnp.float32) * scale
        W_v = jax.random.normal(ks[3], (D, D), dtype=jnp.float32) * scale
        W_o = jax.random.normal(ks[4], (D, D), dtype=jnp.float32) * scale
        return {'x': x, 'W_q': W_q, 'W_k': W_k, 'W_v': W_v, 'W_o': W_o}
    _L1_attn_in = _L1_attn_setup()

    def _L1_ffn_setup():
        import jax, jax.numpy as jnp
        import numpy as np
        D_MODEL = 128
        HIDDEN = 512
        N_EXPERTS = 8
        TOP_K = 2
        key = jax.random.key(seed)
        k_x, k_r, k_w1, k_w2 = jax.random.split(key, 4)
        x = jax.random.normal(k_x, (2, 128, D_MODEL), dtype=jnp.float32)
        Wr = jax.random.normal(k_r, (D_MODEL, N_EXPERTS), dtype=jnp.float32) * 0.02
        W1 = jax.random.normal(k_w1, (N_EXPERTS, D_MODEL, HIDDEN), dtype=jnp.float32) * 0.02
        W2 = jax.random.normal(k_w2, (N_EXPERTS, HIDDEN, D_MODEL), dtype=jnp.float32) * 0.02
        return {'x': x, 'Wr': Wr, 'W1': W1, 'W2': W2}
    _L1_ffn_in = _L1_ffn_setup()
    _L1_c = _w((lambda *s: np.random.randn(*s).astype(np.float32) * 0.05)(4, 128))
    _L1_wmod = _w((lambda *s: np.random.randn(*s).astype(np.float32) * 0.05)(128, 6 * 128) * 128 ** (-0.5))
    _d = {'L0_attn_x': _L0_attn_in['x'], 'L0_attn_norm_w': _L0_attn_in['norm_w'], 'L0_attn_norm_b': _L0_attn_in['norm_b'], 'L0_attn_in_proj_w': _L0_attn_in['in_proj_w'], 'L0_attn_conv_w': _L0_attn_in['conv_w'], 'L0_attn_conv_b': _L0_attn_in['conv_b'], 'L0_attn_dt_bias': _L0_attn_in['dt_bias'], 'L0_attn_A_log': _L0_attn_in['A_log'], 'L0_attn_D': _L0_attn_in['D'], 'L0_attn_rms_w': _L0_attn_in['rms_w'], 'L0_attn_out_proj_w': _L0_attn_in['out_proj_w'], 'L0_ffn_gate_w': _L0_ffn_in['gate_w'], 'L0_ffn_w1': _L0_ffn_in['w1'], 'L0_ffn_b1': _L0_ffn_in['b1'], 'L0_ffn_w2': _L0_ffn_in['w2'], 'L0_ffn_b2': _L0_ffn_in['b2'], 'L0_ffn_w3': _L0_ffn_in['w3'], 'L0_ffn_b3': _L0_ffn_in['b3'], 'L0_ffn_sw1': _L0_ffn_in['sw1'], 'L0_ffn_sw2': _L0_ffn_in['sw2'], 'L0_ffn_sw3': _L0_ffn_in['sw3'], 'L0_c': _L0_c, 'L0_wmod': _L0_wmod, 'L1_attn_W_q': _L1_attn_in['W_q'], 'L1_attn_W_k': _L1_attn_in['W_k'], 'L1_attn_W_v': _L1_attn_in['W_v'], 'L1_attn_W_o': _L1_attn_in['W_o'], 'L1_ffn_Wr': _L1_ffn_in['Wr'], 'L1_ffn_W1': _L1_ffn_in['W1'], 'L1_ffn_W2': _L1_ffn_in['W2'], 'L1_c': _L1_c, 'L1_wmod': _L1_wmod}
    _x0 = _d['L0_attn_x']
    _d['L0_attn_x'] = jax.random.normal(jax.random.fold_in(jax.random.key(seed), 1), (4, 512, 128), dtype=_x0.dtype)
    del _x0
    return _d

def reference(L0_attn_x, L0_attn_norm_w, L0_attn_norm_b, L0_attn_in_proj_w, L0_attn_conv_w, L0_attn_conv_b, L0_attn_dt_bias, L0_attn_A_log, L0_attn_D, L0_attn_rms_w, L0_attn_out_proj_w, L0_ffn_gate_w, L0_ffn_w1, L0_ffn_b1, L0_ffn_w2, L0_ffn_b2, L0_ffn_w3, L0_ffn_b3, L0_ffn_sw1, L0_ffn_sw2, L0_ffn_sw3, L0_c, L0_wmod, L1_attn_W_q, L1_attn_W_k, L1_attn_W_v, L1_attn_W_o, L1_ffn_Wr, L1_ffn_W1, L1_ffn_W2, L1_c, L1_wmod):

    def _L0_attn_ref(x, norm_w, norm_b, in_proj_w, conv_w, conv_b, dt_bias, A_log, D, rms_w, out_proj_w):
        import jax, jax.numpy as jnp
        import numpy as np
        B, L, D_MODEL = (2, 512, 128)
        D_STATE, D_CONV, EXPAND, HEADDIM = (128, 4, 2, 64)
        D_INNER = EXPAND * D_MODEL
        NHEADS = D_INNER // HEADDIM
        CONV_DIM = D_INNER + 2 * D_STATE
        D_IN_PROJ = 2 * D_INNER + 2 * D_STATE + NHEADS
        CHUNK = 128
        EPS = 1e-05

        def _segsum(a):
            T = a.shape[-1]
            cs = jnp.cumsum(a, axis=-1)
            seg = cs[..., :, None] - cs[..., None, :]
            mask = jnp.tril(jnp.ones((T, T), dtype=bool))
            return jnp.where(mask, seg, -jnp.inf)

        def _forward(x, norm_w, norm_b, in_proj_w, conv_w, conv_b, dt_bias, A_log, D, rms_w, out_proj_w):
            b, l, _ = x.shape
            mu = jnp.mean(x, -1, keepdims=True)
            var = jnp.mean(jnp.square(x - mu), -1, keepdims=True)
            xn = (x - mu) * jax.lax.rsqrt(var + EPS) * norm_w + norm_b
            zxbcdt = xn @ in_proj_w.T
            z = zxbcdt[..., :D_INNER]
            xBC = zxbcdt[..., D_INNER:D_INNER + CONV_DIM]
            dt = jax.nn.softplus(zxbcdt[..., -NHEADS:] + dt_bias)
            xc = jnp.pad(xBC.transpose(0, 2, 1), ((0, 0), (0, 0), (D_CONV - 1, 0)))
            xc = jax.lax.conv_general_dilated(xc, conv_w[:, None, :], (1,), 'VALID', feature_group_count=CONV_DIM, dimension_numbers=('NCH', 'OIH', 'NCH'))
            xBC = jax.nn.silu(xc + conv_b[None, :, None]).transpose(0, 2, 1)
            xs = xBC[..., :D_INNER].reshape(b, l, NHEADS, HEADDIM)
            Bm = xBC[..., D_INNER:D_INNER + D_STATE]
            Cm = xBC[..., D_INNER + D_STATE:]
            A = -jnp.exp(A_log)
            a = dt * A
            X = xs * dt[..., None]
            c = l // CHUNK
            a_c = a.reshape(b, c, CHUNK, NHEADS).transpose(0, 3, 1, 2)
            a_cum = jnp.cumsum(a_c, -1)
            Lmat = jnp.exp(_segsum(a_c))
            Xc = X.reshape(b, c, CHUNK, NHEADS, HEADDIM)
            Bc = Bm.reshape(b, c, CHUNK, D_STATE)
            Cc = Cm.reshape(b, c, CHUNK, D_STATE)
            Y_diag = jnp.einsum('bcln,bcsn,bhcls,bcshp->bclhp', Cc, Bc, Lmat, Xc)
            decay_states = jnp.exp(a_cum[..., -1:] - a_cum)
            states = jnp.einsum('bcln,bhcl,bclhp->bchpn', Bc, decay_states, Xc)
            states = jnp.concatenate([jnp.zeros_like(states[:, :1]), states], axis=1)
            chunk_decay = jnp.exp(_segsum(jnp.pad(a_cum[..., -1], ((0, 0), (0, 0), (1, 0)))))
            prev = jnp.einsum('bhzc,bchpn->bzhpn', chunk_decay, states)[:, :-1]
            Y_off = jnp.einsum('bcln,bchpn,bhcl->bclhp', Cc, prev, jnp.exp(a_cum))
            y = (Y_diag + Y_off).reshape(b, l, NHEADS, HEADDIM) + D[None, None, :, None] * xs
            y = y.reshape(b, l, D_INNER)
            y = y * jax.nn.silu(z)
            y = y * jax.lax.rsqrt(jnp.mean(jnp.square(y), -1, keepdims=True) + EPS) * rms_w
            return x + y @ out_proj_w.T
        return _forward(x, norm_w, norm_b, in_proj_w, conv_w, conv_b, dt_bias, A_log, D, rms_w, out_proj_w)

    def _L0_ffn_ref(x, gate_w, w1, b1, w2, b2, w3, b3, sw1, sw2, sw3):
        import jax, jax.numpy as jnp
        import numpy as np
        D = 128
        H = 128
        E = 8
        K = 2
        I = 2 * 128
        ROUTE_SCALE = 1.0
        B, S, _ = x.shape
        xt = x.reshape(-1, D)
        logits = xt @ gate_w.T
        scores = jax.nn.softmax(logits.astype(jnp.float32), axis=-1)
        top_vals, idx = jax.lax.top_k(scores, K)
        weights = jnp.take_along_axis(scores, idx, axis=1).astype(x.dtype) * ROUTE_SCALE
        xs = xt[:, None, :] * weights[:, :, None]
        y = jnp.zeros_like(xt)
        for e in range(E):
            mask = (idx == e).astype(x.dtype)
            h = jax.nn.silu(jnp.einsum('tkd,hd->tkh', xs, w1[e]) + b1[e])
            x2 = jnp.einsum('tkh,dh->tkd', h, w2[e]) + b2[e]
            x3 = jnp.einsum('tkd,hd->tkh', xs, w3[e]) + b3[e]
            y = y + jnp.sum(x2 * x3 * mask[:, :, None], axis=1)
        z = jax.nn.silu(xt @ sw1.T) * (xt @ sw2.T) @ sw3.T
        return (y + z).reshape(B, S, D)

    def _L1_attn_ref(x, W_q, W_k, W_v, W_o):
        import jax, jax.numpy as jnp
        import numpy as np
        D_MODEL = 128
        NUM_HEADS = 16
        D_K = D_MODEL // NUM_HEADS
        ROPE_THETA = 10000.0

        def apply_rope(x, theta=ROPE_THETA):
            S, d = (x.shape[-2], x.shape[-1])
            pos = jnp.arange(S, dtype=x.dtype)
            inv_freq = theta ** (-jnp.arange(0, d, 2, dtype=x.dtype) / d)
            ang = pos[:, None] * inv_freq[None, :]
            cos, sin = (jnp.cos(ang), jnp.sin(ang))
            x1, x2 = (x[..., 0::2], x[..., 1::2])
            o1 = x1 * cos - x2 * sin
            o2 = x1 * sin + x2 * cos
            return jnp.stack([o1, o2], axis=-1).reshape(x.shape)
        B, S, D = x.shape
        H, dk = (NUM_HEADS, D_K)
        q = (x @ W_q.T).reshape(B, S, H, dk).transpose(0, 2, 1, 3)
        k = (x @ W_k.T).reshape(B, S, H, dk).transpose(0, 2, 1, 3)
        v = (x @ W_v.T).reshape(B, S, H, dk).transpose(0, 2, 1, 3)
        q = apply_rope(q)
        k = apply_rope(k)
        scores = jnp.einsum('bhqd,bhkd->bhqk', q, k) / jnp.sqrt(jnp.asarray(dk, x.dtype))
        causal = jnp.tril(jnp.ones((S, S), dtype=bool))
        scores = jnp.where(causal, scores, jnp.asarray(-jnp.inf, x.dtype))
        probs = jax.nn.softmax(scores, axis=-1)
        attn = jnp.einsum('bhqk,bhkd->bhqd', probs, v)
        attn = attn.transpose(0, 2, 1, 3).reshape(B, S, D)
        return attn @ W_o.T

    def _L1_ffn_ref(x, Wr, W1, W2):
        import jax, jax.numpy as jnp
        import numpy as np
        D_MODEL = 128
        HIDDEN = 512
        N_EXPERTS = 8
        TOP_K = 2
        B, S, D = x.shape
        flat = x.reshape(-1, D)
        logits = flat @ Wr
        top_vals, top_idx = jax.lax.top_k(logits, TOP_K)
        weights = jax.nn.softmax(top_vals, axis=-1)
        top1 = top_idx[:, 0]
        w_top1 = weights[:, 0]
        h = jax.nn.gelu(jnp.einsum('td,edh->teh', flat, W1), approximate=False)
        y = jnp.einsum('teh,ehd->ted', h, W2)
        y_sel = jnp.take_along_axis(y, top1[:, None, None], axis=1)[:, 0, :]
        out = (w_top1[:, None] * y_sel).reshape(B, S, D)
        return out
    x = L0_attn_x
    mod = (_silu(L0_c) @ L0_wmod).reshape(L0_c.shape[0], 6, 1, -1)
    sa, ca, ga, sb, cb, gb = (mod[:, 0], mod[:, 1], mod[:, 2], mod[:, 3], mod[:, 4], mod[:, 5])
    ga = (2 * (ga >= 0) - 1) * jnp.maximum(jnp.abs(ga), 0.25)
    gb = (2 * (gb >= 0) - 1) * jnp.maximum(jnp.abs(gb), 0.25)
    h = _layernorm(x, axis=-1) * (1 + ca) + sa
    x = x + ga * _L0_attn_ref(h, L0_attn_norm_w, L0_attn_norm_b, L0_attn_in_proj_w, L0_attn_conv_w, L0_attn_conv_b, L0_attn_dt_bias, L0_attn_A_log, L0_attn_D, L0_attn_rms_w, L0_attn_out_proj_w)
    h = _layernorm(x, axis=-1) * (1 + cb) + sb
    x = x + gb * _L0_ffn_ref(h, L0_ffn_gate_w, L0_ffn_w1, L0_ffn_b1, L0_ffn_w2, L0_ffn_b2, L0_ffn_w3, L0_ffn_b3, L0_ffn_sw1, L0_ffn_sw2, L0_ffn_sw3)
    mod = (_silu(L1_c) @ L1_wmod).reshape(L1_c.shape[0], 6, 1, -1)
    sa, ca, ga, sb, cb, gb = (mod[:, 0], mod[:, 1], mod[:, 2], mod[:, 3], mod[:, 4], mod[:, 5])
    ga = (2 * (ga >= 0) - 1) * jnp.maximum(jnp.abs(ga), 0.25)
    gb = (2 * (gb >= 0) - 1) * jnp.maximum(jnp.abs(gb), 0.25)
    h = _layernorm(x, axis=-1) * (1 + ca) + sa
    x = x + ga * _L1_attn_ref(h, L1_attn_W_q, L1_attn_W_k, L1_attn_W_v, L1_attn_W_o)
    h = _layernorm(x, axis=-1) * (1 + cb) + sb
    x = x + gb * _L1_ffn_ref(h, L1_ffn_Wr, L1_ffn_W1, L1_ffn_W2)
    return x

_drawn_inputs = setup_inputs


def setup_inputs(seed=0):
    import zlib

    import numpy as np

    out = dict(_drawn_inputs(seed))
    spreads = {'L0_attn_norm_w': (1.0, 0.6),
     'L0_attn_norm_b': (0.0, 0.76),
     'L0_attn_conv_b': (0.0, 0.1),
     'L0_attn_D': (1.0, 0.6),
     'L0_attn_rms_w': (1.0, 0.6)}
    factors = {'L0_attn_dt_bias': 8.0,
     'L0_attn_A_log': 8.0,
     'L0_ffn_b1': 8.0,
     'L0_ffn_b2': 8.0,
     'L0_ffn_b3': 8.0,
     'L1_attn_W_q': 8.0,
     'L1_attn_W_k': 8.0,
     'L1_attn_W_v': 8.0,
     'L1_attn_W_o': 8.0,
     'L1_ffn_Wr': 8.0,
     'L1_ffn_W1': 8.0,
     'L1_ffn_W2': 8.0,
     'L1_c': 8.0,
     'L1_wmod': 8.0}
    for name, (base, spread) in spreads.items():
        noise = np.random.default_rng([zlib.crc32(name.encode()), seed]).standard_normal(out[name].shape)
        drawn = base * np.exp(spread * noise) if base else spread * noise
        out[name] = jnp.asarray(drawn.astype(out[name].dtype))
    for name, factor in factors.items():
        out[name] = (out[name] * factor).astype(out[name].dtype)
    return out
```

```python
from contextlib import ExitStack

import concourse.bass as bass
from concourse import mybir

F32 = mybir.dt.float32
BF16 = mybir.dt.bfloat16
ALU = mybir.AluOpType
ACT = mybir.ActivationFunctionType
AX_X = mybir.AxisListType.X

P = 128
B, S, D = 4, 512, 128
TPB = S // P
NT = B * TPB
NTOK = B * S
EPS = 1e-5
DI, HEADS, HP = 256, 4, 64
TAPS = 4
E0, E1 = 8, 8
HID = 512
NH, DK = 16, 8
QG = NH // 4
PIECES = 6
KR = 2 * PIECES * DK
NBLK = NT + E1 - 1
KM = KR + 6
VW = DK + 1
ATT_SCALE = float(DK) ** -0.5
NEG = -1e30
MOD1_BANK = (5, 6, 7, 1)
Z_BANK = (0, 1, 6, 7)
ROUTE0, ROUTE1, ROUTE2 = 24, 29, 45

PACKS = {
    "mixw": [("cT", 8), ("wmod0", 768), ("wmod1", 768), ("norm_w", 1), ("norm_b", 1), ("in_proj", 772),
             ("conv_w", 16), ("conv_b", 4), ("dt_bias", 4), ("A_log", 4), ("D", 4), ("rms_w", 2),
             ("out_proj", 256)],
    "moe0": [("gate", 8), ("w1", 1024), ("w2", 1024), ("w3", 1024), ("b1", 8), ("b2", 8),
             ("sw1", 256), ("sw2", 256), ("sw3", 256)],
    "attn": [("wq", 128), ("wqs", 128), ("wk", 128), ("wks", 128), ("wv", 128), ("wo", 128)],
    "moe1": [("wr", 8), ("W1", 4096), ("W2", 4096)],
    "const": [("ident", 128), ("tri", 128), ("after", 128), ("cos", 512), ("sin", 512), ("iota", 8),
              ("mask", 512), ("segment", NT * E1), ("full", NT), ("block", NBLK)],
}
BPACK = [("identb", 128), ("causal", 128), ("sel0", 1024), ("sel1", 1024)]


def offsets(fields):
    out, at = {}, 0
    for name, width in fields:
        out[name] = (at, at + width)
        at += width
    return out, at


def adaln_kernel(nc, x_in, mixw_in, moe0_in, attn_in, moe1_in, const_in, b3_in, bconst_in, kones_in, out, stop=9):
    with ExitStack() as ctx:
        def sb(name, shape, dt=F32):
            return ctx.enter_context(nc.sbuf_tensor(name, shape, dt))

        sems = {}

        def sem(name):
            if name not in sems:
                sems[name] = ctx.enter_context(nc.semaphore(name))
            return sems[name]

        ps = ctx.enter_context(nc.psum_tensor("ps", [P, 8, 512], F32))

        w = {}
        packed = {}
        for pack, fields in PACKS.items():
            off, total = offsets(fields)
            if pack == "moe1":
                continue
            t = packed[pack] = sb(pack, [P, total])
            for name, (lo, hi) in off.items():
                w[name] = t[:, lo:hi]
        off, total = offsets(BPACK)
        bconst = sb("bconst", [P, total], BF16)
        for name, (lo, hi) in off.items():
            w[name] = bconst[:, lo:hi]
        ident, identb = w["ident"], w["identb"]

        x = sb("x", [P, NT, D])
        xn = sb("xn", [P, NT, D])
        hT = sb("hT", [P, NTOK])
        siluc = sb("siluc", [P, 8])
        modT = sb("modT", [P, 2, 6, B])
        mod0 = sb("mod0", [P, B, 3 * D])
        mod1 = sb("mod1", [P, B, 4 * D])
        zeros = sb("zeros", [P, D])
        gtmpT = sb("gtmpT", [P, 2, 2, 2, B])
        neghalf = sb("neghalf", [P, NT])
        ones = sb("ones", [P, P])
        LN = 5
        st = sb("st", [P, LN, NT, 6])
        mv = sb("mv", [P, LN, NT, 2])
        rs = sb("rs", [P, LN, NT])
        ARENA = 30720
        arena = sb("arena", [P, ARENA])

        class Area:
            def __init__(self, room, size):
                self.room, self.size, self.at = room, size, 0

            def take(self, n, dt=F32):
                words = n if dt == F32 else n // 2
                v = self.room[:, self.at:self.at + words]
                self.at += words
                assert self.at <= self.size, self.at
                return v if dt == F32 else v.bitcast(dt)

        ar = Area(arena, ARENA)
        xcT = ar.take(4 * NTOK).rearrange("p (c t) -> p c t", c=4)
        acc = ar.take(4 * S).rearrange("p (c t) -> p c t", c=4)
        h = ar.take(NT * D).rearrange("p (t d) -> p t d", d=D)
        sz = ar.take(NT * DI).rearrange("p (t d) -> p t d", d=DI)
        xs = ar.take(NT * DI).rearrange("p (t d) -> p t d", d=DI)
        Bt = ar.take(NT * D).rearrange("p (t d) -> p t d", d=D)
        wor = sb("wor", [P, 2, D])
        eA = sb("eA", [P, HEADS])
        ssq = sb("ssq", [P, NT])
        rr = sb("rr", [P, NT])

        def heads(v):
            return v.rearrange("p (k h s) -> p k h s", k=2, h=HEADS)

        dtv = ar.take(8 * NT * HEADS).rearrange("p (i t h) -> p i t h", i=8, h=HEADS)
        av = ar.take(NT * HEADS).rearrange("p (t h) -> p t h", h=HEADS)
        eact = ar.take(2 * NT * HEADS).rearrange("p (i t h) -> p i t h", i=2, h=HEADS)
        ua = heads(ar.take(2 * HEADS * P))
        L = heads(ar.take(2 * HEADS * P))
        M = heads(ar.take(2 * HEADS * P))
        gtmp = M.rearrange("p k h s -> p k (h s)")
        Gm = ar.take(2 * P).rearrange("p (k s) -> p k s", k=2)
        X = heads(ar.take(2 * DI))
        Xd = heads(ar.take(2 * DI))
        Dx = heads(ar.take(2 * DI))
        prev = heads(ar.take(2 * DI))
        Yo = ar.take(DI).rearrange("p (h s) -> p h s", h=HEADS)
        y = ar.take(2 * DI).rearrange("p (k s) -> p k s", k=2)
        ysq = ar.take(DI)
        yT = ar.take(2 * DI).rearrange("p (k i s) -> p k i s", k=2, i=2)
        o = ar.take(2 * D).rearrange("p (k s) -> p k s", k=2)

        ar = Area(arena, ARENA)
        off, total = offsets(PACKS["moe1"])
        packed["moe1"] = ar.take(total)
        for name, (lo, hi) in off.items():
            w[name] = packed["moe1"][:, lo:hi]
        later = ar.at
        rt = ar.take(12 * NT * 8).rearrange("p (i t e) -> p i t e", i=12, e=8)
        wp = ar.take(NT * P, BF16).rearrange("p (t r) -> p t r", t=NT)
        wT = ar.take(NTOK, BF16)
        xm = ar.take(2 * S).rearrange("p (k t) -> p k t", k=2)
        gT = ar.take(4 * S).rearrange("p (k t) -> p k t", k=4)
        s3 = ar.take(2 * S).rearrange("p (k t) -> p k t", k=2)
        pr = ar.take(2 * S).rearrange("p (k t) -> p k t", k=2)
        yacc = ar.take(NTOK)
        b3f = ar.take(1024)
        b3r = ar.take(1024)
        b3c = ar.take(3 * 1024, BF16).rearrange("p (i c) -> p i c", i=3)
        b3p = sb("b3p", [P, E0, D], BF16)
        top = ar.at
        wtop = sb("wtop", [P, NT])
        ar.at = later
        qaug = ar.take(2 * 8 * S, BF16).rearrange("p (k a t) -> p k a t", k=2, a=8)
        kaug = ar.take(2 * NH * S, BF16).rearrange("p (k a t) -> p k a t", k=2, a=NH)
        va = ar.take(2 * TPB * NH * 32).rearrange("p (k t h d) -> p k t h d", k=2, t=TPB, h=NH)
        used = Area(packed["moe0"], offsets(PACKS["moe0"])[1])
        ropet = used.take(4 * S).rearrange("p (k t) -> p k t", k=4)
        qk = used.take(2 * S).rearrange("p (k t) -> p k t", k=2)
        junk = used.take(2 * S, BF16).rearrange("p (k t) -> p k t", k=2)
        pc = ar.take(6 * S, BF16).rearrange("p (a i t) -> p a i t", a=2, i=3)
        pt = ar.take(3 * 2 * S).rearrange("p (k a t) -> p k a t", k=3, a=2)
        mx = ar.take(2 * 16).rearrange("p (k q j) -> p k q j", k=2, q=4)
        mres = ar.take(16).rearrange("p (q j) -> p q j", q=4)
        mpc = ar.take(2 * 48, BF16).rearrange("p (k q j i) -> p k q j i", k=2, q=4, j=4)
        mT = ar.take(2 * S, BF16).rearrange("p (k t) -> p k t", k=2)
        used = Area(packed["mixw"], offsets(PACKS["mixw"])[1])
        ot = used.take(S)
        rden = ar.take(16).rearrange("p (q j) -> p q j", q=4)
        at = ar.take(TPB * D).rearrange("p (q h d) -> p q h d", q=TPB, h=NH)
        aT = used.take(S)
        ao = used.take(S)
        ar.at = later
        ar.take(12 * NT * 8)
        xb = ar.take(NBLK * D).rearrange("p (j d) -> p j d", d=D)
        xT = ar.take(2 * P).rearrange("p (k s) -> p k s", k=2)
        gs = ar.take(2 * HID).rearrange("p (k h) -> p k h", k=2)
        gsT = ar.take(2 * HID).rearrange("p (k h) -> p k h", k=2)
        ys = ar.take(NBLK * D).rearrange("p (j d) -> p j d", d=D)
        yt = ar.take(NT * D).rearrange("p (t d) -> p t d", d=D)
        dp = ar.take(6 * NT * E1).rearrange("p (i e t) -> p i e t", i=6, e=E1)
        nblk = ar.take(4 * E1).rearrange("p (i e) -> p i e", i=4)
        blk = ar.take(NBLK * E1).rearrange("p (j e) -> p j e", e=E1)
        blk1 = ar.take(NBLK).rearrange("p (j e) -> p j e", e=1)
        expert_at = sb("expert_at", [P, NBLK], mybir.dt.int32)
        pos = ar.take(NT).rearrange("p (t e) -> p t e", e=1)
        posu = sb("posu", [P, NT], mybir.dt.uint32)
        slots_x = nc.dram_tensor("slots_x", (NBLK * P, D), F32, kind="Internal").ap()
        slots_y = nc.dram_tensor("slots_y", (NBLK * P, D), F32, kind="Internal").ap()
        qkd = nc.dram_tensor("qk_parts", (B, 2, P, 3, S), BF16, kind="Internal").ap()

        block = ctx.enter_context(nc.Block())

        FINAL = {1: NT, 2: B, 3: B, 9: B}

        BLOCK_GROUPS = [slice(j, min(j + 6, NBLK)) for j in range(0, NBLK, 6)]

        def modrow(i):
            return mod0[:, :, i * D:(i + 1) * D]

        @block.sync
        def _(sp):
            sp.dma_start(packed["mixw"][:, :], mixw_in).then_inc(sem("ld_mixw"), 16)
            sp.dma_start(x[:, :, :], x_in).then_inc(sem("ld_x"), 16)
            sp.dma_start(packed["const"][:, :], const_in).then_inc(sem("ld_const"), 16)
            sp.dma_start(bconst[:, :], bconst_in).then_inc(sem("ld_bconst"), 16)
            sp.dma_start(packed["moe0"][:, :], moe0_in).then_inc(sem("ld_moe0"), 16)
            sp.dma_start(packed["attn"][:, :], attn_in).then_inc(sem("ld_attn"), 16)
            sp.wait_ge(sem("zeros"), 1)
            sp.dma_start(slots_x.rearrange("(j p) d -> p j d", p=P), zeros[:, :].unsqueeze(1)
                         .to_broadcast([P, NBLK, D])).then_inc(sem("slots_clear"), 16)
            if stop >= 2:
                sp.wait_ge(sem("x1"), NT)
                sp.dma_start(b3f[:, :], b3_in.rearrange("p e d -> p (e d)")).then_inc(sem("ld_b3"), 16)
                sp.dma_start(packed["moe1"][:, :], moe1_in).then_inc(sem("ld_moe1"), 16)
            if stop >= 3:
                sp.wait_ge(sem("kaug_clear"), 1)
                for k in range(2):
                    sp.dma_start(kaug[KR:KM, k, :, :], kones_in).then_inc(sem("k_ones"), 16)

                def relayout(b):
                    sp.wait_ge(sem("parts"), 2 * (b + 1))
                    for a in range(2):
                        sp.dma_start(qkd[b, a], pc[:, a]).then_inc(sem("parts_out"), 16)
                    sp.wait_ge(sem("parts_out"), 32 * (b + 1))
                    if b >= 2:
                        sp.wait_ge(sem("pv"), 8 * 4 * (b - 1))
                    for hh in range(2):
                        for c in range(PIECES):
                            rows = slice((hh * PIECES + c) * DK, (hh * PIECES + c + 1) * DK)
                            for a, (dst, part) in enumerate(((qaug[rows, b % 2, :, :], (0, 0, 0, 1, 1, 2)[c]),
                                                             (kaug[rows, b % 2, hh::2, :], (0, 1, 2, 0, 1, 0)[c]))):
                                src = qkd[b, a, :, part, :].rearrange("(r h d) t -> h d r t", h=2, d=DK)[hh]
                                sp.dma_start(dst, src).then_inc(sem(f"aug{b % 2}"), 16)

                relayout(0)
                relayout(1)
                for s in range(NT):
                    sp.wait_ge(sem("mT"), s + 1)
                    b, g = divmod(s, QG)
                    if g == 0 and b >= 2:
                        sp.wait_ge(sem("pv"), 32 * (b - 1))
                    for i in range(2):
                        sp.dma_start(qaug[KR:KM, b % 2, 2 * g + i, :], mT[6 * i:6 * i + 6, s % 2, :])\
                            .then_inc(sem(f"m_rows{s % 2}"), 16)
                    if s in (5, 9):
                        relayout((s - 1) // 4 + 1)
            if stop < 9:
                sp.wait_ge(sem("x_final"), FINAL[stop])
                sp.dma_start(out, x[:, :, :]).then_inc(sem("stored"), 16)
                sp.wait_ge(sem("stored"), 16)
                return
            sp.wait_ge(sem("scattered"), 16 * NT)
            slots = slots_x.rearrange("(j p) d -> p j d", p=P)
            for c, js in enumerate(BLOCK_GROUPS):
                sp.dma_start(xb[:, js, :], slots[:, js, :]).then_inc(sem(f"ld_blocks{c}"), 16)
            slots = slots_y.rearrange("(j p) d -> p j d", p=P)
            for c, js in enumerate(BLOCK_GROUPS):
                sp.wait_ge(sem("ys"), js.stop)
                sp.dma_start(slots[:, js, :], ys[:, js, :]).then_inc(sem("ys_out"), 16)
            for b in range(B):
                sp.wait_ge(sem("x4"), b + 1)
                ts = slice(TPB * b, TPB * (b + 1))
                sp.dma_start(out[:, ts, :], x[:, ts, :]).then_inc(sem("stored"), 16)
            sp.wait_ge(sem("stored"), 16 * B)

        def ln_stats(v, k, src, b):
            for t in range(TPB * b, TPB * (b + 1)):
                v.bn_stats(st[:, k, t, :], src[:, t, :]).then_inc(sem("ln_stats"), 1)

        def ln_moments(v, k, b):
            v.wait_ge(sem("ln_stats"), NT * k + TPB * (b + 1))
            for t in range(TPB * b, TPB * (b + 1)):
                v.bn_aggr(mv[:, k, t, :], st[:, k, t, :]).then_inc(sem("ln_moments"), 1)

        def ln_rstd(pool, k, b):
            ts = slice(TPB * b, TPB * (b + 1))
            pool.wait_ge(sem("ln_moments"), NT * k + TPB * (b + 1))
            pool.tensor_scalar(rs[:, k, ts], mv[:, k, ts, 1], EPS, None, ALU.add).then_inc(sem("ln_var"), 1)
            pool.wait_ge(sem("ln_var"), B * k + b + 1)
            pool.tensor_tensor(rs[:, k, ts], rs[:, k, ts], neghalf[:, ts], ALU.pow).then_inc(sem("ln_rstd"), 1)

        def ln_apply(v, k, src, dst, b):
            v.wait_ge(sem("ln_rstd"), B * k + b + 1)
            for t in range(TPB * b, TPB * (b + 1)):
                v.tensor_scalar(dst[:, t, :], src[:, t, :], mv[:, k, t, 0:1], rs[:, k, t:t + 1],
                                ALU.subtract, ALU.mult).then_inc(sem("ln_out"), 1)

        @block.gpsimd
        def _(pool):
            pool.memset(neghalf[:, :], -0.5).then_inc(sem("pool_const"), 1)
            pool.memset(ones[:, :], 1.0).then_inc(sem("pool_const"), 1)
            pool.memset(zeros[:, :], 0.0).then_inc(sem("zeros"), 1)
            pool.wait_ge(sem("pool_const"), 2)
            for b in range(B):
                ln_rstd(pool, 0, b)
            for b in range(B):
                ln_rstd(pool, 1, b)
            pool.wait_ge(sem("ld_const"), 16)
            pool.wait_ge(sem("decay_in"), 1)

            def head(t):
                k = t % 2
                if t >= 2:
                    pool.wait_ge(sem("seg_ps"), t - 1)
                for hh in range(HEADS):
                    pool.tensor_scalar(ua[:, k, hh, :], w["after"], av[:, t, hh:hh + 1], None,
                                       ALU.mult).then_inc(sem("ua"), 1)
                if t >= 2:
                    pool.wait_ge(sem("y_ps"), t - 1)
                    pool.wait_ge(sem("y_gated"), t - 1)
                    if (t - 2) % TPB < 3:
                        pool.wait_ge(sem("state_ps"), ((t - 2) // TPB) * 3 + (t - 2) % TPB + 1)
                x3 = xs[:, t, :].rearrange("p (h e) -> p h e", h=HEADS)
                pool.wait_ge(sem("xs_tok"), 3 * (t // TPB + 1))
                pool.tensor_tensor(X[:, k], x3, dtv[:, 7, t, :].unsqueeze(2).to_broadcast([P, HEADS, HP]),
                                   ALU.mult).then_inc(sem("X"), 1)
                pool.tensor_tensor(Dx[:, k], x3, w["D"].unsqueeze(2).to_broadcast([P, HEADS, HP]),
                                   ALU.mult).then_inc(sem("Dx"), 1)
                pool.wait_ge(sem("L"), t + 1)
                pool.wait_ge(sem("X"), t + 1)
                pool.tensor_tensor(Xd[:, k], X[:, k], L[:, k, :, P - 1:P].to_broadcast([P, HEADS, HP]),
                                   ALU.mult).then_inc(sem("Xd"), 1)

            def tail(t):
                pool.wait_ge(sem("ssq"), t + 1)
                pool.tensor_scalar(rr[:, t:t + 1], ssq[:, t:t + 1], 1.0 / DI, EPS, ALU.mult,
                                   ALU.add).then_inc(sem("msq"), 1)
                pool.wait_ge(sem("msq"), t + 1)
                pool.tensor_tensor(rr[:, t:t + 1], rr[:, t:t + 1], neghalf[:, 0:1], ALU.pow).then_inc(sem("rms"), 1)
                pool.wait_ge(sem("o_gated"), t + 1)
                pool.tensor_tensor(x[:, t, :], x[:, t, :], o[:, t % 2, :], ALU.add).then_inc(sem("x1"), 1)

            for t in range(NT + 1):
                if t < NT:
                    head(t)
                if t >= 1:
                    tail(t - 1)
            if stop == 1:
                pool.wait_ge(sem("x1"), NT)
                pool.nop().then_inc(sem("x_final"), NT)
                return

            for b in range(B):
                ln_rstd(pool, 2, b)
            pool.wait_ge(sem("ld_b3"), 16)
            pool.memset(wp[:, :, :], 0.0).then_inc(sem("wp_clear"), 1)
            m = [0]

            def step(ins):
                m[0] += 1
                ins.then_inc(sem("b3_step"), 1)
                pool.wait_ge(sem("b3_step"), m[0])

            step(pool.memset(b3p[:, :, :], 0.0))
            step(pool.tensor_copy(b3c[:, 0], b3f[:, :]))
            step(pool.tensor_tensor(b3r[:, :], b3f[:, :], b3c[:, 0], ALU.subtract))
            step(pool.tensor_copy(b3c[:, 1], b3r[:, :]))
            step(pool.tensor_tensor(b3c[:, 2], b3r[:, :], b3c[:, 1], ALU.subtract))
            for i in range(3):
                rows = slice(32 * (i + 1), 32 * (i + 2))
                step(pool.tensor_copy(b3p[rows].rearrange("p e d -> p (e d)"), b3c[rows, i]))
            for i in range(32):
                n, e = divmod(i, E0)
                ts = slice(n * S, (n + 1) * S)
                pool.wait_ge(sem("pr"), i + 1)
                if e == 0:
                    pool.tensor_copy(yacc[:, ts], pr[:, i % 2, :]).then_inc(sem("yacc"), 1)
                else:
                    pool.wait_ge(sem("yacc"), i)
                    pool.tensor_tensor(yacc[:, ts], yacc[:, ts], pr[:, i % 2, :], ALU.add).then_inc(sem("yacc"), 1)
            if stop == 2:
                pool.wait_ge(sem("x2"), B)
                pool.nop().then_inc(sem("x_final"), B)
                return

            pool.wait_ge(sem("x2"), B)
            pool.memset(kaug[:, :, :, :], 0.0).then_inc(sem("kaug_clear"), 1)
            pool.memset(va[:, :, :, :, :], 0.0).then_inc(sem("va_clear"), 1)
            pool.wait_ge(sem("va_clear"), 1)
            pool.memset(va[:, :, :, :, DK:DK + 1], 1.0).then_inc(sem("va_clear"), 1)
            for b in range(B):
                ln_rstd(pool, 3, b)
            for b in range(B):
                for a in range(2):
                    i = 2 * b + a
                    pool.wait_ge(sem("rope"), 2 * (i + 1))
                    if i >= 2:
                        pool.wait_ge(sem("parts"), i - 1)
                    pool.tensor_tensor(qk[:, a, :], ropet[:, 2 * a, :], ropet[:, 2 * a + 1, :], ALU.add)\
                        .then_inc(sem("qk"), 1)
                    pool.wait_ge(sem("part_hi"), i + 1)
                    pool.tensor_tensor(qk[:, a, :], qk[:, a, :], pc[:, a, 0, :], ALU.subtract).then_inc(sem("res"), 1)
                    pool.wait_ge(sem("part_mid"), i + 1)
                    pool.tensor_tensor(pc[:, a, 2, :], qk[:, a, :], pc[:, a, 1, :], ALU.subtract)\
                        .then_inc(sem("parts"), 1)
            if stop > 3:
                for b in range(B):
                    ln_rstd(pool, 4, b)
                pool.wait_ge(sem("posu"), 1)
                pool.wait_ge(sem("h4"), B)
                pool.wait_ge(sem("slots_clear"), 16)
                for t in range(NT):
                    pool.indirect_dma_start(out=slots_x[:, :], out_offset=bass.IndirectOffsetOnAxis(
                        ap=posu[:, t:t + 1], axis=0), in_=xn[:, t, :], in_offset=None).then_inc(sem("scattered"), 16)
                pool.wait_ge(sem("ys_out"), 16 * len(BLOCK_GROUPS))
                for t in range(NT):
                    pool.indirect_dma_start(out=yt[:, t, :], out_offset=None, in_=slots_y[:, :],
                                            in_offset=bass.IndirectOffsetOnAxis(ap=posu[:, t:t + 1], axis=0))\
                        .then_inc(sem(f"gathered{t // TPB}"), 16)

        @block.scalar
        def _(act):
            act.wait_ge(sem("ld_mixw"), 16)
            act.activation(siluc[:, :], w["cT"], ACT.Silu).then_inc(sem("siluc"), 1)
            for b in range(B):
                act.wait_ge(sem("xnT_ps"), b + 1)
                act.activation(hT[:, b * S:(b + 1) * S], ps[:, 6 + b % 2, :], ACT.Identity,
                               scale=w["norm_w"], bias=w["norm_b"]).then_inc(sem("hT"), 1)
            for b in range(B):
                for c in range(4):
                    act.wait_ge(sem("xbc_ps"), 4 * b + c + 1)
                    if b >= 1:
                        act.wait_ge(sem("xbc_silu"), 4 * (b - 1) + c + 1)
                    act.activation(acc[:, c, :], ps[:, c, :], ACT.Identity, scale=w["conv_w"][:, 4 * c + 3:4 * c + 4],
                                   bias=w["conv_b"][:, c:c + 1]).then_inc(sem("conv_last_tap"), 1)
                for i in range(2):
                    act.wait_ge(sem("z_ps"), 2 * b + i + 1)
                    t = TPB * b + 2 * i
                    act.activation(sz[:, t:t + 2, :], ps[:, 4 + i, :].rearrange("p (a d) -> p a d", a=2),
                                   ACT.Silu).then_inc(sem("sz"), 1)
                for c in range(4):
                    act.wait_ge(sem("conv"), 4 * b + c + 1)
                    act.activation(xcT[:, c, b * S:(b + 1) * S], acc[:, c, :], ACT.Silu).then_inc(sem("xbc_silu"), 1)
            act.wait_ge(sem("dt_nabs"), 1)
            act.activation(dtv[:, 2, :, :], dtv[:, 1, :, :], ACT.Exp).then_inc(sem("dt_exp"), 1)
            act.activation(eA[:, :], w["A_log"], ACT.Exp).then_inc(sem("eA"), 1)
            act.wait_ge(sem("acum_ps"), 1)
            act.activation(eact[:, :, :, :].rearrange("p a t h -> p (a t h)"), ps[:, 7, 0:2 * NT * HEADS],
                           ACT.Exp).then_inc(sem("eact"), 1)

            def head(t):
                k = t % 2
                act.wait_ge(sem("seg_ps"), t + 1)
                if t >= 2:
                    act.wait_ge(sem("M"), t - 1)
                    act.wait_ge(sem("Xd"), t - 1)
                act.activation(L[:, k].rearrange("p h s -> p (h s)"), ps[:, k, :], ACT.Exp).then_inc(sem("L"), 1)

            def tail(t):
                k = t % 2
                act.wait_ge(sem("y_gated"), t + 1)
                if t >= 1:
                    act.wait_ge(sem("ssq"), t)
                act.activation(ysq[:, :], y[:, k, :], ACT.Square, accum_out=ssq[:, t:t + 1]).then_inc(sem("ssq"), 1)
                act.wait_ge(sem("yT_ps"), t + 1)
                if t >= 2:
                    act.wait_ge(sem("o_ps"), t - 1)
                act.activation(yT[:, k].rearrange("p a s -> p (a s)"), ps[:, 6, k * 256:(k + 1) * 256],
                               ACT.Identity).then_inc(sem("yT"), 1)

            for t in range(NT + 1):
                if t < NT:
                    head(t)
                if t >= 1:
                    tail(t - 1)

            if stop == 1:
                return

            def hT_evac(k, layer, scale, bias):
                for b in range(B):
                    act.wait_ge(sem("xnT_ps"), B * (k - 1) + b + 1)
                    act.activation(hT[:, b * S:(b + 1) * S], ps[:, 6 + b % 2, :], ACT.Identity,
                                   scale=modT[:, layer, scale, b:b + 1], bias=modT[:, layer, bias, b:b + 1])\
                        .then_inc(sem("hT"), 1)

            hT_evac(2, 0, 4, 3)
            act.wait_ge(sem("gate_shifted"), 1)
            act.activation(rt[:, 1], rt[:, 0], ACT.Exp).then_inc(sem("gate_exp"), 1)
            for i in range(32):
                n, e = divmod(i, E0)
                act.wait_ge(sem("p1_ps"), i + 1)
                if i >= 2:
                    act.wait_ge(sem("p2_ps"), i - 1)
                act.activation(gT[:, i % 2, :], ps[:, 2 + i % 2, :], ACT.Silu, bias=w["b1"][:, e:e + 1])\
                    .then_inc(sem("h1"), 1)
                act.wait_ge(sem("p3_ps"), i + 1)
                if i >= 2:
                    act.wait_ge(sem("pr"), i - 1)
                act.activation(s3[:, i % 2, :], ps[:, 4 + i % 2, :], ACT.Identity).then_inc(sem("s3"), 1)
            for j in range(8):
                act.wait_ge(sem("sa_ps"), j + 1)
                if j >= 2:
                    act.wait_ge(sem("sg"), j - 1)
                else:
                    act.wait_ge(sem("p2_ps"), 31 + j)
                act.activation(gT[:, j % 2, :], ps[:, 2 + j % 2, :], ACT.Silu).then_inc(sem("sh"), 1)
            if stop == 2:
                return

            hT_evac(3, 1, 1, 0)

            def parts(b):
                for a in range(2):
                    i = 2 * b + a
                    act.wait_ge(sem("qk"), i + 1)
                    if b >= 1:
                        act.wait_ge(sem("parts_out"), 32 * b)
                    act.activation(pc[:, a, 0, :], qk[:, a, :], ACT.Identity).then_inc(sem("part_hi"), 1)
                    act.wait_ge(sem("res"), i + 1)
                    act.activation(pc[:, a, 1, :], qk[:, a, :], ACT.Identity).then_inc(sem("part_mid"), 1)

            def probs(u):
                kt = 3 - (u % 8) // 2
                n = S - kt * P
                k = u % 2
                act.wait_ge(sem("st_ps"), u + 1)
                if u >= 3:
                    act.wait_ge(sem("pv"), u - 2)
                act.activation(pt[:, u % 3, :, 0:n], ps[:, 4 + 2 * k:6 + 2 * k, 0:n], ACT.Exp,
                               scale=ATT_SCALE).then_inc(sem("probs"), 1)

            parts(0)
            parts(1)
            for it in range(-2, 16):
                if it in (4, 8):
                    parts(it // 4 + 1)
                if it >= 0:
                    for i in range(8):
                        probs(8 * it + i)
            if stop == 3:
                return
            for b in range(B):
                act.wait_ge(sem("xnT_ps"), B * 3 + b + 1)
                act.activation(hT[:, b * S:(b + 1) * S], ps[:, 6 + b % 2, :], ACT.Identity).then_inc(sem("hT"), 1)
            act.wait_ge(sem("top_diff"), 1)
            act.activation(rt[:, 10, :, 0], rt[:, 9, :, 0], ACT.Exp).then_inc(sem("top_exp"), 1)
            for j in range(NBLK):
                act.wait_ge(sem("m1_ps"), j + 1)
                if j >= 2:
                    act.wait_ge(sem("gsT_ps"), j - 1)
                act.activation(gs[:, j % 2, :], ps[:, j % 2, :], ACT.Gelu).then_inc(sem("gelu"), 1)

        @block.vector
        def _(v):
            v.wait_ge(sem("ld_x"), 16)
            for b in range(B):
                ln_stats(v, 0, x, b)
            for b in range(B):
                ln_moments(v, 0, b)
            for b in range(B):
                ln_apply(v, 0, x, h, b)
            v.wait_ge(sem("modT_ps"), 1)
            v.tensor_copy(modT[:, :, :, :].rearrange("p l c b -> p (l c b)"), ps[:, 0, 0:48]).then_inc(sem("mod_sb"), 1)
            for b in range(B):
                v.wait_ge(sem("mod0_ps"), b + 1)
                v.tensor_copy(mod0[:, b, :], ps[:, 1 + b, 0:384]).then_inc(sem("mod_sb"), 1)
            for b in range(B):
                v.wait_ge(sem("mod1_ps"), b + 1)
                v.tensor_copy(mod1[:, b, :], ps[:, MOD1_BANK[b], :]).then_inc(sem("mod_sb"), 1)
            v.wait_ge(sem("mod_sb"), 9)
            n = [9]

            def step(ins):
                n[0] += 1
                ins.then_inc(sem("mod_sb"), 1)
                v.wait_ge(sem("mod_sb"), n[0])

            g3 = gtmp[:, :, :].rearrange("p k (b d) -> p k b d", b=B)

            def guard(g, s, a):
                step(v.tensor_scalar(s, g, 0.0, -0.5, ALU.is_ge, ALU.add))
                step(v.scalar_tensor_tensor(out=a, in0=g, scalar=-1.0, in1=g, op0=ALU.mult, op1=ALU.max))
                step(v.scalar_tensor_tensor(out=g, in0=a, scalar=0.25, in1=s, op0=ALU.max, op1=ALU.mult))
                step(v.tensor_scalar(g, g, 2.0, None, ALU.mult))

            step(v.tensor_scalar(modrow(1), modrow(1), 1.0, None, ALU.add))
            guard(modrow(2), g3[:, 0], g3[:, 1])
            guard(mod1[:, :, 0:D], g3[:, 0], g3[:, 1])
            guard(mod1[:, :, 3 * D:4 * D], g3[:, 0], g3[:, 1])
            step(v.tensor_scalar(mod1[:, :, 2 * D:3 * D], mod1[:, :, 2 * D:3 * D], 1.0, None, ALU.add))
            for layer in range(2):
                guard(modT[:, layer, 5, :], gtmpT[:, 0, layer, 0, :], gtmpT[:, 1, layer, 0, :])
                step(v.tensor_scalar(modT[:, layer, 1:5:3, :], modT[:, layer, 1:5:3, :], 1.0, None, ALU.add))
            v.wait_ge(sem("ld_mixw"), 16)
            for i in range(2):
                v.tensor_scalar(wor[:, i, :], w["out_proj"][:, i * D:(i + 1) * D], w["rms_w"][:, i:i + 1], None,
                                ALU.mult).then_inc(sem("wor"), 1)
            v.wait_ge(sem("ln_out"), NT)
            for b in range(B):
                ts = slice(TPB * b, TPB * (b + 1))
                v.tensor_tensor(h[:, ts, :], h[:, ts, :], mod0[:, b, D:2 * D].unsqueeze(1).to_broadcast([P, TPB, D]),
                                ALU.mult).then_inc(sem("h_scaled"), 1)
            for b in range(B):
                ts = slice(TPB * b, TPB * (b + 1))
                v.wait_ge(sem("h_scaled"), b + 1)
                v.tensor_tensor(h[:, ts, :], h[:, ts, :], mod0[:, b, 0:D].unsqueeze(1).to_broadcast([P, TPB, D]),
                                ALU.add).then_inc(sem("h"), 1)
            for b in range(B):
                v.wait_ge(sem("h"), b + 1)
                ln_stats(v, 1, h, b)
            for b in range(B):
                ln_moments(v, 1, b)
            for b in range(B):
                ln_apply(v, 1, h, xn, b)

            def evacuate(b):
                for c in range(3):
                    v.wait_ge(sem("xs_ps"), 3 * b + c + 1)
                    src = ps[:, 6, :].rearrange("p (t d) -> p t d", t=TPB)
                    ts = slice(TPB * b, TPB * (b + 1))
                    dst = xs[:, ts, c * P:(c + 1) * P] if c < 2 else Bt[:, ts, :]
                    v.tensor_copy(dst, src).then_inc(sem("xs_tok"), 1)

            for b in range(B):
                for c in range(4):
                    v.wait_ge(sem("conv_last_tap"), 4 * b + c + 1)
                    for s in range(1, TAPS):
                        ins = v.scalar_tensor_tensor(out=acc[:, c, s:S], in0=ps[:, c, 0:S - s],
                                                     scalar=w["conv_w"][:, 4 * c + 3 - s:4 * c + 4 - s],
                                                     in1=acc[:, c, s:S], op0=ALU.mult, op1=ALU.add)
                        if s < TAPS - 1:
                            ins.then_inc(sem("conv_tap"), 1)
                            v.wait_ge(sem("conv_tap"), 2 * (4 * b + c) + s)
                        else:
                            ins.then_inc(sem("conv"), 1)
                if b >= 1:
                    evacuate(b - 1)
            v.wait_ge(sem("dt_ps"), 1)
            d = [dtv[:, i, :, :] for i in range(8)]
            m = [0]

            def dstep(ins):
                m[0] += 1
                ins.then_inc(sem("dt_step"), 1)
                v.wait_ge(sem("dt_step"), m[0])

            dstep(v.tensor_tensor(d[0], ps[:, 7, 0:NT * HEADS].rearrange("p (t h) -> p t h", t=NT),
                                  w["dt_bias"].unsqueeze(1).to_broadcast([P, NT, HEADS]), ALU.add))
            v.scalar_tensor_tensor(out=d[1], in0=d[0], scalar=-1.0, in1=d[0], op0=ALU.mult,
                                   op1=ALU.min).then_inc(sem("dt_nabs"), 1)
            evacuate(B - 1)
            v.wait_ge(sem("dt_exp"), 1)
            dstep(v.tensor_scalar(d[3], d[2], 2.0, None, ALU.add))
            dstep(v.reciprocal(d[4], d[3]))
            dstep(v.tensor_tensor(d[3], d[2], d[4], ALU.mult))
            dstep(v.tensor_tensor(d[4], d[3], d[3], ALU.mult))
            dstep(v.tensor_scalar(d[5], d[4], 1.0 / 15.0, None, ALU.mult))
            for k in (13, 11, 9, 7, 5, 3):
                dstep(v.scalar_tensor_tensor(out=d[5], in0=d[5], scalar=1.0 / k, in1=d[4], op0=ALU.add, op1=ALU.mult))
            dstep(v.scalar_tensor_tensor(out=d[6], in0=d[5], scalar=1.0, in1=d[3], op0=ALU.add, op1=ALU.mult))
            dstep(v.tensor_scalar(d[5], d[0], 0.0, None, ALU.max))
            dstep(v.scalar_tensor_tensor(out=d[7], in0=d[6], scalar=2.0, in1=d[5], op0=ALU.mult, op1=ALU.add))
            v.wait_ge(sem("eA"), 1)
            v.scalar_tensor_tensor(out=av[:, :, :], in0=d[7], scalar=-1.0,
                                   in1=eA[:, :].unsqueeze(1).to_broadcast([P, NT, HEADS]),
                                   op0=ALU.mult, op1=ALU.mult).then_inc(sem("decay_in"), 1)

            def bc(a):
                return a.unsqueeze(2).to_broadcast([P, HEADS, HP])

            def head(t):
                k = t % 2
                c, b = t % TPB, t // TPB
                v.wait_ge(sem("g_ps"), t + 1)
                v.tensor_tensor(Gm[:, k, :], ps[:, 2, k * P:(k + 1) * P], w["tri"], ALU.mult).then_inc(sem("Gm"), 1)
                v.wait_ge(sem("Gm"), t + 1)
                v.wait_ge(sem("L"), t + 1)
                if t >= 2:
                    v.wait_ge(sem("y_ps"), t - 1)
                v.tensor_tensor(M[:, k], L[:, k], Gm[:, k, :].unsqueeze(1).to_broadcast([P, HEADS, P]),
                                ALU.mult).then_inc(sem("M"), 1)
                if c < TPB - 1:
                    n_st = 3 * b + c
                    stp = ps[:, 5, k * DI:(k + 1) * DI].rearrange("p (h e) -> p h e", h=HEADS)
                    v.wait_ge(sem("state_ps"), n_st + 1)
                    if c == 0:
                        if b >= 1:
                            v.wait_ge(sem("y_ps"), t - 2)
                        v.tensor_copy(prev[:, k], stp).then_inc(sem("prev"), 1)
                    else:
                        v.tensor_tensor(prev[:, k], prev[:, 1 - k], bc(eact[:, 1, t, :]), ALU.mult)\
                            .then_inc(sem("prev_decayed"), 1)
                        v.wait_ge(sem("prev_decayed"), 2 * b + c)
                        v.tensor_tensor(prev[:, k], prev[:, k], stp, ALU.add).then_inc(sem("prev"), 1)

            def tail(t):
                k = t % 2
                c, b = t % TPB, t // TPB
                y3 = y[:, k, :].rearrange("p (h e) -> p h e", h=HEADS)
                yd = ps[:, 3 + k, 0:DI].rearrange("p (h e) -> p h e", h=HEADS)
                yo = ps[:, 3 + k, DI:2 * DI].rearrange("p (h e) -> p h e", h=HEADS)
                v.wait_ge(sem("y_ps"), t + 1)
                v.wait_ge(sem("Dx"), t + 1)
                if t >= 2:
                    v.wait_ge(sem("yT_ps"), t - 1)
                    v.wait_ge(sem("ssq"), t - 1)
                v.tensor_tensor(y3, yd, Dx[:, k], ALU.add).then_inc(sem("y_a"), 1)
                v.wait_ge(sem("y_a"), t + 1)
                if c > 0:
                    v.tensor_tensor(Yo[:, :, :], yo, bc(eact[:, 0, t, :]), ALU.mult).then_inc(sem("y_b"), 1)
                    v.wait_ge(sem("y_b"), 2 * (3 * b + c - 1) + 1)
                    v.tensor_tensor(y3, y3, Yo[:, :, :], ALU.add).then_inc(sem("y_b"), 1)
                    v.wait_ge(sem("y_b"), 2 * (3 * b + c - 1) + 2)
                v.wait_ge(sem("sz"), 2 * (b + 1))
                v.tensor_tensor(y[:, k, :], y[:, k, :], sz[:, t, :], ALU.mult).then_inc(sem("y_gated"), 1)
                v.wait_ge(sem("o_ps"), t + 1)
                v.wait_ge(sem("rms"), t + 1)
                if t >= 2:
                    v.wait_ge(sem("x1"), t - 1)
                v.scalar_tensor_tensor(out=o[:, k, :], in0=ps[:, 7, P * (1 + k):P * (2 + k)], scalar=rr[:, t:t + 1],
                                       in1=h[:, t, :], op0=ALU.mult, op1=ALU.add).then_inc(sem("o_sum"), 1)
                v.wait_ge(sem("o_sum"), t + 1)
                v.tensor_tensor(o[:, k, :], o[:, k, :], mod0[:, b, 2 * D:3 * D], ALU.mult).then_inc(sem("o_gated"), 1)

            v.wait_ge(sem("eact"), 1)
            for t in range(NT + 1):
                if t < NT:
                    head(t)
                if t >= 1:
                    tail(t - 1)

            if stop == 1:
                return

            for b in range(B):
                v.wait_ge(sem("x1"), TPB * (b + 1))
                ln_stats(v, 2, x, b)
                ln_moments(v, 2, b)
            for b in range(B):
                ln_apply(v, 2, x, xn, b)
            q = [rt[:, i] for i in range(12)]
            one = [rt[:, i, :, 0:1] for i in range(12)]
            nr = [0]

            def rstep(ins):
                nr[0] += 1
                ins.then_inc(sem("route"), 1)
                v.wait_ge(sem("route"), nr[0])

            def bc8(a):
                return a.to_broadcast([P, NT, 8])

            iota = w["iota"].unsqueeze(1).to_broadcast([P, NT, 8])

            def first_of_largest(src, top, hot, tmp, tmp1):
                rstep(v.tensor_reduce(top, src, AX_X, ALU.max))
                rstep(v.tensor_tensor(tmp, src, bc8(top), ALU.is_ge))
                rstep(v.tensor_tensor(tmp, tmp, iota, ALU.mult))
                rstep(v.tensor_reduce(tmp1, tmp, AX_X, ALU.max))
                rstep(v.tensor_tensor(hot, tmp, bc8(tmp1), ALU.is_equal))

            logits = ps[:, 5, 0:NT * 8].rearrange("p (t e) -> p t e", e=8)
            v.wait_ge(sem("gate_ps"), 1)
            rstep(v.tensor_reduce(one[2], logits, AX_X, ALU.max))
            v.tensor_tensor(q[0], logits, bc8(one[2]), ALU.subtract).then_inc(sem("gate_shifted"), 1)
            v.wait_ge(sem("gate_exp"), 1)
            rstep(v.tensor_reduce(one[2], q[1], AX_X, ALU.add))
            rstep(v.reciprocal(one[3], one[2]))
            rstep(v.tensor_tensor(q[4], q[1], bc8(one[3]), ALU.mult))
            first_of_largest(q[4], one[2], q[5], q[7], one[3])
            rstep(v.scalar_tensor_tensor(out=q[6], in0=q[5], scalar=-2.0, in1=q[4], op0=ALU.mult, op1=ALU.add))
            first_of_largest(q[6], one[2], q[8], q[7], one[3])
            rstep(v.tensor_tensor(q[5], q[5], q[8], ALU.add))
            rstep(v.tensor_tensor(q[6], q[5], q[4], ALU.mult))
            v.wait_ge(sem("wp_clear"), 1)
            rstep(v.tensor_copy(wp[:, :, 0:8], q[6]))
            rstep(v.tensor_tensor(q[7], q[6], wp[:, :, 0:8], ALU.subtract))
            rstep(v.tensor_copy(wp[:, :, 8:16], q[7]))
            rstep(v.tensor_tensor(wp[:, :, 16:24], q[7], wp[:, :, 8:16], ALU.subtract))
            for i in range(3):
                rstep(v.tensor_copy(wp[:, :, 32 * (i + 1):32 * (i + 1) + 8], q[5]))

            def wT_evac(name):
                for b in range(B):
                    v.wait_ge(sem(f"{name}_ps"), b + 1)
                    v.tensor_copy(wT[:, b * S:(b + 1) * S], ps[:, 6 + b % 2, 0:256].bitcast(BF16))\
                        .then_inc(sem(name), 1)

            wT_evac("wT0")

            def masked(i, ready, reads, bank, name):
                n = i // 8
                v.wait_ge(sem(ready), i + 1)
                if i >= 2:
                    v.wait_ge(sem(reads[0]), reads[1] * (i - 1))
                v.tensor_tensor(xm[:, i % 2, :], hT[:, n * S:(n + 1) * S], ps[:, bank + i % 2, :], ALU.mult)\
                    .then_inc(sem(name), 1)

            def product(i):
                e = i % E0
                v.wait_ge(sem("p2_ps"), i + 1)
                v.wait_ge(sem("s3"), i + 1)
                if i >= 2:
                    v.wait_ge(sem("yacc"), i - 1)
                v.scalar_tensor_tensor(out=pr[:, i % 2, :], in0=ps[:, 6 + i % 2, :], scalar=w["b2"][:, e:e + 1],
                                       in1=s3[:, i % 2, :], op0=ALU.add, op1=ALU.mult).then_inc(sem("pr"), 1)

            masked(0, "wbc_ps", ("p3_ps", 1), 0, "xm")
            for i in range(32):
                if i + 1 < 32:
                    masked(i + 1, "wbc_ps", ("p3_ps", 1), 0, "xm")
                if i >= 1:
                    product(i - 1)
            product(31)
            v.wait_ge(sem("p3_ps"), 32)
            for j in range(8):
                v.wait_ge(sem("sh"), j + 1)
                v.wait_ge(sem("sb_ps"), j + 1)
                if j >= 2:
                    v.wait_ge(sem("z_acc"), j - 1)
                v.tensor_tensor(xm[:, j % 2, :], ps[:, 4 + j % 2, :], gT[:, j % 2, :], ALU.mult).then_inc(sem("sg"), 1)
            for n in range(B):
                ts = slice(n * S, (n + 1) * S)
                v.wait_ge(sem("z_acc"), 2 * (n + 1))
                v.wait_ge(sem("yacc"), 8 * (n + 1))
                v.tensor_tensor(yacc[:, ts], yacc[:, ts], ps[:, Z_BANK[n], :], ALU.add).then_inc(sem("y0_sum"), 1)
                v.wait_ge(sem("y0_sum"), n + 1)
                v.tensor_scalar(yacc[:, ts], yacc[:, ts], modT[:, 0, 5, n:n + 1], None, ALU.mult)\
                    .then_inc(sem("y0"), 1)
            for n in range(B):
                tt = slice(TPB * n, TPB * (n + 1))
                v.wait_ge(sem("y0T_ps"), n + 1)
                v.tensor_tensor(x[:, tt, :], x[:, tt, :], ps[:, 4 + n % 2, :].rearrange("p (t d) -> p t d", t=TPB),
                                ALU.add).then_inc(sem("x2"), 1)
            if stop == 2:
                return

            for b in range(B):
                v.wait_ge(sem("x2"), b + 1)
                ln_stats(v, 3, x, b)
                ln_moments(v, 3, b)
            for b in range(B):
                ln_apply(v, 3, x, xn, b)
            ring = [0]

            def ring_wait():
                ring[0] += 1
                v.wait_ge(sem("ring_ps"), ring[0])
                return (ring[0] - 1) % 2

            def projections(b):
                for a in range(2):
                    for half, table in enumerate(("cos", "sin")):
                        k = ring_wait()
                        if b >= 1:
                            v.wait_ge(sem("qk"), 2 * (b - 1) + a + 1)
                        v.tensor_tensor(ropet[:, 2 * a + half, :], ps[:, k, :], w[table], ALU.mult)\
                            .then_inc(sem("rope"), 1)
                k = ring_wait()
                v.wait_ge(sem("va_clear"), 2)
                if b >= 2:
                    v.wait_ge(sem("pv"), 32 * (b - 1))
                v.tensor_copy(va[:, b % 2, :, :, 0:DK], ps[:, k, :].rearrange("p (t h d) -> p t h d", t=TPB, h=NH))\
                    .then_inc(sem("va"), 1)

            def maxima(s):
                def unit(i):
                    qt, j = divmod(i, 4)
                    n = P * (qt + 1)
                    k = ring_wait()
                    if i == 0 and s >= 2:
                        v.wait_ge(sem("m_parts"), 4 * (s - 1))
                    if 16 * s + i >= 2:
                        v.wait_ge(sem("mx"), 16 * s + i - 1)
                    v.tensor_tensor_reduce(out=junk[:, i % 2, 0:n], in0=ps[:, k, 0:n], in1=w["mask"][:, (3 - qt) * P:4 * P],
                                           scale=1.0, scalar=3 * NEG, op0=ALU.add, op1=ALU.max,
                                           accum_out=mx[:, s % 2, qt, j:j + 1]).then_inc(sem("mx"), 1)
                return unit

            def max_parts(s):
                k = s % 2
                v.wait_ge(sem("mx"), 16 * (s + 1))
                v.tensor_scalar(mpc[:, k, :, :, 0], mx[:, k], -1.0, None, ALU.mult).then_inc(sem("m_parts"), 1)
                v.wait_ge(sem("m_parts"), 4 * s + 1)
                v.scalar_tensor_tensor(out=mres[:, :, :], in0=mx[:, k], scalar=-1.0, in1=mpc[:, k, :, :, 0],
                                       op0=ALU.mult, op1=ALU.subtract).then_inc(sem("m_parts"), 1)
                v.wait_ge(sem("m_parts"), 4 * s + 2)
                v.tensor_copy(mpc[:, k, :, :, 1], mres[:, :, :]).then_inc(sem("m_parts"), 1)
                v.wait_ge(sem("m_parts"), 4 * s + 3)
                v.tensor_tensor(mpc[:, k, :, :, 2], mres[:, :, :], mpc[:, k, :, :, 1], ALU.subtract)\
                    .then_inc(sem("m_parts"), 1)

            def mT_evac(s):
                k = ring_wait()
                if s >= 2:
                    v.wait_ge(sem(f"m_rows{s % 2}"), 32 * (s // 2))
                v.tensor_copy(mT[0:12, s % 2, :], ps[0:12, k, 0:256].bitcast(BF16)).then_inc(sem("mT"), 1)

            def o_evac(s):
                v.wait_ge(sem("pv"), 8 * (s + 1))
                if s >= 1:
                    v.wait_ge(sem("oT_ps"), s)
                v.tensor_copy(ot[:, :], ps[:, 3, :]).then_inc(sem("ot"), 1)

            def o_norm(s):
                b, g = divmod(s, QG)
                o4 = ps[:, 2, :].rearrange("p (q j d) -> p q j d", q=4, j=4)
                v.wait_ge(sem("oT_ps"), s + 1)
                if s >= 1:
                    v.wait_ge(sem("at"), s)
                v.reciprocal(rden[:, :, :], o4[:, :, :, DK]).then_inc(sem("rden"), 1)
                v.wait_ge(sem("rden"), s + 1)
                if g == 0 and b >= 1:
                    v.wait_ge(sem("aT_ps"), b)
                v.tensor_tensor(at[:, :, 4 * g:4 * g + 4, :], o4[:, :, :, 0:DK],
                                rden[:, :, :].unsqueeze(3).to_broadcast([P, 4, 4, DK]), ALU.mult).then_inc(sem("at"), 1)

            def attn_out(b):
                v.wait_ge(sem("aT_ps"), b + 1)
                v.tensor_copy(aT[:, :], ps[:, 2, :]).then_inc(sem("aT"), 1)
                v.wait_ge(sem("ao_ps"), b + 1)
                tt = slice(TPB * b, TPB * (b + 1))
                v.tensor_tensor(ao[:, :].rearrange("p (t d) -> p t d", t=TPB),
                                ps[:, 2, :].rearrange("p (t d) -> p t d", t=TPB),
                                mod1[:, b, 0:D].unsqueeze(1).to_broadcast([P, TPB, D]), ALU.mult).then_inc(sem("ao"), 1)
                v.wait_ge(sem("ao"), b + 1)
                v.tensor_tensor(x[:, tt, :], x[:, tt, :], ao[:, :].rearrange("p (t d) -> p t d", t=TPB), ALU.add)\
                    .then_inc(sem("x3"), 1)

            projections(0)
            projections(1)
            for it in range(-2, 16):
                if it in (4, 8):
                    projections(it // 4 + 1)
                if 0 <= it + 1 < 16:
                    mT_evac(it + 1)
                if it + 2 < 16:
                    unit = maxima(it + 2)
                    for i in range(8):
                        unit(2 * i)
                        unit(2 * i + 1)
                    max_parts(it + 2)
                if it >= 0:
                    o_evac(it)
                    o_norm(it)
                    if it % QG == QG - 1:
                        attn_out(it // QG)
            if stop == 3:
                v.wait_ge(sem("x3"), B)
                v.nop().then_inc(sem("x_final"), B)
                return

            for b in range(B):
                v.wait_ge(sem("x3"), b + 1)
                ln_stats(v, 4, x, b)
                ln_moments(v, 4, b)
            for b in range(B):
                ln_apply(v, 4, x, xn, b)
                ts = slice(TPB * b, TPB * (b + 1))
                for i, op in ((2, ALU.mult), (1, ALU.add)):
                    v.wait_ge(sem("ln_out"), NT * 4 + TPB * (b + 1))
                    if i == 1:
                        v.wait_ge(sem("h4_scaled"), b + 1)
                    v.tensor_tensor(xn[:, ts, :], xn[:, ts, :],
                                    mod1[:, b, i * D:(i + 1) * D].unsqueeze(1).to_broadcast([P, TPB, D]), op)\
                        .then_inc(sem("h4_scaled" if i == 2 else "h4"), 1)
            v.wait_ge(sem("gate1_ps"), 1)
            q[4] = logits
            first_of_largest(q[4], one[2], q[5], q[7], one[3])
            v.wait_ge(sem("rank_ps"), 1)
            d = [dp[:, i] for i in range(6)]
            flat = [dp[:, i].rearrange("p e t -> p (e t)") for i in range(6)]
            rank = ps[:, 7, 0:NT * E1].rearrange("p (e t) -> p e t", e=E1)
            rstep(v.tensor_copy(flat[0], ps[:, 7, NT * E1:2 * NT * E1]))
            rstep(v.tensor_tensor_scan(flat[1], w["segment"], flat[0], 0.0, ALU.mult, ALU.add))
            rstep(v.tensor_tensor(d[2], d[1][:, :, NT - 1:NT].to_broadcast([P, E1, NT]),
                                  w["full"].unsqueeze(1).to_broadcast([P, E1, NT]), ALU.is_gt))
            rstep(v.tensor_reduce(nblk[:, 0, :].unsqueeze(2), d[2], AX_X, ALU.add))
            rstep(v.tensor_tensor_scan(nblk[:, 1, :], ones[:, 0:E1], nblk[:, 0, :], 0.0, ALU.mult, ALU.add))
            rstep(v.tensor_tensor(nblk[:, 2, :], nblk[:, 1, :], nblk[:, 0, :], ALU.subtract))
            rstep(v.tensor_tensor(d[3], d[1], d[0], ALU.subtract))
            rstep(v.scalar_tensor_tensor(out=d[4], in0=nblk[:, 2, :].unsqueeze(2).to_broadcast([P, E1, NT]),
                                         scalar=float(P), in1=d[3], op0=ALU.mult, op1=ALU.add))
            rstep(v.tensor_tensor(d[4], d[4], rank, ALU.add))
            rstep(v.tensor_tensor(d[5], d[4], q[5].rearrange("p t e -> p e t"), ALU.mult))
            rstep(v.tensor_reduce(pos, d[5].rearrange("p e t -> p t e"), AX_X, ALU.add))
            v.tensor_scalar(posu[:, :], pos[:, :, 0], -1.0, None, ALU.add).then_inc(sem("posu"), 1)
            rstep(v.tensor_tensor(blk[:, :, :], nblk[:, 1, :].unsqueeze(1).to_broadcast([P, NBLK, E1]),
                                  w["block"].unsqueeze(2).to_broadcast([P, NBLK, E1]), ALU.is_le))
            rstep(v.tensor_reduce(blk1, blk[:, :, :], AX_X, ALU.add))
            v.tensor_scalar(expert_at[:, :], blk1[:, :, 0], float(E1 - 1), float(HID), ALU.min, ALU.mult)\
                .then_inc(sem("expert_at"), 1)
            rstep(v.scalar_tensor_tensor(out=q[6], in0=q[5], scalar=NEG, in1=q[4], op0=ALU.mult, op1=ALU.add))
            rstep(v.tensor_reduce(one[8], q[6], AX_X, ALU.max))
            v.tensor_tensor(rt[:, 9, :, 0], rt[:, 8, :, 0], rt[:, 2, :, 0], ALU.subtract).then_inc(sem("top_diff"), 1)
            v.wait_ge(sem("top_exp"), 1)
            rstep(v.tensor_scalar(rt[:, 11, :, 0], rt[:, 10, :, 0], 1.0, None, ALU.add))
            v.reciprocal(wtop[:, :], rt[:, 11, :, 0]).then_inc(sem("wtop"), 1)

            for i in range(-1, NBLK + 2):
                if 0 <= i + 1 < NBLK:
                    j = i + 1
                    v.wait_ge(sem("xT_ps"), j + 1)
                    if j >= 2:
                        v.wait_ge(sem("m1_ps"), j - 1)
                    v.tensor_copy(xT[:, j % 2, :], ps[:, 2 + j % 2, 0:P]).then_inc(sem("xT"), 1)
                if 0 <= i - 1 < NBLK:
                    j = i - 1
                    v.wait_ge(sem("gsT_ps"), j + 1)
                    if j >= 2:
                        v.wait_ge(sem("m2_ps"), j - 1)
                    v.tensor_copy(gsT[:, j % 2, :], ps[:, 4 + j % 2, :]).then_inc(sem("gsT"), 1)
                if 0 <= i - 2 < NBLK:
                    j = i - 2
                    v.wait_ge(sem("m2_ps"), j + 1)
                    v.tensor_copy(ys[:, j, :], ps[:, 6 + j % 2, 0:D]).then_inc(sem("ys"), 1)
            v.wait_ge(sem("wtop"), 1)
            for b in range(B):
                ts = slice(TPB * b, TPB * (b + 1))
                v.wait_ge(sem(f"gathered{b}"), 16 * TPB)
                for t in range(TPB * b, TPB * (b + 1)):
                    v.scalar_tensor_tensor(out=yt[:, t, :], in0=yt[:, t, :], scalar=wtop[:, t:t + 1],
                                           in1=mod1[:, b, 3 * D:4 * D], op0=ALU.mult, op1=ALU.mult)\
                        .then_inc(sem("y_weighted"), 1)
                v.wait_ge(sem("y_weighted"), TPB * (b + 1))
                v.tensor_tensor(x[:, ts, :], x[:, ts, :], yt[:, ts, :], ALU.add).then_inc(sem("x4"), 1)

        @block.tensor
        def _(pe):
            pe.wait_ge(sem("siluc"), 1)
            for layer in range(2):
                for c in range(6):
                    mm = pe.matmul(ps[:, 0, (layer * 6 + c) * B:(layer * 6 + c + 1) * B],
                                   w[f"wmod{layer}"][:, c * D:(c + 1) * D], siluc[:, layer * B:(layer + 1) * B],
                                   start=True, stop=True)
            mm.then_inc(sem("modT_ps"), 1)
            for b in range(B):
                pe.matmul(ps[:, 1 + b, 0:3 * D], siluc[:, b:b + 1].to_broadcast([P, P]), w["wmod0"][:, 0:3 * D],
                          start=True, stop=True).then_inc(sem("mod0_ps"), 1)
            for b in range(B):
                if b == 3:
                    pe.wait_ge(sem("mod_sb"), 2)
                pe.matmul(ps[:, MOD1_BANK[b], :], siluc[:, B + b:B + b + 1].to_broadcast([P, P]),
                          w["wmod1"][:, 2 * D:6 * D], start=True, stop=True).then_inc(sem("mod1_ps"), 1)
            pe.wait_ge(sem("ld_const"), 16)

            def transposes(k, b):
                pe.wait_ge(sem("ln_out"), NT * k + TPB * (b + 1))
                if b >= 2:
                    pe.wait_ge(sem("hT"), B * (k - 1) + b - 1)
                for i in range(TPB):
                    mm = pe.transpose(ps[:, 6 + b % 2, i * P:(i + 1) * P], xn[:, TPB * b + i, :], ident)
                mm.then_inc(sem("xnT_ps"), 1)

            pe.wait_ge(sem("mod_sb"), 9)
            for b in range(B):
                transposes(1, b)

            def to_tokens(b):
                for c in range(3):
                    pe.wait_ge(sem("xbc_silu"), 4 * b + c + 1)
                    if 3 * b + c >= 1:
                        pe.wait_ge(sem("xs_tok"), 3 * b + c)
                    else:
                        pe.wait_ge(sem("hT"), B)
                    for i in range(TPB):
                        mm = pe.transpose(ps[:, 6, i * P:(i + 1) * P],
                                          xcT[:, c, b * S + i * P:b * S + (i + 1) * P], ident)
                    mm.then_inc(sem("xs_ps"), 1)

            
            for b in range(B):
                pe.wait_ge(sem("hT"), b + 1)
                for c in range(4):
                    if b >= 1:
                        pe.wait_ge(sem("conv"), 4 * (b - 1) + c + 1)
                    pe.matmul(ps[:, c, :], w["in_proj"][:, DI + c * P:DI + (c + 1) * P], hT[:, b * S:(b + 1) * S],
                              start=True, stop=True).then_inc(sem("xbc_ps"), 1)
                for i in range(2):
                    if b >= 1:
                        pe.wait_ge(sem("sz"), 2 * (b - 1) + i + 1)
                    for j in range(2):
                        t = TPB * b + 2 * i + j
                        mm = pe.matmul(ps[:, 4 + i, j * DI:(j + 1) * DI], hT[:, t * P:(t + 1) * P],
                                       w["in_proj"][:, 0:DI], start=True, stop=True)
                    mm.then_inc(sem("z_ps"), 1)
                if b == 0:
                    pe.wait_ge(sem("hT"), B)
                for t in range(TPB * b, TPB * (b + 1)):
                    mm = pe.matmul(ps[:, 7, t * HEADS:(t + 1) * HEADS], hT[:, t * P:(t + 1) * P],
                                   w["in_proj"][:, 768:772], start=True, stop=True)
                if b == B - 1:
                    mm.then_inc(sem("dt_ps"), 1)
                if b >= 1:
                    to_tokens(b - 1)
            to_tokens(B - 1)

            pe.wait_ge(sem("decay_in"), 1)
            pe.wait_ge(sem("pool_const"), 2)
            a2 = av[:, :, :].rearrange("p t h -> p (t h)")
            pe.matmul(ps[:, 7, 0:64], w["tri"], a2, start=True, stop=True)
            pe.matmul(ps[:, 7, 64:128], ones[:, :], a2, start=True, stop=True).then_inc(sem("acum_ps"), 1)

            def head(t):
                k = t % 2
                c, b = t % TPB, t // TPB
                tok = slice(t * P, (t + 1) * P)
                pe.wait_ge(sem("ua"), HEADS * (t + 1))
                if t >= 2:
                    pe.wait_ge(sem("L"), t - 1)
                else:
                    pe.wait_ge(sem("conv"), 16)
                for hh in range(HEADS):
                    mm = pe.matmul(ps[:, k, hh * P:(hh + 1) * P], ua[:, k, hh, :], w["tri"], start=True, stop=True)
                mm.then_inc(sem("seg_ps"), 1)
                if t >= 2:
                    pe.wait_ge(sem("Gm"), t - 1)
                pe.wait_ge(sem("xbc_silu"), 4 * (b + 1))
                pe.matmul(ps[:, 2, k * P:(k + 1) * P], xcT[:, 2, tok], xcT[:, 3, tok], start=True,
                          stop=True).then_inc(sem("g_ps"), 1)
                if c < TPB - 1:
                    pe.wait_ge(sem("Xd"), t + 1)
                    n_st = 3 * b + c
                    if n_st >= 1:
                        pe.wait_ge(sem("prev"), n_st)
                    else:
                        pe.wait_ge(sem("sz"), 8)
                    pe.matmul(ps[:, 5, k * DI:(k + 1) * DI], Bt[:, t, :], Xd[:, k].rearrange("p h e -> p (h e)"),
                              start=True, stop=True).then_inc(sem("state_ps"), 1)
                pe.wait_ge(sem("M"), t + 1)
                pe.wait_ge(sem("X"), t + 1)
                if t >= 2:
                    pe.wait_ge(sem("y_gated"), t - 1)
                if c > 0:
                    pe.wait_ge(sem("prev"), 3 * b + c)
                    pe.matmul(ps[:, 3 + k, DI:2 * DI], xcT[:, 3, tok],
                              prev[:, 1 - k].rearrange("p h e -> p (h e)"), start=True, stop=True)
                for hh in range(HEADS):
                    mm = pe.matmul(ps[:, 3 + k, hh * HP:(hh + 1) * HP], M[:, k, hh, :], X[:, k, hh, :],
                                   start=True, stop=True)
                mm.then_inc(sem("y_ps"), 1)

            def tail(t):
                k = t % 2
                pe.wait_ge(sem("y_gated"), t + 1)
                if t >= 2:
                    pe.wait_ge(sem("yT"), t - 1)
                elif t == 0:
                    pe.wait_ge(sem("xs_tok"), 12)
                for i in range(2):
                    mm = pe.transpose(ps[:, 6, k * 256 + i * P:k * 256 + (i + 1) * P], y[:, k, i * P:(i + 1) * P],
                                      ident)
                mm.then_inc(sem("yT_ps"), 1)
                pe.wait_ge(sem("yT"), t + 1)
                if t >= 2:
                    pe.wait_ge(sem("o_sum"), t - 1)
                elif t == 0:
                    pe.wait_ge(sem("wor"), 2)
                    pe.wait_ge(sem("eact"), 1)
                for i in range(2):
                    mm = pe.matmul(ps[:, 7, P * (1 + k):P * (2 + k)], yT[:, k, i, :], wor[:, i, :],
                                   start=(i == 0), stop=(i == 1))
                mm.then_inc(sem("o_ps"), 1)

            for t in range(NT + 1):
                if t < NT:
                    head(t)
                if t >= 1:
                    tail(t - 1)
            if stop == 1:
                return

            def router(k, weights, name):
                for b in range(B):
                    transposes(k, b)
                logits(k, weights, name)

            def logits(k, weights, name):
                for b in range(B):
                    pe.wait_ge(sem("hT"), B * (k - 1) + b + 1)
                    for t in range(TPB * b, TPB * (b + 1)):
                        mm = pe.matmul(ps[:, 5, 8 * t:8 * t + 8], hT[:, t * P:(t + 1) * P], weights, start=True,
                                       stop=True)
                mm.then_inc(sem(name), 1)

            def weights_T(ready, name):
                pe.wait_ge(sem("route"), ready)
                for b in range(B):
                    if b >= 2:
                        pe.wait_ge(sem(name), b - 1)
                    for i in range(TPB):
                        mm = pe.transpose(ps[:, 6 + b % 2, i * 64:(i + 1) * 64].bitcast(BF16), wp[:, TPB * b + i, :],
                                          identb)
                    mm.then_inc(sem(f"{name}_ps"), 1)

            pe.wait_ge(sem("yT"), NT)
            pe.wait_ge(sem("x1"), NT)
            pe.wait_ge(sem("ld_moe0"), 16)
            router(2, w["gate"], "gate_ps")
            pe.wait_ge(sem("ld_bconst"), 16)
            weights_T(ROUTE0, "wT0")
            pe.wait_ge(sem("b3_step"), 8)

            def spread(i, sel, rows, name, reads):
                n, e = divmod(i, 8)
                pe.wait_ge(sem(WT[name]), n + 1)
                if i >= 2:
                    pe.wait_ge(sem(reads), i - 1)
                pe.matmul(ps[:, i % 2, :], sel[0:rows, e * P:(e + 1) * P], wT[0:rows, n * S:(n + 1) * S],
                          start=True, stop=True).then_inc(sem(name), 1)

            WT = {"wbc_ps": "wT0", "hot_ps": "wT1"}

            def expert_in(i):
                n, e = divmod(i, E0)
                pe.wait_ge(sem("xm"), i + 1)
                if i >= 2:
                    pe.wait_ge(sem("h1"), i - 1)
                    pe.wait_ge(sem("s3"), i - 1)
                pe.matmul(ps[:, 2 + i % 2, :], w["w1"][:, e * D:(e + 1) * D], xm[:, i % 2, :], start=True,
                          stop=True).then_inc(sem("p1_ps"), 1)
                pe.matmul(ps[:, 4 + i % 2, :], w["w3"][:, e * D:(e + 1) * D], xm[:, i % 2, :], start=True, stop=False)
                pe.matmul(ps[:, 4 + i % 2, :], b3p[0:104, e, :], wT[0:104, n * S:(n + 1) * S], start=False,
                          stop=True).then_inc(sem("p3_ps"), 1)

            def expert_out(i):
                e = i % E0
                pe.wait_ge(sem("h1"), i + 1)
                if i >= 2:
                    pe.wait_ge(sem("pr"), i - 1)
                pe.matmul(ps[:, 6 + i % 2, :], w["w2"][:, e * D:(e + 1) * D], gT[:, i % 2, :], start=True,
                          stop=True).then_inc(sem("p2_ps"), 1)

            spread(0, w["sel0"], 104, "wbc_ps", "xm")
            spread(1, w["sel0"], 104, "wbc_ps", "xm")
            pe.wait_ge(sem("wT0"), B)
            for i in range(32):
                expert_in(i)
                if i + 2 < 32:
                    spread(i + 2, w["sel0"], 104, "wbc_ps", "xm")
                if i >= 1:
                    expert_out(i - 1)
            expert_out(31)
            pe.wait_ge(sem("h1"), 32)
            pe.wait_ge(sem("s3"), 32)

            def shared_out(j):
                n, i = divmod(j, 2)
                pe.wait_ge(sem("sg"), j + 1)
                if j == 0:
                    pe.wait_ge(sem("pr"), 32)
                pe.matmul(ps[:, Z_BANK[n], :], w["sw3"][:, i * D:(i + 1) * D],
                          xm[:, j % 2, :], start=(i == 0), stop=(i == 1)).then_inc(sem("z_acc"), 1)

            for j in range(8):
                n, i = divmod(j, 2)
                ts = slice(n * S, (n + 1) * S)
                if j >= 2:
                    pe.wait_ge(sem("sh"), j - 1)
                    pe.wait_ge(sem("sg"), j - 1)
                pe.matmul(ps[:, 2 + j % 2, :], w["sw1"][:, i * P:(i + 1) * P], hT[:, ts], start=True,
                          stop=True).then_inc(sem("sa_ps"), 1)
                pe.matmul(ps[:, 4 + j % 2, :], w["sw2"][:, i * P:(i + 1) * P], hT[:, ts], start=True,
                          stop=True).then_inc(sem("sb_ps"), 1)
                if j >= 1:
                    shared_out(j - 1)
            shared_out(7)
            for n in range(B):
                pe.wait_ge(sem("y0"), n + 1)
                if n >= 2:
                    pe.wait_ge(sem("x2"), n - 1)
                for i in range(TPB):
                    mm = pe.transpose(ps[:, 4 + n % 2, i * P:(i + 1) * P], yacc[:, n * S + i * P:n * S + (i + 1) * P],
                                      ident)
                mm.then_inc(sem("y0T_ps"), 1)
            if stop == 2:
                return

            pe.wait_ge(sem("ld_attn"), 16)
            pe.wait_ge(sem("y0"), B)
            for b in range(B):
                transposes(3, b)
            pe.wait_ge(sem("hT"), B * 3)
            pe.wait_ge(sem("x2"), B)
            ring = [0]
            read = []

            def ring_bank(name, count):
                if len(read) >= 2:
                    pe.wait_ge(sem(read[-2][0]), read[-2][1])
                read.append((name, count))
                return (len(read) - 1) % 2

            def projections(b):
                for a, n in enumerate("qk"):
                    for half in range(2):
                        k = ring_bank("rope", 4 * b + 2 * a + half + 1)
                        pe.matmul(ps[:, k, :], w[f"w{n}" + "s" * half], hT[:, b * S:(b + 1) * S], start=True,
                                  stop=True).then_inc(sem("ring_ps"), 1)
                k = ring_bank("va", b + 1)
                for i in range(TPB):
                    t = TPB * b + i
                    mm = pe.matmul(ps[:, k, i * P:(i + 1) * P], hT[:, t * P:(t + 1) * P], w["wv"], start=True,
                                   stop=True)
                mm.then_inc(sem("ring_ps"), 1)

            def scores(s, i):
                b, g = divmod(s, QG)
                qt, j = divmod(i, 4)
                n = P * (qt + 1)
                if g == 0 and i == 0:
                    pe.wait_ge(sem(f"aug{b % 2}"), 16 * 24 * (b // 2 + 1))
                    pe.wait_ge(sem("k_ones"), 32)
                k = ring_bank("mx", 16 * s + i + 1)
                pe.matmul(ps[:, k, 0:n], qaug[0:KR, b % 2, 2 * g + j // 2, qt * P:(qt + 1) * P],
                          kaug[0:KR, b % 2, 4 * g + j, 0:n], start=True, stop=True).then_inc(sem("ring_ps"), 1)

            def maxima_T(s):
                pe.wait_ge(sem("m_parts"), 4 * (s + 1))
                k = ring_bank("mT", s + 1)
                for qt in range(4):
                    mm = pe.transpose(ps[0:12, k, 64 * qt:64 * (qt + 1)].bitcast(BF16),
                                      mpc[:, s % 2, qt].rearrange("p j i -> p (j i)"), identb)
                mm.then_inc(sem("ring_ps"), 1)

            def scores_T(u):
                s, i = divmod(u, 8)
                b, g = divmod(s, QG)
                kt, jp = 3 - i // 2, i % 2
                n = S - kt * P
                if i == 0:
                    pe.wait_ge(sem(f"m_rows{s % 2}"), 32 * (s // 2 + 1))
                if u >= 2:
                    pe.wait_ge(sem("probs"), u - 1)
                for hh in range(2):
                    bank = 4 + 2 * (u % 2) + hh
                    pe.matmul(ps[:, bank, 0:P], identb, w["causal"], start=True, stop=True)
                    mm = pe.matmul(ps[:, bank, 0:n], kaug[0:KM, b % 2, 4 * g + 2 * jp + hh, kt * P:(kt + 1) * P],
                                   qaug[0:KM, b % 2, 2 * g + jp, kt * P:S], start=False, stop=True,
                                   skip_group_check=True)
                mm.then_inc(sem("st_ps"), 1)

            def values(u):
                s, i = divmod(u, 8)
                b, g = divmod(s, QG)
                kt, jp = 3 - i // 2, i % 2
                n = S - kt * P
                if i == 0 and s >= 1:
                    pe.wait_ge(sem("ot"), s)
                pe.wait_ge(sem("probs"), u + 1)
                pe.wait_ge(sem("va"), b + 1)
                for hh in range(2):
                    j = 2 * jp + hh
                    mm = pe.matmul(ps[32 * j:32 * j + 32, 3, kt * P:S], va[:, b % 2, kt, 4 * g + j, :],
                                   pt[:, u % 3, hh, 0:n], start=(kt == 3), stop=True, skip_group_check=True)
                mm.then_inc(sem("pv"), 1)

            def o_T(s):
                pe.wait_ge(sem("ot"), s + 1)
                if s >= 1:
                    pe.wait_ge(sem("at"), s)
                for qt in range(4):
                    mm = pe.transpose(ps[:, 2, qt * P:(qt + 1) * P], ot[:, qt * P:(qt + 1) * P], ident)
                mm.then_inc(sem("oT_ps"), 1)

            def attn_out(b):
                pe.wait_ge(sem("at"), 4 * (b + 1))
                for qt in range(4):
                    mm = pe.transpose(ps[:, 2, qt * P:(qt + 1) * P], at[:, qt].rearrange("p h d -> p (h d)"), ident)
                mm.then_inc(sem("aT_ps"), 1)
                pe.wait_ge(sem("aT"), b + 1)
                for qt in range(4):
                    mm = pe.matmul(ps[:, 2, qt * P:(qt + 1) * P], aT[:, qt * P:(qt + 1) * P], w["wo"], start=True,
                                   stop=True)
                mm.then_inc(sem("ao_ps"), 1)

            projections(0)
            projections(1)
            for it in range(-2, 16):
                if it in (4, 8):
                    projections(it // 4 + 1)
                if 0 <= it + 1 < 16:
                    maxima_T(it + 1)
                for i in range(8):
                    if it + 2 < 16:
                        scores(it + 2, 2 * i)
                        scores(it + 2, 2 * i + 1)
                    if it >= 0:
                        scores_T(8 * it + i)
                        if i >= 1:
                            values(8 * it + i - 1)
                if it >= 0:
                    values(8 * it + 7)
                    o_T(it)
                    if it % QG == QG - 1:
                        attn_out(it // QG)
            if stop == 3:
                return

            pe.wait_ge(sem("ao"), B)
            pe.wait_ge(sem("probs"), 128)
            pe.wait_ge(sem("ld_moe1"), 16)
            for b in range(B):
                pe.wait_ge(sem("h4"), b + 1)
                transposes(4, b)
            logits(4, w["wr"], "gate1_ps")
            pe.wait_ge(sem("route"), ROUTE1)
            hot = rt[:, 5].rearrange("p t e -> p e t")
            pe.matmul(ps[:, 7, 0:NT * E1], w["tri"], hot, start=True, stop=True)
            pe.matmul(ps[:, 7, NT * E1:2 * NT * E1], ones[:, :], hot, start=True, stop=True).then_inc(sem("rank_ps"), 1)
            pe.wait_ge(sem("expert_at"), 1)
            at_w = {}
            for i in range(-1, NBLK + 2):
                if 0 <= i + 1 < NBLK:
                    j = i + 1
                    for c, js in enumerate(BLOCK_GROUPS):
                        if js.start == j:
                            pe.wait_ge(sem(f"ld_blocks{c}"), 16)
                    if j >= 2:
                        pe.wait_ge(sem("xT"), j - 1)
                    pe.transpose(ps[:, 2 + j % 2, 0:P], xb[:, j, :], ident).then_inc(sem("xT_ps"), 1)
                if 0 <= i < NBLK:
                    j = i
                    at_w[j] = pe.value_load(expert_at[0:1, j:j + 1], min_val=0, max_val=(E1 - 1) * HID)
                    pe.wait_ge(sem("xT"), j + 1)
                    if j >= 2:
                        pe.wait_ge(sem("gelu"), j - 1)
                    pe.matmul(ps[:, j % 2, :], xT[:, j % 2, :], w["W1"][:, bass.ds(at_w[j], HID)], start=True,
                              stop=True).then_inc(sem("m1_ps"), 1)
                if 0 <= i - 1 < NBLK:
                    j = i - 1
                    pe.wait_ge(sem("gelu"), j + 1)
                    if j >= 2:
                        pe.wait_ge(sem("gsT"), j - 1)
                    for q in range(4):
                        mm = pe.transpose(ps[:, 4 + j % 2, q * P:(q + 1) * P], gs[:, j % 2, q * P:(q + 1) * P], ident)
                    mm.then_inc(sem("gsT_ps"), 1)
                if 0 <= i - 2 < NBLK:
                    j = i - 2
                    pe.wait_ge(sem("gsT"), j + 1)
                    if j >= 2:
                        pe.wait_ge(sem("ys"), j - 1)
                    elif j == 0:
                        pe.wait_ge(sem("posu"), 1)
                    for q in range(4):
                        mm = pe.matmul(ps[:, 6 + j % 2, 0:D], gsT[:, j % 2, q * P:(q + 1) * P],
                                       w["W2"][:, bass.ds(at_w[j] + q * D, D)], start=(q == 0), stop=(q == 3))
                    mm.then_inc(sem("m2_ps"), 1)


def shape_constants():
    import numpy as np

    k = np.arange(P)
    pos = np.arange(S, dtype=np.float32)
    inv = np.float32(10000.0) ** (-np.arange(0, DK, 2, dtype=np.float32) / np.float32(DK))
    ang = (pos[:, None] * inv[None, :]).astype(np.float32)
    d = np.arange(P) % DK
    cos = np.cos(ang)[:, d // 2].T
    sin = np.sin(ang)[:, d // 2].T * np.where(d % 2 == 0, -1.0, 1.0)[:, None]
    mask = np.zeros((P, 4 * P), np.float32)
    mask[:, 3 * P:4 * P] = np.where(k[None, :] > k[:, None], NEG, 0.0)
    const = {
        "ident": np.eye(P), "tri": k[:, None] <= k[None, :], "after": k[:, None] > k[None, :],
        "cos": cos, "sin": sin, "iota": np.broadcast_to(8.0 - np.arange(8), (P, 8)), "mask": mask,
        "segment": np.broadcast_to(np.arange(NT * E1) % NT > 0, (P, NT * E1)),
        "full": np.broadcast_to(P * np.arange(NT), (P, NT)),
        "block": np.broadcast_to(np.arange(NBLK), (P, NBLK)),
    }
    sel0 = np.zeros((P, 8, P))
    for e in range(8):
        for piece in range(3):
            sel0[8 * piece + e, e, :] = 1.0
    sel1 = np.zeros((P, 8, P))
    for e in range(8):
        sel1[e, e, :] = 1.0
    bconst = {
        "identb": np.eye(P), "causal": np.where(k[:, None] > k[None, :], NEG, 0.0),
        "sel0": sel0.reshape(P, -1), "sel1": sel1.reshape(P, -1),
    }
    fc = np.concatenate([np.asarray(const[n], np.float32) for n, _ in PACKS["const"]], axis=1)
    bc = np.concatenate([np.asarray(bconst[n], np.float32) for n, _ in BPACK], axis=1).astype(np.dtype("bfloat16"))
    kones = np.zeros((6, NH, S), np.float32)
    kones[0:3, 0::2] = 1.0
    kones[3:6, 1::2] = 1.0
    return fc, bc, kones.astype(np.dtype("bfloat16"))


def lay_out(i):
    import numpy as np

    a = {k: np.asarray(v) for k, v in i.items()}

    def rows(v):
        return np.broadcast_to(v, (P, v.shape[-1]))

    def cols(v):
        return v.reshape(-1, P).T

    def experts(wt):
        return wt.transpose(2, 0, 1).reshape(P, -1)

    fields = {
        "cT": np.concatenate([a["L0_c"].T, a["L1_c"].T], axis=1),
        "wmod0": a["L0_wmod"], "wmod1": a["L1_wmod"],
        "norm_w": cols(a["L0_attn_norm_w"]), "norm_b": cols(a["L0_attn_norm_b"]),
        "in_proj": a["L0_attn_in_proj_w"].T,
        "conv_w": a["L0_attn_conv_w"].reshape(4, P, TAPS).transpose(1, 0, 2).reshape(P, -1),
        "conv_b": cols(a["L0_attn_conv_b"]),
        "dt_bias": rows(a["L0_attn_dt_bias"]), "A_log": rows(a["L0_attn_A_log"]), "D": rows(a["L0_attn_D"]),
        "rms_w": cols(a["L0_attn_rms_w"]),
        "out_proj": a["L0_attn_out_proj_w"].T.reshape(2, P, D).transpose(1, 0, 2).reshape(P, -1),
        "gate": a["L0_ffn_gate_w"].T,
        "w1": experts(a["L0_ffn_w1"]), "w2": experts(a["L0_ffn_w2"]), "w3": experts(a["L0_ffn_w3"]),
        "b1": a["L0_ffn_b1"].T, "b2": a["L0_ffn_b2"].T,
        "sw1": a["L0_ffn_sw1"].T, "sw2": a["L0_ffn_sw2"].T,
        "sw3": a["L0_ffn_sw3"].T.reshape(2, P, D).transpose(1, 0, 2).reshape(P, -1),
        "wr": a["L1_ffn_Wr"],
        "W1": a["L1_ffn_W1"].transpose(1, 0, 2).reshape(P, -1),
        "W2": a["L1_ffn_W2"].reshape(E1, 4, P, D).transpose(2, 0, 1, 3).reshape(P, -1),
    }
    swap = np.arange(P) ^ 1
    for n in "qkvo":
        wt = a[f"L1_attn_W_{n}"]
        fields["w" + n] = wt.T
        if n in "qk":
            fields["w" + n + "s"] = wt[swap].T
    packs = {
        f"{pack}_in": np.ascontiguousarray(np.concatenate([fields[n] for n, _ in PACKS[pack]], axis=1))
        for pack in ("mixw", "moe0", "attn", "moe1")
    }
    packs["x_in"] = np.ascontiguousarray(a["L0_attn_x"].reshape(NT, P, D).transpose(1, 0, 2))
    b3 = np.zeros((P, E0, D), np.float32)
    for piece in range(3):
        for e in range(E0):
            b3[32 + 32 * piece + e, e, :] = a["L0_ffn_b3"][e]
    packs["b3_in"] = b3
    packs["const_in"], packs["bconst_in"], packs["kones_in"] = shape_constants()
    return packs


def kernel(**inputs):
    import concourse.bacc as bacc
    import numpy as np
    from concourse.bass_utils import run_bass_kernel_spmd

    nc = bacc.Bacc("TRN2", target_bir_lowering=False, num_devices=1)
    arrays = lay_out(inputs)
    args = {n: nc.dram_tensor(n, v.shape, mybir.dt.from_np(v.dtype), kind="ExternalInput").ap()
            for n, v in arrays.items()}
    out = nc.dram_tensor("y_out", (P, NT, D), F32, kind="ExternalOutput").ap()
    adaln_kernel(nc, out=out, **args)
    got = run_bass_kernel_spmd(nc, [arrays], core_ids=[0]).results[0]["y_out"]
    return np.ascontiguousarray(np.asarray(got).transpose(1, 0, 2)).reshape(B, S, D)
```

```python
from contextlib import ExitStack

import concourse.bass as bass
from concourse import mybir

F32 = mybir.dt.float32
BF16 = mybir.dt.bfloat16
ALU = mybir.AluOpType
ACT = mybir.ActivationFunctionType
AX_X = mybir.AxisListType.X

P = 128
B, S, D = 4, 512, 128
TPB = S // P
NT = B * TPB
NTOK = B * S
EPS = 1e-5
DI, HEADS, HP = 256, 4, 64
TAPS = 4
E0, E1 = 8, 8
HID = 512
NH, DK = 16, 8
QG = NH // 4
PIECES = 6
KR = 2 * PIECES * DK
NBLK = NT + E1 - 1
KM = KR + 6
VW = DK + 1
ATT_SCALE = float(DK) ** -0.5
DENSE = B * E0
NEG = -1e30
MOD1_BANK = (5, 6, 7, 1)
Z_BANK = (0, 1, 6, 7)
ROUTE0, ROUTE1, ROUTE2 = 24, 29, 45

PACKS = {
    "mixw": [("cT", 8), ("wmod0", 768), ("wmod1", 768), ("norm_w", 1), ("norm_b", 1), ("in_proj", 772),
             ("conv_w", 16), ("conv_b", 4), ("dt_bias", 4), ("A_log", 4), ("D", 4), ("rms_w", 2),
             ("out_proj", 256)],
    "moe0": [("gate", 8), ("w1", 1024), ("w2", 1024), ("w3", 1024), ("b1", 8), ("b2", 8),
             ("sw1", 256), ("sw2", 256), ("sw3", 256)],
    "attn": [("wq", 128), ("wqs", 128), ("wk", 128), ("wks", 128), ("wv", 128), ("wo", 128)],
    "moe1": [("wr", 8), ("W1", 4096), ("W2", 4096)],
    "const": [("ident", 128), ("tri", 128), ("after", 128), ("cos", 512), ("sin", 512), ("iota", 8),
              ("mask", 512), ("segment", NT * E1), ("full", NT), ("block", NBLK)],
}
BPACK = [("identb", 128), ("causal", 128), ("sel0", 1024), ("sel1", 1024)]


def offsets(fields):
    out, at = {}, 0
    for name, width in fields:
        out[name] = (at, at + width)
        at += width
    return out, at


def adaln_kernel(nc, x_in, mixw_in, moe0_in, attn_in, moe1_in, const_in, b3_in, bconst_in, kones_in, out, stop=9):
    with ExitStack() as ctx:
        def sb(name, shape, dt=F32):
            return ctx.enter_context(nc.sbuf_tensor(name, shape, dt))

        sems = {}

        def sem(name):
            if name not in sems:
                sems[name] = ctx.enter_context(nc.semaphore(name))
            return sems[name]

        ps = ctx.enter_context(nc.psum_tensor("ps", [P, 8, 512], F32))

        w = {}
        packed = {}
        for pack, fields in PACKS.items():
            off, total = offsets(fields)
            if pack == "moe1":
                continue
            t = packed[pack] = sb(pack, [P, total])
            for name, (lo, hi) in off.items():
                w[name] = t[:, lo:hi]
        off, total = offsets(BPACK)
        bconst = sb("bconst", [P, total], BF16)
        for name, (lo, hi) in off.items():
            w[name] = bconst[:, lo:hi]
        ident, identb = w["ident"], w["identb"]

        x = sb("x", [P, NT, D])
        xn = sb("xn", [P, NT, D])
        hT = sb("hT", [P, NTOK])
        siluc = sb("siluc", [P, 8])
        modT = sb("modT", [P, 6, 2, B])
        mod0 = sb("mod0", [P, B, 3 * D])
        mod1 = sb("mod1", [P, B, 4 * D])
        zeros = sb("zeros", [P, D])
        guard_tmp = sb("guard_tmp", [P, 2, 2, 2 * B])
        neghalf = sb("neghalf", [P, NT])
        ones = sb("ones", [P, P])
        LN = 5
        st = sb("st", [P, LN, NT, 6])
        mv = sb("mv", [P, LN, NT, 2])
        rs = sb("rs", [P, LN, NT])
        nmean = sb("nmean", [P, NT])
        ARENA = 30720
        arena = sb("arena", [P, ARENA])

        class Area:
            def __init__(self, room, size):
                self.room, self.size, self.at = room, size, 0

            def take(self, n, dt=F32):
                words = n if dt == F32 else n // 2
                v = self.room[:, self.at:self.at + words]
                self.at += words
                assert self.at <= self.size, self.at
                return v if dt == F32 else v.bitcast(dt)

        ar = Area(arena, ARENA)
        xcT = ar.take(4 * NTOK).rearrange("p (c t) -> p c t", c=4)
        acc = ar.take(4 * S).rearrange("p (c t) -> p c t", c=4)
        h = ar.take(NT * D).rearrange("p (t d) -> p t d", d=D)
        sz = ar.take(NT * DI).rearrange("p (t d) -> p t d", d=DI)
        xs = ar.take(NT * DI).rearrange("p (t d) -> p t d", d=DI)
        Bt = ar.take(NT * D).rearrange("p (t d) -> p t d", d=D)
        wor = sb("wor", [P, 2, D])
        eA = sb("eA", [P, HEADS])
        ssq = sb("ssq", [P, NT])
        rr = sb("rr", [P, NT])

        def heads(v):
            return v.rearrange("p (k h s) -> p k h s", k=2, h=HEADS)

        dtv = ar.take(8 * NT * HEADS).rearrange("p (i t h) -> p i t h", i=8, h=HEADS)
        av = ar.take(NT * HEADS).rearrange("p (t h) -> p t h", h=HEADS)
        eact = ar.take(2 * NT * HEADS).rearrange("p (i t h) -> p i t h", i=2, h=HEADS)
        ua = heads(ar.take(2 * HEADS * P))
        L = heads(ar.take(2 * HEADS * P))
        M = heads(ar.take(2 * HEADS * P))
        Gm = ar.take(2 * P).rearrange("p (k s) -> p k s", k=2)
        X = heads(ar.take(2 * DI))
        Xd = heads(ar.take(2 * DI))
        Dx = heads(ar.take(2 * DI))
        prev = heads(ar.take(2 * DI))
        Yo = ar.take(DI).rearrange("p (h s) -> p h s", h=HEADS)
        y = ar.take(2 * DI).rearrange("p (k s) -> p k s", k=2)
        ysq = ar.take(DI)
        yT = ar.take(2 * DI).rearrange("p (k i s) -> p k i s", k=2, i=2)
        o = ar.take(2 * D).rearrange("p (k s) -> p k s", k=2)

        ar = Area(arena, ARENA)
        off, total = offsets(PACKS["moe1"])
        packed["moe1"] = ar.take(total)
        for name, (lo, hi) in off.items():
            w[name] = packed["moe1"][:, lo:hi]
        later = ar.at
        rt = ar.take(12 * NT * 8).rearrange("p (i t e) -> p i t e", i=12, e=8)
        wp = ar.take(NT * P, BF16).rearrange("p (t r) -> p t r", t=NT)
        wT = ar.take(NTOK, BF16)
        xm = ar.take(2 * S).rearrange("p (k t) -> p k t", k=2)
        gT = ar.take(4 * S).rearrange("p (k t) -> p k t", k=4)
        s3 = ar.take(2 * S).rearrange("p (k t) -> p k t", k=2)
        pr = ar.take(2 * S).rearrange("p (k t) -> p k t", k=2)
        yacc = ar.take(NTOK)
        b3f = ar.take(1024)
        b3r = ar.take(1024)
        b3c = ar.take(3 * 1024, BF16).rearrange("p (i c) -> p i c", i=3)
        b3p = sb("b3p", [P, E0, D], BF16)
        top = ar.at
        wtop = sb("wtop", [P, NT])
        ar.at = later
        qaug = ar.take(2 * 8 * S, BF16).rearrange("p (k a t) -> p k a t", k=2, a=8)
        kaug = ar.take(2 * NH * S, BF16).rearrange("p (k a t) -> p k a t", k=2, a=NH)
        va = ar.take(2 * TPB * NH * 32).rearrange("p (k t h d) -> p k t h d", k=2, t=TPB, h=NH)
        used = Area(packed["moe0"], offsets(PACKS["moe0"])[1])
        ropet = used.take(4 * S).rearrange("p (k t) -> p k t", k=4)
        qk = used.take(2 * S).rearrange("p (k t) -> p k t", k=2)
        junk = used.take(2 * S, BF16).rearrange("p (k t) -> p k t", k=2)
        pc = ar.take(6 * S, BF16).rearrange("p (a i t) -> p a i t", a=2, i=3)
        pt = ar.take(3 * 2 * S).rearrange("p (k a t) -> p k a t", k=3, a=2)
        mx = ar.take(2 * 16).rearrange("p (k q j) -> p k q j", k=2, q=4)
        mres = ar.take(16).rearrange("p (q j) -> p q j", q=4)
        mpc = ar.take(2 * 48, BF16).rearrange("p (k q j i) -> p k q j i", k=2, q=4, j=4)
        mT = ar.take(2 * S, BF16).rearrange("p (k t) -> p k t", k=2)
        used = Area(packed["mixw"], offsets(PACKS["mixw"])[1])
        ot = used.take(S)
        rden = ar.take(16).rearrange("p (q j) -> p q j", q=4)
        at = ar.take(TPB * D).rearrange("p (q h d) -> p q h d", q=TPB, h=NH)
        aT = used.take(S)
        ao = used.take(S)
        ar.at = later
        ar.take(12 * NT * 8)
        xb = ar.take(NBLK * D).rearrange("p (j d) -> p j d", d=D)
        xT = ar.take(2 * P).rearrange("p (k s) -> p k s", k=2)
        gs = ar.take(2 * HID).rearrange("p (k h) -> p k h", k=2)
        gsT = ar.take(2 * HID).rearrange("p (k h) -> p k h", k=2)
        ys = ar.take(NBLK * D).rearrange("p (j d) -> p j d", d=D)
        yt = ar.take(NT * D).rearrange("p (t d) -> p t d", d=D)
        dp = ar.take(6 * NT * E1).rearrange("p (i e t) -> p i e t", i=6, e=E1)
        nblk = ar.take(4 * E1).rearrange("p (i e) -> p i e", i=4)
        blk = ar.take(NBLK * E1).rearrange("p (j e) -> p j e", e=E1)
        blk1 = ar.take(NBLK).rearrange("p (j e) -> p j e", e=1)
        expert_at = sb("expert_at", [P, NBLK], mybir.dt.int32)
        pos = ar.take(NT).rearrange("p (t e) -> p t e", e=1)
        posu = sb("posu", [P, NT], mybir.dt.uint32)
        slots_x = nc.dram_tensor("slots_x", (NBLK * P, D), F32, kind="Internal").ap()
        slots_y = nc.dram_tensor("slots_y", (NBLK * P, D), F32, kind="Internal").ap()
        qkd = nc.dram_tensor("qk_parts", (B, 2, P, 3, S), BF16, kind="Internal").ap()

        block = ctx.enter_context(nc.Block())

        FINAL = {1: NT, 2: B, 3: B, 9: B}

        BLOCK_GROUPS = [slice(j, min(j + 6, NBLK)) for j in range(0, NBLK, 6)]

        def modrow(i):
            return mod0[:, :, i * D:(i + 1) * D]

        @block.sync
        def _(sp):
            sp.dma_start(x[:, :, :], x_in).then_inc(sem("ld_x"), 16)
            sp.dma_start(packed["mixw"][:, :], mixw_in).then_inc(sem("ld_mixw"), 16)
            sp.dma_start(packed["const"][:, :], const_in).then_inc(sem("ld_const"), 16)
            sp.dma_start(bconst[:, :], bconst_in).then_inc(sem("ld_bconst"), 16)
            sp.dma_start(packed["moe0"][:, :], moe0_in).then_inc(sem("ld_moe0"), 16)
            sp.dma_start(packed["attn"][:, :], attn_in).then_inc(sem("ld_attn"), 16)
            sp.wait_ge(sem("pool_const"), 3)
            sp.dma_start(slots_x.rearrange("(j p) d -> p j d", p=P), zeros[:, :].unsqueeze(1)
                         .to_broadcast([P, NBLK, D])).then_inc(sem("slots_clear"), 16)
            if stop >= 2:
                sp.wait_ge(sem("x1"), NT)
                sp.dma_start(b3f[:, :], b3_in.rearrange("p e d -> p (e d)")).then_inc(sem("ld_b3"), 16)
                sp.dma_start(packed["moe1"][:, :], moe1_in).then_inc(sem("ld_moe1"), 16)
            if stop >= 3:
                sp.wait_ge(sem("kaug_clear"), 1)
                for k in range(2):
                    sp.dma_start(kaug[KR:KM, k, :, :], kones_in).then_inc(sem("k_ones"), 16)

                def relayout(b):
                    sp.wait_ge(sem("parts"), 2 * (b + 1))
                    for a in range(2):
                        sp.dma_start(qkd[b, a], pc[:, a]).then_inc(sem("parts_out"), 16)
                    sp.wait_ge(sem("parts_out"), 32 * (b + 1))
                    if b >= 2:
                        sp.wait_ge(sem("pv"), 8 * 4 * (b - 1))
                    for hh in range(2):
                        for c in range(PIECES):
                            rows = slice((hh * PIECES + c) * DK, (hh * PIECES + c + 1) * DK)
                            for a, (dst, part) in enumerate(((qaug[rows, b % 2, :, :], (0, 0, 0, 1, 1, 2)[c]),
                                                             (kaug[rows, b % 2, hh::2, :], (0, 1, 2, 0, 1, 0)[c]))):
                                src = qkd[b, a, :, part, :].rearrange("(r h d) t -> h d r t", h=2, d=DK)[hh]
                                sp.dma_start(dst, src).then_inc(sem(f"aug{b % 2}"), 16)

                relayout(0)
                relayout(1)
                for s in range(NT):
                    sp.wait_ge(sem("mT"), s + 1)
                    b, g = divmod(s, QG)
                    if g == 0 and b >= 2:
                        sp.wait_ge(sem("pv"), 32 * (b - 1))
                    for i in range(2):
                        sp.dma_start(qaug[KR:KM, b % 2, 2 * g + i, :], mT[6 * i:6 * i + 6, s % 2, :])\
                            .then_inc(sem(f"m_rows{s % 2}"), 16)
                    if s in (5, 9):
                        relayout((s - 1) // 4 + 1)
            if stop < 9:
                sp.wait_ge(sem("x_final"), FINAL[stop])
                sp.dma_start(out, x[:, :, :]).then_inc(sem("stored"), 16)
                sp.wait_ge(sem("stored"), 16)
                return
            sp.wait_ge(sem("scattered"), 16 * NT)
            slots = slots_x.rearrange("(j p) d -> p j d", p=P)
            for c, js in enumerate(BLOCK_GROUPS):
                sp.dma_start(xb[:, js, :], slots[:, js, :]).then_inc(sem(f"ld_blocks{c}"), 16)
            slots = slots_y.rearrange("(j p) d -> p j d", p=P)
            for c, js in enumerate(BLOCK_GROUPS):
                sp.wait_ge(sem("pr"), DENSE + js.stop)
                sp.dma_start(slots[:, js, :], ys[:, js, :]).then_inc(sem("ys_out"), 16)
            for b in range(B):
                sp.wait_ge(sem("x4"), b + 1)
                ts = slice(TPB * b, TPB * (b + 1))
                sp.dma_start(out[:, ts, :], x[:, ts, :]).then_inc(sem("stored"), 16)
            sp.wait_ge(sem("stored"), 16 * B)

        def ln_stats(v, k, src, b):
            for t in range(TPB * b, TPB * (b + 1)):
                v.bn_stats(st[:, k, t, :], src[:, t, :]).then_inc(sem("ln_stats"), 1)

        def ln_moments(v, k, b):
            v.wait_ge(sem("ln_stats"), NT * k + TPB * (b + 1))
            for t in range(TPB * b, TPB * (b + 1)):
                v.bn_aggr(mv[:, k, t, :], st[:, k, t, :]).then_inc(sem("ln_moments"), 1)

        def ln_rstd(pool, k, b):
            ts = slice(TPB * b, TPB * (b + 1))
            pool.wait_ge(sem("ln_moments"), NT * k + TPB * (b + 1))
            if k == 0:
                pool.tensor_scalar(nmean[:, ts], mv[:, k, ts, 0], -1.0, None, ALU.mult)
            pool.tensor_scalar(rs[:, k, ts], mv[:, k, ts, 1], EPS, None, ALU.add).then_inc(sem("ln_var"), 1)
            pool.wait_ge(sem("ln_var"), B * k + b + 1)
            pool.tensor_tensor(rs[:, k, ts], rs[:, k, ts], neghalf[:, ts], ALU.pow).then_inc(sem("ln_rstd"), 1)

        def ln_apply(v, k, src, dst, b):
            v.wait_ge(sem("ln_rstd"), B * k + b + 1)
            for t in range(TPB * b, TPB * (b + 1)):
                v.tensor_scalar(dst[:, t, :], src[:, t, :], mv[:, k, t, 0:1], rs[:, k, t:t + 1],
                                ALU.subtract, ALU.mult).then_inc(sem("ln_out"), 1)

        @block.gpsimd
        def _(pool):
            pool.memset(neghalf[:, :], -0.5).then_inc(sem("pool_const"), 1)
            pool.memset(ones[:, :], 1.0).then_inc(sem("pool_const"), 1)
            pool.memset(zeros[:, :], 0.0).then_inc(sem("pool_const"), 1)
            pool.wait_ge(sem("pool_const"), 2)
            for b in range(B):
                ln_rstd(pool, 0, b)
            for b in range(B):
                ln_rstd(pool, 1, b)
            pool.wait_ge(sem("ld_const"), 16)
            pool.wait_ge(sem("ld_mixw"), 16)
            pool.wait_ge(sem("decay_in"), 1)

            for i in range(NT + 3):
                if i < NT:
                    t, k = i, i % 2
                    if t >= 2:
                        pool.wait_ge(sem("y_ps"), t - 1)
                        pool.wait_ge(sem("y_gated"), t - 1)
                    x3 = xs[:, t, :].rearrange("p (h e) -> p h e", h=HEADS)
                    pool.wait_ge(sem("xs_tok"), 3 * (t // TPB + 1))
                    pool.tensor_tensor(X[:, k], x3, dtv[:, 7, t, :].unsqueeze(2).to_broadcast([P, HEADS, HP]),
                                       ALU.mult).then_inc(sem("X"), 1)
                    pool.tensor_tensor(Dx[:, k], x3, w["D"].unsqueeze(2).to_broadcast([P, HEADS, HP]),
                                       ALU.mult).then_inc(sem("Dx"), 1)
                    if t >= 2 and (t - 2) % TPB < 3:
                        pool.wait_ge(sem("state_ps"), ((t - 2) // TPB) * 3 + (t - 2) % TPB + 1)
                    pool.wait_ge(sem("L"), t + 1)
                    pool.wait_ge(sem("X"), t + 1)
                    pool.tensor_tensor(Xd[:, k], X[:, k], L[:, k, :, P - 1:P].to_broadcast([P, HEADS, HP]),
                                       ALU.mult).then_inc(sem("Xd"), 1)
                if 0 <= i - 2 < NT:
                    t = i - 2
                    pool.wait_ge(sem("ssq"), t + 1)
                    pool.tensor_scalar(rr[:, t:t + 1], ssq[:, t:t + 1], 1.0 / DI, EPS, ALU.mult,
                                       ALU.add).then_inc(sem("msq"), 1)
                    pool.wait_ge(sem("msq"), t + 1)
                    pool.tensor_tensor(rr[:, t:t + 1], rr[:, t:t + 1], neghalf[:, 0:1], ALU.pow)\
                        .then_inc(sem("rms"), 1)
                if 0 <= i - 3:
                    t = i - 3
                    pool.wait_ge(sem("o_gated"), t + 1)
                    pool.tensor_tensor(x[:, t, :], x[:, t, :], o[:, t % 2, :], ALU.add).then_inc(sem("x1"), 1)
            if stop == 1:
                pool.wait_ge(sem("x1"), NT)
                pool.nop().then_inc(sem("x_final"), NT)
                return

            for b in range(B):
                ln_rstd(pool, 2, b)
            pool.wait_ge(sem("ld_b3"), 16)
            pool.memset(wp[:, :, :], 0.0).then_inc(sem("wp_clear"), 1)
            m = [0]

            def step(ins):
                m[0] += 1
                ins.then_inc(sem("b3_step"), 1)
                pool.wait_ge(sem("b3_step"), m[0])

            step(pool.memset(b3p[:, :, :], 0.0))
            step(pool.tensor_copy(b3c[:, 0], b3f[:, :]))
            step(pool.tensor_tensor(b3r[:, :], b3f[:, :], b3c[:, 0], ALU.subtract))
            step(pool.tensor_copy(b3c[:, 1], b3r[:, :]))
            step(pool.tensor_tensor(b3c[:, 2], b3r[:, :], b3c[:, 1], ALU.subtract))
            for i in range(3):
                rows = slice(32 * (i + 1), 32 * (i + 2))
                step(pool.tensor_copy(b3p[rows].rearrange("p e d -> p (e d)"), b3c[rows, i]))
            for i in range(32):
                n, e = divmod(i, E0)
                ts = slice(n * S, (n + 1) * S)
                pool.wait_ge(sem("pr"), i + 1)
                if e == 0:
                    pool.tensor_copy(yacc[:, ts], pr[:, i % 2, :]).then_inc(sem("yacc"), 1)
                else:
                    pool.wait_ge(sem("yacc"), i)
                    pool.tensor_tensor(yacc[:, ts], yacc[:, ts], pr[:, i % 2, :], ALU.add).then_inc(sem("yacc"), 1)
            if stop == 2:
                pool.wait_ge(sem("x2"), B)
                pool.nop().then_inc(sem("x_final"), B)
                return

            pool.wait_ge(sem("x2"), B)
            pool.memset(kaug[:, :, :, :], 0.0).then_inc(sem("kaug_clear"), 1)
            pool.memset(va[:, :, :, :, :], 0.0).then_inc(sem("va_clear"), 1)
            pool.wait_ge(sem("va_clear"), 1)
            pool.memset(va[:, :, :, :, DK:DK + 1], 1.0).then_inc(sem("va_clear"), 1)
            for b in range(B):
                ln_rstd(pool, 3, b)
            for b in range(B):
                for a in range(2):
                    i = 2 * b + a
                    pool.wait_ge(sem("rope"), 2 * (i + 1))
                    if i >= 2:
                        pool.wait_ge(sem("parts"), i - 1)
                    pool.tensor_tensor(qk[:, a, :], ropet[:, 2 * a, :], ropet[:, 2 * a + 1, :], ALU.add)\
                        .then_inc(sem("qk"), 1)
                    pool.wait_ge(sem("part_hi"), i + 1)
                    pool.tensor_tensor(qk[:, a, :], qk[:, a, :], pc[:, a, 0, :], ALU.subtract).then_inc(sem("res"), 1)
                    pool.wait_ge(sem("part_mid"), i + 1)
                    pool.tensor_tensor(pc[:, a, 2, :], qk[:, a, :], pc[:, a, 1, :], ALU.subtract)\
                        .then_inc(sem("parts"), 1)
            if stop > 3:
                for b in range(B):
                    ln_rstd(pool, 4, b)
                pool.wait_ge(sem("posu"), 1)
                pool.wait_ge(sem("h4"), B)
                pool.wait_ge(sem("slots_clear"), 16)
                for t in range(NT):
                    pool.indirect_dma_start(out=slots_x[:, :], out_offset=bass.IndirectOffsetOnAxis(
                        ap=posu[:, t:t + 1], axis=0), in_=xn[:, t, :], in_offset=None).then_inc(sem("scattered"), 16)
                pool.wait_ge(sem("ys_out"), 16 * len(BLOCK_GROUPS))
                for t in range(NT):
                    pool.indirect_dma_start(out=yt[:, t, :], out_offset=None, in_=slots_y[:, :],
                                            in_offset=bass.IndirectOffsetOnAxis(ap=posu[:, t:t + 1], axis=0))\
                        .then_inc(sem(f"gathered{t // TPB}"), 16)

        @block.scalar
        def _(act):
            act.wait_ge(sem("ld_mixw"), 16)
            act.activation(siluc[:, :], w["cT"], ACT.Silu).then_inc(sem("siluc"), 1)
            for b in range(B):
                act.wait_ge(sem("ln_rstd"), b + 1)
                for t in range(TPB * b, TPB * (b + 1)):
                    act.activation(h[:, t, :], x[:, t, :], ACT.Identity, bias=nmean[:, t:t + 1])\
                        .then_inc(sem("h_centered"), 1)
                for t in range(TPB * b, TPB * (b + 1)):
                    act.wait_ge(sem("h_centered"), t + 1)
                    act.activation(h[:, t, :], h[:, t, :], ACT.Identity, scale=rs[:, 0, t:t + 1])\
                        .then_inc(sem("h_normed"), 1)
            for b in range(B):
                act.wait_ge(sem("mod0_ps"), b + 1)
                act.activation(mod0[:, b, :], ps[:, 1 + b, 0:384], ACT.Identity).then_inc(sem("mod0"), 1)
            for b in range(B):
                act.wait_ge(sem("mod1_ps"), b + 1)
                act.activation(mod1[:, b, :], ps[:, MOD1_BANK[b], :], ACT.Identity).then_inc(sem("mod0"), 1)
            for b in range(B):
                act.wait_ge(sem("xnT_ps"), b + 1)
                act.activation(hT[:, b * S:(b + 1) * S], ps[:, 6 + b % 2, :], ACT.Identity,
                               scale=w["norm_w"], bias=w["norm_b"]).then_inc(sem("hT"), 1)

            def to_tokens(b):
                for c in range(3):
                    m = 3 * b + c
                    act.wait_ge(sem("xs_ps"), m + 1)
                    src = ps[:, 6 + m % 2, :].rearrange("p (t d) -> p t d", t=TPB)
                    ts = slice(TPB * b, TPB * (b + 1))
                    dst = xs[:, ts, c * P:(c + 1) * P] if c < 2 else Bt[:, ts, :]
                    act.activation(dst, src, ACT.Identity).then_inc(sem("xs_tok"), 1)

            for b in range(B):
                for c in range(4):
                    act.wait_ge(sem("xbc_ps"), 4 * b + c + 1)
                    if b >= 1:
                        act.wait_ge(sem("xbc_silu"), 4 * (b - 1) + c + 1)
                    act.activation(acc[:, c, :], ps[:, c, :], ACT.Identity, scale=w["conv_w"][:, 4 * c + 3:4 * c + 4],
                                   bias=w["conv_b"][:, c:c + 1]).then_inc(sem("conv_last_tap"), 1)
                for i in range(2):
                    act.wait_ge(sem("z_ps"), 2 * b + i + 1)
                    t = TPB * b + 2 * i
                    act.activation(sz[:, t:t + 2, :], ps[:, 4 + i, :].rearrange("p (a d) -> p a d", a=2),
                                   ACT.Silu).then_inc(sem("sz"), 1)
                if b >= 1:
                    to_tokens(b - 1)
                for c in range(4):
                    act.wait_ge(sem("conv"), 4 * b + c + 1)
                    act.activation(xcT[:, c, b * S:(b + 1) * S], acc[:, c, :], ACT.Silu).then_inc(sem("xbc_silu"), 1)
                if b == 1:
                    act.wait_ge(sem("dt_nabs"), 1)
                    act.activation(dtv[:, 2, :, :], dtv[:, 1, :, :], ACT.Exp).then_inc(sem("dt_exp"), 1)
                    act.activation(eA[:, :], w["A_log"], ACT.Exp).then_inc(sem("dt_exp"), 1)
            to_tokens(B - 1)
            act.wait_ge(sem("acum_ps"), 1)
            act.activation(eact[:, :, :, :].rearrange("p a t h -> p (a t h)"), ps[:, 7, 0:2 * NT * HEADS],
                           ACT.Exp).then_inc(sem("eact"), 1)

            def decays(t):
                k = t % 2
                if t >= 2:
                    act.wait_ge(sem("seg_ps"), t - 1)
                for hh in range(HEADS):
                    act.activation(ua[:, k, hh, :], w["tri"], ACT.Identity, scale=av[:, t, hh:hh + 1])\
                        .then_inc(sem("ua"), 1)

            decays(0)
            for i in range(NT + 2):
                if i < NT:
                    t, k = i, i % 2
                    if t + 1 < NT:
                        decays(t + 1)
                    act.wait_ge(sem("seg_ps"), t + 1)
                    if t >= 2:
                        act.wait_ge(sem("M"), t - 1)
                        act.wait_ge(sem("Xd"), t - 1)
                    act.activation(L[:, k].rearrange("p h s -> p (h s)"), ps[:, k, :], ACT.Exp).then_inc(sem("L"), 1)
                if 0 <= i - 2:
                    t, k = i - 2, i % 2
                    act.wait_ge(sem("yT_ps"), t + 1)
                    if t >= 2:
                        act.wait_ge(sem("o_ps"), t - 1)
                    act.activation(yT[:, k].rearrange("p a s -> p (a s)"), ps[:, 6, k * 256:(k + 1) * 256],
                                   ACT.Identity).then_inc(sem("yT"), 1)
                    if t >= 1:
                        act.wait_ge(sem("ssq"), t)
                    act.activation(ysq[:, :], y[:, k, :], ACT.Square, accum_out=ssq[:, t:t + 1])\
                        .then_inc(sem("ssq"), 1)

            if stop == 1:
                return

            def hT_evac(k, layer, scale, bias):
                for b in range(B):
                    act.wait_ge(sem("xnT_ps"), B * (k - 1) + b + 1)
                    act.activation(hT[:, b * S:(b + 1) * S], ps[:, 6 + b % 2, :], ACT.Identity,
                                   scale=modT[:, scale, layer, b:b + 1], bias=modT[:, bias, layer, b:b + 1])\
                        .then_inc(sem("hT"), 1)

            hT_evac(2, 0, 4, 3)
            act.wait_ge(sem("gate_shifted"), 1)
            act.activation(rt[:, 1], rt[:, 0], ACT.Exp).then_inc(sem("gate_exp"), 1)
            for i in range(32):
                n, e = divmod(i, E0)
                act.wait_ge(sem("p1_ps"), i + 1)
                if i >= 2:
                    act.wait_ge(sem("p2_ps"), i - 1)
                act.activation(gT[:, i % 2, :], ps[:, 2 + i % 2, :], ACT.Silu, bias=w["b1"][:, e:e + 1])\
                    .then_inc(sem("h1"), 1)
                act.wait_ge(sem("p3_ps"), i + 1)
                if i >= 2:
                    act.wait_ge(sem("pr"), i - 1)
                act.activation(s3[:, i % 2, :], ps[:, 4 + i % 2, :], ACT.Identity).then_inc(sem("s3"), 1)
            for j in range(8):
                act.wait_ge(sem("sa_ps"), j + 1)
                if j >= 2:
                    act.wait_ge(sem("sg"), j - 1)
                else:
                    act.wait_ge(sem("p2_ps"), 31 + j)
                act.activation(gT[:, j % 2, :], ps[:, 2 + j % 2, :], ACT.Silu).then_inc(sem("sh"), 1)
            if stop == 2:
                return

            hT_evac(3, 1, 1, 0)

            def parts(b):
                for a in range(2):
                    i = 2 * b + a
                    act.wait_ge(sem("qk"), i + 1)
                    if b >= 1:
                        act.wait_ge(sem("parts_out"), 32 * b)
                    act.activation(pc[:, a, 0, :], qk[:, a, :], ACT.Identity).then_inc(sem("part_hi"), 1)
                    act.wait_ge(sem("res"), i + 1)
                    act.activation(pc[:, a, 1, :], qk[:, a, :], ACT.Identity).then_inc(sem("part_mid"), 1)

            def probs(u):
                kt = 3 - (u % 8) // 2
                n = S - kt * P
                k = u % 2
                act.wait_ge(sem("st_ps"), u + 1)
                if u >= 3:
                    act.wait_ge(sem("pv"), u - 2)
                act.activation(pt[:, u % 3, :, 0:n], ps[:, 4 + 2 * k:6 + 2 * k, 0:n], ACT.Exp,
                               scale=ATT_SCALE).then_inc(sem("probs"), 1)

            parts(0)
            parts(1)
            for it in range(-2, 16):
                if it in (4, 8):
                    parts(it // 4 + 1)
                if it >= 0:
                    for i in range(8):
                        probs(8 * it + i)
            if stop == 3:
                return
            for b in range(B):
                act.wait_ge(sem("xnT_ps"), B * 3 + b + 1)
                act.activation(hT[:, b * S:(b + 1) * S], ps[:, 6 + b % 2, :], ACT.Identity).then_inc(sem("hT"), 1)
            act.wait_ge(sem("top_diff"), 1)
            act.activation(rt[:, 10, :, 0], rt[:, 9, :, 0], ACT.Exp).then_inc(sem("top_exp"), 1)
            for j in range(NBLK):
                act.wait_ge(sem("p1_ps"), DENSE + j + 1)
                if j >= 2:
                    act.wait_ge(sem("gsT_ps"), j - 1)
                act.activation(gs[:, j % 2, :], ps[:, j % 2, :], ACT.Gelu).then_inc(sem("h1"), 1)

        @block.vector
        def _(v):
            v.wait_ge(sem("ld_x"), 16)
            for b in range(B + 1):
                if b < B:
                    ln_stats(v, 0, x, b)
                if b >= 1:
                    ln_moments(v, 0, b - 1)
            v.wait_ge(sem("modT_ps"), 1)
            n = [0]

            def step(ins):
                n[0] += 1
                ins.then_inc(sem("mod_step"), 1)
                v.wait_ge(sem("mod_step"), n[0])

            step(v.tensor_copy(modT[:, :, :, :].rearrange("p c l b -> p (c l b)"), ps[:, 0, 0:48]))
            g = modT[:, 2:6:3].rearrange("p i l b -> p i (l b)")
            step(v.tensor_scalar(guard_tmp[:, 0], g, 0.0, -0.5, ALU.is_ge, ALU.add))
            step(v.scalar_tensor_tensor(out=guard_tmp[:, 1], in0=g, scalar=-1.0, in1=g, op0=ALU.mult, op1=ALU.max))
            step(v.scalar_tensor_tensor(out=g, in0=guard_tmp[:, 1], scalar=0.25, in1=guard_tmp[:, 0], op0=ALU.max,
                                        op1=ALU.mult))
            v.tensor_scalar(g, g, 2.0, None, ALU.mult).then_inc(sem("modT"), 1)
            v.tensor_scalar(modT[:, 1:5:3], modT[:, 1:5:3], 1.0, None, ALU.add).then_inc(sem("modT"), 1)
            for i in range(B + 3):
                if i < B:
                    b, ts = i, slice(TPB * i, TPB * (i + 1))
                    v.wait_ge(sem("h_normed"), TPB * (b + 1))
                    v.wait_ge(sem("mod0"), b + 1)
                    v.tensor_tensor(h[:, ts, :], h[:, ts, :], mod0[:, b, D:2 * D].unsqueeze(1)
                                    .to_broadcast([P, TPB, D]), ALU.mult).then_inc(sem("h_scaled"), 1)
                if 0 <= i - 1 < B:
                    b, ts = i - 1, slice(TPB * (i - 1), TPB * i)
                    v.wait_ge(sem("h_scaled"), b + 1)
                    v.tensor_tensor(h[:, ts, :], h[:, ts, :], mod0[:, b, 0:D].unsqueeze(1)
                                    .to_broadcast([P, TPB, D]), ALU.add).then_inc(sem("h"), 1)
                if 0 <= i - 2 < B:
                    v.wait_ge(sem("h"), i - 1)
                    ln_stats(v, 1, h, i - 2)
                if 0 <= i - 3:
                    ln_moments(v, 1, i - 3)
            for b in range(B):
                ln_apply(v, 1, h, xn, b)

            d = [dtv[:, i, :, :] for i in range(8)]

            def softplus():
                m = 0
                v.wait_ge(sem("dt_ps"), 1)
                v.tensor_tensor(d[0], ps[:, 7, 0:NT * HEADS].rearrange("p (t h) -> p t h", t=NT),
                                w["dt_bias"].unsqueeze(1).to_broadcast([P, NT, HEADS]), ALU.add)\
                    .then_inc(sem("dt_step"), 1)
                yield
                v.wait_ge(sem("dt_step"), 1)
                v.scalar_tensor_tensor(out=d[1], in0=d[0], scalar=-1.0, in1=d[0], op0=ALU.mult,
                                       op1=ALU.min).then_inc(sem("dt_nabs"), 1)
                yield
                for _ in range(10):
                    yield
                v.wait_ge(sem("dt_exp"), 1)
                chain = [lambda: v.tensor_scalar(d[3], d[2], 2.0, None, ALU.add),
                         lambda: v.reciprocal(d[4], d[3]),
                         lambda: v.tensor_tensor(d[3], d[2], d[4], ALU.mult),
                         lambda: v.tensor_tensor(d[4], d[3], d[3], ALU.mult),
                         lambda: v.tensor_scalar(d[5], d[4], 1.0 / 15.0, None, ALU.mult)]
                for k in (13, 11, 9, 7, 5, 3):
                    chain.append(lambda k=k: v.scalar_tensor_tensor(out=d[5], in0=d[5], scalar=1.0 / k, in1=d[4],
                                                                    op0=ALU.add, op1=ALU.mult))
                chain += [lambda: v.scalar_tensor_tensor(out=d[6], in0=d[5], scalar=1.0, in1=d[3], op0=ALU.add,
                                                         op1=ALU.mult),
                          lambda: v.tensor_scalar(d[5], d[0], 0.0, None, ALU.max),
                          lambda: v.scalar_tensor_tensor(out=d[7], in0=d[6], scalar=2.0, in1=d[5], op0=ALU.mult,
                                                         op1=ALU.add)]
                for m, ins in enumerate(chain):
                    v.wait_ge(sem("dt_step"), m + 1)
                    ins().then_inc(sem("dt_step"), 1)
                    yield
                v.wait_ge(sem("dt_step"), len(chain) + 1)
                v.wait_ge(sem("dt_exp"), 2)
                v.scalar_tensor_tensor(out=av[:, :, :], in0=d[7], scalar=-1.0,
                                       in1=eA[:, :].unsqueeze(1).to_broadcast([P, NT, HEADS]),
                                       op0=ALU.mult, op1=ALU.mult).then_inc(sem("decay_in"), 1)
                yield

            steps = softplus()
            v.wait_ge(sem("ld_mixw"), 16)
            for b in range(B):
                for c0 in (0, 2):
                    for s in range(1, TAPS):
                        for c in (c0, c0 + 1):
                            if s == 1:
                                v.wait_ge(sem("conv_last_tap"), 4 * b + c + 1)
                            else:
                                v.wait_ge(sem("conv_tap"), 4 * (2 * b + c0 // 2) + 2 * (s - 2) + c - c0 + 1)
                            v.scalar_tensor_tensor(out=acc[:, c, s:S], in0=ps[:, c, 0:S - s],
                                                   scalar=w["conv_w"][:, 4 * c + 3 - s:4 * c + 4 - s],
                                                   in1=acc[:, c, s:S], op0=ALU.mult, op1=ALU.add)\
                                .then_inc(sem("conv_tap" if s < TAPS - 1 else "conv"), 1)
                            if b >= 1:
                                next(steps, None)
            for _ in steps:
                pass
            for i in range(2):
                v.tensor_scalar(wor[:, i, :], w["out_proj"][:, i * D:(i + 1) * D], w["rms_w"][:, i:i + 1], None,
                                ALU.mult).then_inc(sem("wor"), 1)

            def bc(a):
                return a.unsqueeze(2).to_broadcast([P, HEADS, HP])

            v.wait_ge(sem("eact"), 1)
            for i in range(NT + 3):
                if i < NT:
                    t, k = i, i % 2
                    v.wait_ge(sem("g_ps"), t + 1)
                    v.tensor_tensor(Gm[:, k, :], ps[:, 2, k * P:(k + 1) * P], w["tri"], ALU.mult).then_inc(sem("Gm"), 1)
                if 0 <= i - 1 < NT and (i - 1) % TPB < TPB - 1:
                    t, k = i - 1, (i - 1) % 2
                    c, b = t % TPB, t // TPB
                    stp = ps[:, 5, k * DI:(k + 1) * DI].rearrange("p (h e) -> p h e", h=HEADS)
                    if c == 0:
                        v.wait_ge(sem("state_ps"), 3 * b + c + 1)
                        if b >= 1:
                            v.wait_ge(sem("y_ps"), t)
                        v.tensor_copy(prev[:, k], stp).then_inc(sem("prev"), 1)
                    else:
                        v.wait_ge(sem("y_ps"), t)
                        v.tensor_tensor(prev[:, k], prev[:, 1 - k], bc(eact[:, 1, t, :]), ALU.mult)\
                            .then_inc(sem("prev_decayed"), 1)
                if i < NT:
                    t, k = i, i % 2
                    v.wait_ge(sem("Gm"), t + 1)
                    v.wait_ge(sem("L"), t + 1)
                    if t >= 2:
                        v.wait_ge(sem("y_ps"), t - 1)
                    v.tensor_tensor(M[:, k], L[:, k], Gm[:, k, :].unsqueeze(1).to_broadcast([P, HEADS, P]),
                                    ALU.mult).then_inc(sem("M"), 1)
                if 0 <= i - 1 < NT and 0 < (i - 1) % TPB < TPB - 1:
                    t, k = i - 1, (i - 1) % 2
                    c, b = t % TPB, t // TPB
                    stp = ps[:, 5, k * DI:(k + 1) * DI].rearrange("p (h e) -> p h e", h=HEADS)
                    v.wait_ge(sem("state_ps"), 3 * b + c + 1)
                    v.wait_ge(sem("prev_decayed"), 2 * b + c)
                    v.tensor_tensor(prev[:, k], prev[:, k], stp, ALU.add).then_inc(sem("prev"), 1)
                t, k = i - 1, (i - 1) % 2
                c, b = t % TPB, t // TPB
                u, l = i - 3, (i - 3) % 2
                y3 = y[:, k, :].rearrange("p (h e) -> p h e", h=HEADS)
                if 0 <= t < NT:
                    yd = ps[:, 3 + k, 0:DI].rearrange("p (h e) -> p h e", h=HEADS)
                    yo = ps[:, 3 + k, DI:2 * DI].rearrange("p (h e) -> p h e", h=HEADS)
                    v.wait_ge(sem("y_ps"), t + 1)
                    v.wait_ge(sem("Dx"), t + 1)
                    if t >= 2:
                        v.wait_ge(sem("yT_ps"), t - 1)
                        v.wait_ge(sem("ssq"), t - 1)
                    v.tensor_tensor(y3, yd, Dx[:, k], ALU.add).then_inc(sem("y_a"), 1)
                    if c > 0:
                        v.tensor_tensor(Yo[:, :, :], yo, bc(eact[:, 0, t, :]), ALU.mult).then_inc(sem("y_b"), 1)
                if u >= 0:
                    v.wait_ge(sem("o_ps"), u + 1)
                    v.wait_ge(sem("rms"), u + 1)
                    if u >= 2:
                        v.wait_ge(sem("x1"), u - 1)
                    v.scalar_tensor_tensor(out=o[:, l, :], in0=ps[:, 7, P * (1 + l):P * (2 + l)],
                                           scalar=rr[:, u:u + 1], in1=h[:, u, :], op0=ALU.mult,
                                           op1=ALU.add).then_inc(sem("o_sum"), 1)
                if 0 <= t < NT:
                    v.wait_ge(sem("y_a"), t + 1)
                    if c > 0:
                        v.wait_ge(sem("y_b"), 2 * (3 * b + c - 1) + 1)
                        v.tensor_tensor(y3, y3, Yo[:, :, :], ALU.add).then_inc(sem("y_b"), 1)
                if u >= 0:
                    v.wait_ge(sem("o_sum"), u + 1)
                    v.tensor_tensor(o[:, l, :], o[:, l, :], mod0[:, u // TPB, 2 * D:3 * D], ALU.mult)\
                        .then_inc(sem("o_gated"), 1)
                if 0 <= t < NT:
                    if c > 0:
                        v.wait_ge(sem("y_b"), 2 * (3 * b + c - 1) + 2)
                    v.wait_ge(sem("sz"), 2 * (b + 1))
                    v.tensor_tensor(y[:, k, :], y[:, k, :], sz[:, t, :], ALU.mult).then_inc(sem("y_gated"), 1)

            if stop == 1:
                return

            for b in range(B):
                v.wait_ge(sem("x1"), TPB * (b + 1))
                ln_stats(v, 2, x, b)
                ln_moments(v, 2, b)
            for b in range(B):
                ln_apply(v, 2, x, xn, b)
            q = [rt[:, i] for i in range(12)]
            one = [rt[:, i, :, 0:1] for i in range(12)]
            nr = [0]

            def rstep(ins):
                nr[0] += 1
                ins.then_inc(sem("route"), 1)
                v.wait_ge(sem("route"), nr[0])

            def bc8(a):
                return a.to_broadcast([P, NT, 8])

            iota = w["iota"].unsqueeze(1).to_broadcast([P, NT, 8])

            def first_of_largest(src, top, hot, tmp, tmp1):
                rstep(v.tensor_reduce(top, src, AX_X, ALU.max))
                rstep(v.tensor_tensor(tmp, src, bc8(top), ALU.is_ge))
                rstep(v.tensor_tensor(tmp, tmp, iota, ALU.mult))
                rstep(v.tensor_reduce(tmp1, tmp, AX_X, ALU.max))
                rstep(v.tensor_tensor(hot, tmp, bc8(tmp1), ALU.is_equal))

            logits = ps[:, 5, 0:NT * 8].rearrange("p (t e) -> p t e", e=8)
            v.wait_ge(sem("gate_ps"), 1)
            rstep(v.tensor_reduce(one[2], logits, AX_X, ALU.max))
            v.tensor_tensor(q[0], logits, bc8(one[2]), ALU.subtract).then_inc(sem("gate_shifted"), 1)
            v.wait_ge(sem("gate_exp"), 1)
            rstep(v.tensor_reduce(one[2], q[1], AX_X, ALU.add))
            rstep(v.reciprocal(one[3], one[2]))
            rstep(v.tensor_tensor(q[4], q[1], bc8(one[3]), ALU.mult))
            first_of_largest(q[4], one[2], q[5], q[7], one[3])
            rstep(v.scalar_tensor_tensor(out=q[6], in0=q[5], scalar=-2.0, in1=q[4], op0=ALU.mult, op1=ALU.add))
            first_of_largest(q[6], one[2], q[8], q[7], one[3])
            rstep(v.tensor_tensor(q[5], q[5], q[8], ALU.add))
            rstep(v.tensor_tensor(q[6], q[5], q[4], ALU.mult))
            v.wait_ge(sem("wp_clear"), 1)
            rstep(v.tensor_copy(wp[:, :, 0:8], q[6]))
            rstep(v.tensor_tensor(q[7], q[6], wp[:, :, 0:8], ALU.subtract))
            rstep(v.tensor_copy(wp[:, :, 8:16], q[7]))
            rstep(v.tensor_tensor(wp[:, :, 16:24], q[7], wp[:, :, 8:16], ALU.subtract))
            for i in range(3):
                rstep(v.tensor_copy(wp[:, :, 32 * (i + 1):32 * (i + 1) + 8], q[5]))

            def wT_evac(name):
                for b in range(B):
                    v.wait_ge(sem(f"{name}_ps"), b + 1)
                    v.tensor_copy(wT[:, b * S:(b + 1) * S], ps[:, 6 + b % 2, 0:256].bitcast(BF16))\
                        .then_inc(sem(name), 1)

            wT_evac("wT0")

            def masked(i, ready, reads, bank, name):
                n = i // 8
                v.wait_ge(sem(ready), i + 1)
                if i >= 2:
                    v.wait_ge(sem(reads[0]), reads[1] * (i - 1))
                v.tensor_tensor(xm[:, i % 2, :], hT[:, n * S:(n + 1) * S], ps[:, bank + i % 2, :], ALU.mult)\
                    .then_inc(sem(name), 1)

            def product(i):
                e = i % E0
                v.wait_ge(sem("p2_ps"), i + 1)
                v.wait_ge(sem("s3"), i + 1)
                if i >= 2:
                    v.wait_ge(sem("yacc"), i - 1)
                v.scalar_tensor_tensor(out=pr[:, i % 2, :], in0=ps[:, 6 + i % 2, :], scalar=w["b2"][:, e:e + 1],
                                       in1=s3[:, i % 2, :], op0=ALU.add, op1=ALU.mult).then_inc(sem("pr"), 1)

            masked(0, "wbc_ps", ("p3_ps", 1), 0, "xm")
            for i in range(32):
                if i + 1 < 32:
                    masked(i + 1, "wbc_ps", ("p3_ps", 1), 0, "xm")
                if i >= 1:
                    product(i - 1)
            product(31)
            v.wait_ge(sem("p3_ps"), 32)
            for j in range(8):
                v.wait_ge(sem("sh"), j + 1)
                v.wait_ge(sem("sb_ps"), j + 1)
                if j >= 2:
                    v.wait_ge(sem("z_acc"), j - 1)
                v.tensor_tensor(xm[:, j % 2, :], ps[:, 4 + j % 2, :], gT[:, j % 2, :], ALU.mult).then_inc(sem("sg"), 1)
            for n in range(B):
                ts = slice(n * S, (n + 1) * S)
                v.wait_ge(sem("z_acc"), 2 * (n + 1))
                v.wait_ge(sem("yacc"), 8 * (n + 1))
                v.tensor_tensor(yacc[:, ts], yacc[:, ts], ps[:, Z_BANK[n], :], ALU.add).then_inc(sem("y0_sum"), 1)
                v.wait_ge(sem("y0_sum"), n + 1)
                v.tensor_scalar(yacc[:, ts], yacc[:, ts], modT[:, 5, 0, n:n + 1], None, ALU.mult)\
                    .then_inc(sem("y0"), 1)
            for n in range(B):
                tt = slice(TPB * n, TPB * (n + 1))
                v.wait_ge(sem("y0T_ps"), n + 1)
                v.tensor_tensor(x[:, tt, :], x[:, tt, :], ps[:, 4 + n % 2, :].rearrange("p (t d) -> p t d", t=TPB),
                                ALU.add).then_inc(sem("x2"), 1)
            if stop == 2:
                return

            for b in range(B):
                v.wait_ge(sem("x2"), b + 1)
                ln_stats(v, 3, x, b)
                ln_moments(v, 3, b)
            for b in range(B):
                ln_apply(v, 3, x, xn, b)
            ring = [0]

            def ring_wait():
                ring[0] += 1
                v.wait_ge(sem("ring_ps"), ring[0])
                return (ring[0] - 1) % 2

            def projections(b):
                for a in range(2):
                    for half, table in enumerate(("cos", "sin")):
                        k = ring_wait()
                        if b >= 1:
                            v.wait_ge(sem("qk"), 2 * (b - 1) + a + 1)
                        v.tensor_tensor(ropet[:, 2 * a + half, :], ps[:, k, :], w[table], ALU.mult)\
                            .then_inc(sem("rope"), 1)
                k = ring_wait()
                v.wait_ge(sem("va_clear"), 2)
                if b >= 2:
                    v.wait_ge(sem("pv"), 32 * (b - 1))
                v.tensor_copy(va[:, b % 2, :, :, 0:DK], ps[:, k, :].rearrange("p (t h d) -> p t h d", t=TPB, h=NH))\
                    .then_inc(sem("va"), 1)

            def maxima(s):
                def unit(i):
                    qt, j = divmod(i, 4)
                    n = P * (qt + 1)
                    k = ring_wait()
                    if i == 0 and s >= 2:
                        v.wait_ge(sem("m_parts"), 4 * (s - 1))
                    if 16 * s + i >= 2:
                        v.wait_ge(sem("mx"), 16 * s + i - 1)
                    v.tensor_tensor_reduce(out=junk[:, i % 2, 0:n], in0=ps[:, k, 0:n], in1=w["mask"][:, (3 - qt) * P:4 * P],
                                           scale=1.0, scalar=3 * NEG, op0=ALU.add, op1=ALU.max,
                                           accum_out=mx[:, s % 2, qt, j:j + 1]).then_inc(sem("mx"), 1)
                return unit

            def max_parts(s):
                k = s % 2
                v.wait_ge(sem("mx"), 16 * (s + 1))
                v.tensor_scalar(mpc[:, k, :, :, 0], mx[:, k], -1.0, None, ALU.mult).then_inc(sem("m_parts"), 1)
                v.wait_ge(sem("m_parts"), 4 * s + 1)
                v.scalar_tensor_tensor(out=mres[:, :, :], in0=mx[:, k], scalar=-1.0, in1=mpc[:, k, :, :, 0],
                                       op0=ALU.mult, op1=ALU.subtract).then_inc(sem("m_parts"), 1)
                v.wait_ge(sem("m_parts"), 4 * s + 2)
                v.tensor_copy(mpc[:, k, :, :, 1], mres[:, :, :]).then_inc(sem("m_parts"), 1)
                v.wait_ge(sem("m_parts"), 4 * s + 3)
                v.tensor_tensor(mpc[:, k, :, :, 2], mres[:, :, :], mpc[:, k, :, :, 1], ALU.subtract)\
                    .then_inc(sem("m_parts"), 1)

            def mT_evac(s):
                k = ring_wait()
                if s >= 2:
                    v.wait_ge(sem(f"m_rows{s % 2}"), 32 * (s // 2))
                v.tensor_copy(mT[0:12, s % 2, :], ps[0:12, k, 0:256].bitcast(BF16)).then_inc(sem("mT"), 1)

            def o_evac(s):
                v.wait_ge(sem("pv"), 8 * (s + 1))
                if s >= 1:
                    v.wait_ge(sem("oT_ps"), s)
                v.tensor_copy(ot[:, :], ps[:, 3, :]).then_inc(sem("ot"), 1)

            def o_norm(s):
                b, g = divmod(s, QG)
                o4 = ps[:, 2, :].rearrange("p (q j d) -> p q j d", q=4, j=4)
                v.wait_ge(sem("oT_ps"), s + 1)
                if s >= 1:
                    v.wait_ge(sem("at"), s)
                v.reciprocal(rden[:, :, :], o4[:, :, :, DK]).then_inc(sem("rden"), 1)
                v.wait_ge(sem("rden"), s + 1)
                if g == 0 and b >= 1:
                    v.wait_ge(sem("aT_ps"), b)
                v.tensor_tensor(at[:, :, 4 * g:4 * g + 4, :], o4[:, :, :, 0:DK],
                                rden[:, :, :].unsqueeze(3).to_broadcast([P, 4, 4, DK]), ALU.mult).then_inc(sem("at"), 1)

            def attn_out(b):
                v.wait_ge(sem("aT_ps"), b + 1)
                v.tensor_copy(aT[:, :], ps[:, 2, :]).then_inc(sem("aT"), 1)
                v.wait_ge(sem("ao_ps"), b + 1)
                tt = slice(TPB * b, TPB * (b + 1))
                v.tensor_tensor(ao[:, :].rearrange("p (t d) -> p t d", t=TPB),
                                ps[:, 2, :].rearrange("p (t d) -> p t d", t=TPB),
                                mod1[:, b, 0:D].unsqueeze(1).to_broadcast([P, TPB, D]), ALU.mult).then_inc(sem("ao"), 1)
                v.wait_ge(sem("ao"), b + 1)
                v.tensor_tensor(x[:, tt, :], x[:, tt, :], ao[:, :].rearrange("p (t d) -> p t d", t=TPB), ALU.add)\
                    .then_inc(sem("x3"), 1)

            projections(0)
            projections(1)
            for it in range(-2, 16):
                if it in (4, 8):
                    projections(it // 4 + 1)
                if 0 <= it + 1 < 16:
                    mT_evac(it + 1)
                if it + 2 < 16:
                    unit = maxima(it + 2)
                    for i in range(8):
                        unit(2 * i)
                        unit(2 * i + 1)
                    max_parts(it + 2)
                if it >= 0:
                    o_evac(it)
                    o_norm(it)
                    if it % QG == QG - 1:
                        attn_out(it // QG)
            if stop == 3:
                v.wait_ge(sem("x3"), B)
                v.nop().then_inc(sem("x_final"), B)
                return

            for b in range(B):
                v.wait_ge(sem("x3"), b + 1)
                ln_stats(v, 4, x, b)
                ln_moments(v, 4, b)
            for b in range(B):
                ln_apply(v, 4, x, xn, b)
                ts = slice(TPB * b, TPB * (b + 1))
                for i, op in ((2, ALU.mult), (1, ALU.add)):
                    v.wait_ge(sem("ln_out"), NT * 3 + TPB * (b + 1))
                    if i == 1:
                        v.wait_ge(sem("h4_scaled"), b + 1)
                    v.tensor_tensor(xn[:, ts, :], xn[:, ts, :],
                                    mod1[:, b, i * D:(i + 1) * D].unsqueeze(1).to_broadcast([P, TPB, D]), op)\
                        .then_inc(sem("h4_scaled" if i == 2 else "h4"), 1)
            v.wait_ge(sem("gate1_ps"), 1)
            q[4] = logits
            first_of_largest(q[4], one[2], q[5], q[7], one[3])
            v.wait_ge(sem("rank_ps"), 1)
            d = [dp[:, i] for i in range(6)]
            flat = [dp[:, i].rearrange("p e t -> p (e t)") for i in range(6)]
            rank = ps[:, 7, 0:NT * E1].rearrange("p (e t) -> p e t", e=E1)
            rstep(v.tensor_copy(flat[0], ps[:, 7, NT * E1:2 * NT * E1]))
            rstep(v.tensor_tensor_scan(flat[1], w["segment"], flat[0], 0.0, ALU.mult, ALU.add))
            rstep(v.tensor_tensor(d[2], d[1][:, :, NT - 1:NT].to_broadcast([P, E1, NT]),
                                  w["full"].unsqueeze(1).to_broadcast([P, E1, NT]), ALU.is_gt))
            rstep(v.tensor_reduce(nblk[:, 0, :].unsqueeze(2), d[2], AX_X, ALU.add))
            rstep(v.tensor_tensor_scan(nblk[:, 1, :], ones[:, 0:E1], nblk[:, 0, :], 0.0, ALU.mult, ALU.add))
            rstep(v.tensor_tensor(nblk[:, 2, :], nblk[:, 1, :], nblk[:, 0, :], ALU.subtract))
            rstep(v.tensor_tensor(d[3], d[1], d[0], ALU.subtract))
            rstep(v.scalar_tensor_tensor(out=d[4], in0=nblk[:, 2, :].unsqueeze(2).to_broadcast([P, E1, NT]),
                                         scalar=float(P), in1=d[3], op0=ALU.mult, op1=ALU.add))
            rstep(v.tensor_tensor(d[4], d[4], rank, ALU.add))
            rstep(v.tensor_tensor(d[5], d[4], q[5].rearrange("p t e -> p e t"), ALU.mult))
            rstep(v.tensor_reduce(pos, d[5].rearrange("p e t -> p t e"), AX_X, ALU.add))
            v.tensor_scalar(posu[:, :], pos[:, :, 0], -1.0, None, ALU.add).then_inc(sem("posu"), 1)
            rstep(v.tensor_tensor(blk[:, :, :], nblk[:, 1, :].unsqueeze(1).to_broadcast([P, NBLK, E1]),
                                  w["block"].unsqueeze(2).to_broadcast([P, NBLK, E1]), ALU.is_le))
            rstep(v.tensor_reduce(blk1, blk[:, :, :], AX_X, ALU.add))
            v.tensor_scalar(expert_at[:, :], blk1[:, :, 0], float(E1 - 1), float(HID), ALU.min, ALU.mult)\
                .then_inc(sem("expert_at"), 1)
            rstep(v.scalar_tensor_tensor(out=q[6], in0=q[5], scalar=NEG, in1=q[4], op0=ALU.mult, op1=ALU.add))
            rstep(v.tensor_reduce(one[8], q[6], AX_X, ALU.max))
            v.tensor_tensor(rt[:, 9, :, 0], rt[:, 8, :, 0], rt[:, 2, :, 0], ALU.subtract).then_inc(sem("top_diff"), 1)
            v.wait_ge(sem("top_exp"), 1)
            rstep(v.tensor_scalar(rt[:, 11, :, 0], rt[:, 10, :, 0], 1.0, None, ALU.add))
            v.reciprocal(wtop[:, :], rt[:, 11, :, 0]).then_inc(sem("wtop"), 1)

            for i in range(-1, NBLK + 2):
                if 0 <= i + 1 < NBLK:
                    j = i + 1
                    v.wait_ge(sem("xT_ps"), j + 1)
                    if j >= 2:
                        v.wait_ge(sem("p1_ps"), DENSE + j - 1)
                    v.tensor_copy(xT[:, j % 2, :], ps[:, 2 + j % 2, 0:P]).then_inc(sem("xT"), 1)
                if 0 <= i - 1 < NBLK:
                    j = i - 1
                    v.wait_ge(sem("gsT_ps"), j + 1)
                    if j >= 2:
                        v.wait_ge(sem("p2_ps"), DENSE + j - 1)
                    v.tensor_copy(gsT[:, j % 2, :], ps[:, 4 + j % 2, :]).then_inc(sem("gsT"), 1)
                if 0 <= i - 2 < NBLK:
                    j = i - 2
                    v.wait_ge(sem("p2_ps"), DENSE + j + 1)
                    v.tensor_copy(ys[:, j, :], ps[:, 6 + j % 2, 0:D]).then_inc(sem("pr"), 1)
            v.wait_ge(sem("wtop"), 1)
            for b in range(B):
                ts = slice(TPB * b, TPB * (b + 1))
                v.wait_ge(sem(f"gathered{b}"), 16 * TPB)
                for t in range(TPB * b, TPB * (b + 1)):
                    v.scalar_tensor_tensor(out=yt[:, t, :], in0=yt[:, t, :], scalar=wtop[:, t:t + 1],
                                           in1=mod1[:, b, 3 * D:4 * D], op0=ALU.mult, op1=ALU.mult)\
                        .then_inc(sem("y_weighted"), 1)
                v.wait_ge(sem("y_weighted"), TPB * (b + 1))
                v.tensor_tensor(x[:, ts, :], x[:, ts, :], yt[:, ts, :], ALU.add).then_inc(sem("x4"), 1)

        @block.tensor
        def _(pe):
            pe.wait_ge(sem("siluc"), 1)
            for c in range(6):
                for layer in range(2):
                    mm = pe.matmul(ps[:, 0, (2 * c + layer) * B:(2 * c + layer + 1) * B],
                                   w[f"wmod{layer}"][:, c * D:(c + 1) * D], siluc[:, layer * B:(layer + 1) * B],
                                   start=True, stop=True)
            mm.then_inc(sem("modT_ps"), 1)
            pe.wait_ge(sem("ld_const"), 16)
            pe.wait_ge(sem("modT"), 2)
            for b in range(B):
                for n, c in enumerate((0, 1, 2)):
                    mm = pe.matmul(ps[:, 1 + b, n * D:(n + 1) * D], modT[:, c, 0, b:b + 1].to_broadcast([P, P]), ident,
                                   start=True, stop=True)
                mm.then_inc(sem("mod0_ps"), 1)
            for b in range(B):
                if b == 3:
                    pe.wait_ge(sem("mod0"), 1)
                for n, c in enumerate((2, 3, 4, 5)):
                    mm = pe.matmul(ps[:, MOD1_BANK[b], n * D:(n + 1) * D], modT[:, c, 1, b:b + 1].to_broadcast([P, P]),
                                   ident, start=True, stop=True)
                mm.then_inc(sem("mod1_ps"), 1)

            def transposes(k, b):
                pe.wait_ge(sem("ln_out"), NT * (k - 1) + TPB * (b + 1))
                if b >= 2:
                    pe.wait_ge(sem("hT"), B * (k - 1) + b - 1)
                for i in range(TPB):
                    mm = pe.transpose(ps[:, 6 + b % 2, i * P:(i + 1) * P], xn[:, TPB * b + i, :], ident)
                mm.then_inc(sem("xnT_ps"), 1)

            pe.wait_ge(sem("mod0"), 2 * B)
            for b in range(B):
                transposes(1, b)

            def to_tokens(b):
                for c in range(3):
                    m = 3 * b + c
                    pe.wait_ge(sem("xbc_silu"), 4 * b + c + 1)
                    if m >= 2:
                        pe.wait_ge(sem("xs_tok"), m - 1)
                    elif m == 1:
                        pe.wait_ge(sem("dt_step"), 1)
                    for i in range(TPB):
                        mm = pe.transpose(ps[:, 6 + m % 2, i * P:(i + 1) * P],
                                          xcT[:, c, b * S + i * P:b * S + (i + 1) * P], ident)
                    mm.then_inc(sem("xs_ps"), 1)

            for b in range(B):
                pe.wait_ge(sem("hT"), b + 1)
                for c in range(4):
                    if b >= 1:
                        pe.wait_ge(sem("conv"), 4 * (b - 1) + c + 1)
                    pe.matmul(ps[:, c, :], w["in_proj"][:, DI + c * P:DI + (c + 1) * P], hT[:, b * S:(b + 1) * S],
                              start=True, stop=True).then_inc(sem("xbc_ps"), 1)
                for i in range(2):
                    if b >= 1:
                        pe.wait_ge(sem("sz"), 2 * (b - 1) + i + 1)
                    for j in range(2):
                        t = TPB * b + 2 * i + j
                        mm = pe.matmul(ps[:, 4 + i, j * DI:(j + 1) * DI], hT[:, t * P:(t + 1) * P],
                                       w["in_proj"][:, 0:DI], start=True, stop=True)
                    mm.then_inc(sem("z_ps"), 1)
                if b == 0:
                    pe.wait_ge(sem("hT"), B)
                    for t in range(NT):
                        mm = pe.matmul(ps[:, 7, t * HEADS:(t + 1) * HEADS], hT[:, t * P:(t + 1) * P],
                                       w["in_proj"][:, 768:772], start=True, stop=True)
                    mm.then_inc(sem("dt_ps"), 1)
                else:
                    to_tokens(b - 1)
            to_tokens(B - 1)

            pe.wait_ge(sem("decay_in"), 1)
            pe.wait_ge(sem("pool_const"), 2)
            pe.wait_ge(sem("xs_tok"), 12)
            a2 = av[:, :, :].rearrange("p t h -> p (t h)")
            pe.matmul(ps[:, 7, 0:64], w["tri"], a2, start=True, stop=True)
            pe.matmul(ps[:, 7, 64:128], ones[:, :], a2, start=True, stop=True).then_inc(sem("acum_ps"), 1)

            pe.wait_ge(sem("conv"), 16)
            pe.wait_ge(sem("sz"), 8)
            for i in range(NT + 3):
                if i < NT:
                    t, k = i, i % 2
                    tok = slice(t * P, (t + 1) * P)
                    pe.wait_ge(sem("ua"), HEADS * (t + 1))
                    if t >= 2:
                        pe.wait_ge(sem("L"), t - 1)
                    pe.matmul(ps[:, k, :], w["after"], ua[:, k].rearrange("p h s -> p (h s)"), start=True,
                              stop=True).then_inc(sem("seg_ps"), 1)
                    if t >= 1:
                        pe.wait_ge(sem("Gm"), t)
                    pe.wait_ge(sem("xbc_silu"), 4 * (t // TPB + 1))
                    pe.matmul(ps[:, 2, k * P:(k + 1) * P], xcT[:, 2, tok], xcT[:, 3, tok], start=True,
                              stop=True).then_inc(sem("g_ps"), 1)
                if 0 <= i - 2 < NT:
                    t, k = i - 2, i % 2
                    pe.wait_ge(sem("y_gated"), t + 1)
                    if t >= 1:
                        pe.wait_ge(sem("yT"), t)
                    for q in range(2):
                        mm = pe.transpose(ps[:, 6, k * 256 + q * P:k * 256 + (q + 1) * P], y[:, k, q * P:(q + 1) * P],
                                          ident)
                    mm.then_inc(sem("yT_ps"), 1)
                if 0 <= i - 1 < NT:
                    t, k = i - 1, (i - 1) % 2
                    c, b = t % TPB, t // TPB
                    tok = slice(t * P, (t + 1) * P)
                    if c < TPB - 1:
                        pe.wait_ge(sem("Xd"), t + 1)
                        if t >= 1:
                            pe.wait_ge(sem("prev"), 3 * b + c)
                        pe.matmul(ps[:, 5, k * DI:(k + 1) * DI], Bt[:, t, :], Xd[:, k].rearrange("p h e -> p (h e)"),
                                  start=True, stop=True).then_inc(sem("state_ps"), 1)
                    pe.wait_ge(sem("M"), t + 1)
                    pe.wait_ge(sem("X"), t + 1)
                    if t >= 2:
                        pe.wait_ge(sem("y_gated"), t - 1)
                    if c > 0:
                        pe.wait_ge(sem("prev"), 3 * b + c)
                        pe.matmul(ps[:, 3 + k, DI:2 * DI], xcT[:, 3, tok],
                                  prev[:, 1 - k].rearrange("p h e -> p (h e)"), start=True, stop=True)
                    for hh in range(HEADS):
                        mm = pe.matmul(ps[:, 3 + k, hh * HP:(hh + 1) * HP], M[:, k, hh, :], X[:, k, hh, :],
                                       start=True, stop=True)
                    mm.then_inc(sem("y_ps"), 1)
                if 0 <= i - 3:
                    t, k = i - 3, (i - 3) % 2
                    pe.wait_ge(sem("yT"), t + 1)
                    if t >= 1:
                        pe.wait_ge(sem("o_sum"), t)
                    else:
                        pe.wait_ge(sem("wor"), 2)
                        pe.wait_ge(sem("eact"), 1)
                    for q in range(2):
                        mm = pe.matmul(ps[:, 7, P * (1 + k):P * (2 + k)], yT[:, k, q, :], wor[:, q, :],
                                       start=(q == 0), stop=(q == 1))
                    mm.then_inc(sem("o_ps"), 1)
            if stop == 1:
                return

            def router(k, weights, name):
                for b in range(B):
                    transposes(k, b)
                logits(k, weights, name)

            def logits(k, weights, name):
                for b in range(B):
                    pe.wait_ge(sem("hT"), B * (k - 1) + b + 1)
                    for t in range(TPB * b, TPB * (b + 1)):
                        mm = pe.matmul(ps[:, 5, 8 * t:8 * t + 8], hT[:, t * P:(t + 1) * P], weights, start=True,
                                       stop=True)
                mm.then_inc(sem(name), 1)

            def weights_T(ready, name):
                pe.wait_ge(sem("route"), ready)
                for b in range(B):
                    if b >= 2:
                        pe.wait_ge(sem(name), b - 1)
                    for i in range(TPB):
                        mm = pe.transpose(ps[:, 6 + b % 2, i * 64:(i + 1) * 64].bitcast(BF16), wp[:, TPB * b + i, :],
                                          identb)
                    mm.then_inc(sem(f"{name}_ps"), 1)

            pe.wait_ge(sem("yT"), NT)
            pe.wait_ge(sem("x1"), NT)
            pe.wait_ge(sem("ld_moe0"), 16)
            router(2, w["gate"], "gate_ps")
            pe.wait_ge(sem("ld_bconst"), 16)
            weights_T(ROUTE0, "wT0")
            pe.wait_ge(sem("b3_step"), 8)

            def spread(i, sel, rows, name, reads):
                n, e = divmod(i, 8)
                pe.wait_ge(sem(WT[name]), n + 1)
                if i >= 2:
                    pe.wait_ge(sem(reads), i - 1)
                pe.matmul(ps[:, i % 2, :], sel[0:rows, e * P:(e + 1) * P], wT[0:rows, n * S:(n + 1) * S],
                          start=True, stop=True).then_inc(sem(name), 1)

            WT = {"wbc_ps": "wT0", "hot_ps": "wT1"}

            def expert_in(i):
                n, e = divmod(i, E0)
                pe.wait_ge(sem("xm"), i + 1)
                if i >= 2:
                    pe.wait_ge(sem("h1"), i - 1)
                    pe.wait_ge(sem("s3"), i - 1)
                pe.matmul(ps[:, 2 + i % 2, :], w["w1"][:, e * D:(e + 1) * D], xm[:, i % 2, :], start=True,
                          stop=True).then_inc(sem("p1_ps"), 1)
                pe.matmul(ps[:, 4 + i % 2, :], w["w3"][:, e * D:(e + 1) * D], xm[:, i % 2, :], start=True, stop=False)
                pe.matmul(ps[:, 4 + i % 2, :], b3p[0:104, e, :], wT[0:104, n * S:(n + 1) * S], start=False,
                          stop=True).then_inc(sem("p3_ps"), 1)

            def expert_out(i):
                e = i % E0
                pe.wait_ge(sem("h1"), i + 1)
                if i >= 2:
                    pe.wait_ge(sem("pr"), i - 1)
                pe.matmul(ps[:, 6 + i % 2, :], w["w2"][:, e * D:(e + 1) * D], gT[:, i % 2, :], start=True,
                          stop=True).then_inc(sem("p2_ps"), 1)

            spread(0, w["sel0"], 104, "wbc_ps", "xm")
            spread(1, w["sel0"], 104, "wbc_ps", "xm")
            pe.wait_ge(sem("wT0"), B)
            for i in range(32):
                expert_in(i)
                if i + 2 < 32:
                    spread(i + 2, w["sel0"], 104, "wbc_ps", "xm")
                if i >= 1:
                    expert_out(i - 1)
            expert_out(31)
            pe.wait_ge(sem("h1"), 32)
            pe.wait_ge(sem("s3"), 32)

            def shared_out(j):
                n, i = divmod(j, 2)
                pe.wait_ge(sem("sg"), j + 1)
                if j == 0:
                    pe.wait_ge(sem("pr"), 32)
                pe.matmul(ps[:, Z_BANK[n], :], w["sw3"][:, i * D:(i + 1) * D],
                          xm[:, j % 2, :], start=(i == 0), stop=(i == 1)).then_inc(sem("z_acc"), 1)

            for j in range(8):
                n, i = divmod(j, 2)
                ts = slice(n * S, (n + 1) * S)
                if j >= 2:
                    pe.wait_ge(sem("sh"), j - 1)
                    pe.wait_ge(sem("sg"), j - 1)
                pe.matmul(ps[:, 2 + j % 2, :], w["sw1"][:, i * P:(i + 1) * P], hT[:, ts], start=True,
                          stop=True).then_inc(sem("sa_ps"), 1)
                pe.matmul(ps[:, 4 + j % 2, :], w["sw2"][:, i * P:(i + 1) * P], hT[:, ts], start=True,
                          stop=True).then_inc(sem("sb_ps"), 1)
                if j >= 1:
                    shared_out(j - 1)
            shared_out(7)
            for n in range(B):
                pe.wait_ge(sem("y0"), n + 1)
                if n >= 2:
                    pe.wait_ge(sem("x2"), n - 1)
                for i in range(TPB):
                    mm = pe.transpose(ps[:, 4 + n % 2, i * P:(i + 1) * P], yacc[:, n * S + i * P:n * S + (i + 1) * P],
                                      ident)
                mm.then_inc(sem("y0T_ps"), 1)
            if stop == 2:
                return

            pe.wait_ge(sem("ld_attn"), 16)
            pe.wait_ge(sem("y0"), B)
            for b in range(B):
                transposes(3, b)
            pe.wait_ge(sem("hT"), B * 3)
            pe.wait_ge(sem("x2"), B)
            ring = [0]
            read = []

            def ring_bank(name, count):
                if len(read) >= 2:
                    pe.wait_ge(sem(read[-2][0]), read[-2][1])
                read.append((name, count))
                return (len(read) - 1) % 2

            def projections(b):
                for a, n in enumerate("qk"):
                    for half in range(2):
                        k = ring_bank("rope", 4 * b + 2 * a + half + 1)
                        pe.matmul(ps[:, k, :], w[f"w{n}" + "s" * half], hT[:, b * S:(b + 1) * S], start=True,
                                  stop=True).then_inc(sem("ring_ps"), 1)
                k = ring_bank("va", b + 1)
                for i in range(TPB):
                    t = TPB * b + i
                    mm = pe.matmul(ps[:, k, i * P:(i + 1) * P], hT[:, t * P:(t + 1) * P], w["wv"], start=True,
                                   stop=True)
                mm.then_inc(sem("ring_ps"), 1)

            def scores(s, i):
                b, g = divmod(s, QG)
                qt, j = divmod(i, 4)
                n = P * (qt + 1)
                if g == 0 and i == 0:
                    pe.wait_ge(sem(f"aug{b % 2}"), 16 * 24 * (b // 2 + 1))
                    pe.wait_ge(sem("k_ones"), 32)
                k = ring_bank("mx", 16 * s + i + 1)
                pe.matmul(ps[:, k, 0:n], qaug[0:KR, b % 2, 2 * g + j // 2, qt * P:(qt + 1) * P],
                          kaug[0:KR, b % 2, 4 * g + j, 0:n], start=True, stop=True).then_inc(sem("ring_ps"), 1)

            def maxima_T(s):
                pe.wait_ge(sem("m_parts"), 4 * (s + 1))
                k = ring_bank("mT", s + 1)
                for qt in range(4):
                    mm = pe.transpose(ps[0:12, k, 64 * qt:64 * (qt + 1)].bitcast(BF16),
                                      mpc[:, s % 2, qt].rearrange("p j i -> p (j i)"), identb)
                mm.then_inc(sem("ring_ps"), 1)

            def scores_T(u):
                s, i = divmod(u, 8)
                b, g = divmod(s, QG)
                kt, jp = 3 - i // 2, i % 2
                n = S - kt * P
                if i == 0:
                    pe.wait_ge(sem(f"m_rows{s % 2}"), 32 * (s // 2 + 1))
                if u >= 2:
                    pe.wait_ge(sem("probs"), u - 1)
                for hh in range(2):
                    bank = 4 + 2 * (u % 2) + hh
                    pe.matmul(ps[:, bank, 0:P], identb, w["causal"], start=True, stop=True)
                    mm = pe.matmul(ps[:, bank, 0:n], kaug[0:KM, b % 2, 4 * g + 2 * jp + hh, kt * P:(kt + 1) * P],
                                   qaug[0:KM, b % 2, 2 * g + jp, kt * P:S], start=False, stop=True,
                                   skip_group_check=True)
                mm.then_inc(sem("st_ps"), 1)

            def values(u):
                s, i = divmod(u, 8)
                b, g = divmod(s, QG)
                kt, jp = 3 - i // 2, i % 2
                n = S - kt * P
                if i == 0 and s >= 1:
                    pe.wait_ge(sem("ot"), s)
                pe.wait_ge(sem("probs"), u + 1)
                pe.wait_ge(sem("va"), b + 1)
                for hh in range(2):
                    j = 2 * jp + hh
                    mm = pe.matmul(ps[32 * j:32 * j + 32, 3, kt * P:S], va[:, b % 2, kt, 4 * g + j, :],
                                   pt[:, u % 3, hh, 0:n], start=(kt == 3), stop=True, skip_group_check=True)
                mm.then_inc(sem("pv"), 1)

            def o_T(s):
                pe.wait_ge(sem("ot"), s + 1)
                if s >= 1:
                    pe.wait_ge(sem("at"), s)
                for qt in range(4):
                    mm = pe.transpose(ps[:, 2, qt * P:(qt + 1) * P], ot[:, qt * P:(qt + 1) * P], ident)
                mm.then_inc(sem("oT_ps"), 1)

            def attn_out(b):
                pe.wait_ge(sem("at"), 4 * (b + 1))
                for qt in range(4):
                    mm = pe.transpose(ps[:, 2, qt * P:(qt + 1) * P], at[:, qt].rearrange("p h d -> p (h d)"), ident)
                mm.then_inc(sem("aT_ps"), 1)
                pe.wait_ge(sem("aT"), b + 1)
                for qt in range(4):
                    mm = pe.matmul(ps[:, 2, qt * P:(qt + 1) * P], aT[:, qt * P:(qt + 1) * P], w["wo"], start=True,
                                   stop=True)
                mm.then_inc(sem("ao_ps"), 1)

            projections(0)
            projections(1)
            for it in range(-2, 16):
                if it in (4, 8):
                    projections(it // 4 + 1)
                if 0 <= it + 1 < 16:
                    maxima_T(it + 1)
                for i in range(8):
                    if it + 2 < 16:
                        scores(it + 2, 2 * i)
                        scores(it + 2, 2 * i + 1)
                    if it >= 0:
                        scores_T(8 * it + i)
                        if i >= 1:
                            values(8 * it + i - 1)
                if it >= 0:
                    values(8 * it + 7)
                    o_T(it)
                    if it % QG == QG - 1:
                        attn_out(it // QG)
            if stop == 3:
                return

            pe.wait_ge(sem("ao"), B)
            pe.wait_ge(sem("probs"), 128)
            pe.wait_ge(sem("ld_moe1"), 16)
            for b in range(B):
                pe.wait_ge(sem("h4"), b + 1)
                transposes(4, b)
            logits(4, w["wr"], "gate1_ps")
            pe.wait_ge(sem("route"), ROUTE1)
            hot = rt[:, 5].rearrange("p t e -> p e t")
            pe.matmul(ps[:, 7, 0:NT * E1], w["tri"], hot, start=True, stop=True)
            pe.matmul(ps[:, 7, NT * E1:2 * NT * E1], ones[:, :], hot, start=True, stop=True).then_inc(sem("rank_ps"), 1)
            pe.wait_ge(sem("expert_at"), 1)
            at_w = {}
            for i in range(-1, NBLK + 2):
                if 0 <= i + 1 < NBLK:
                    j = i + 1
                    for c, js in enumerate(BLOCK_GROUPS):
                        if js.start == j:
                            pe.wait_ge(sem(f"ld_blocks{c}"), 16)
                    if j >= 2:
                        pe.wait_ge(sem("xT"), j - 1)
                    pe.transpose(ps[:, 2 + j % 2, 0:P], xb[:, j, :], ident).then_inc(sem("xT_ps"), 1)
                if 0 <= i < NBLK:
                    j = i
                    at_w[j] = pe.value_load(expert_at[0:1, j:j + 1], min_val=0, max_val=(E1 - 1) * HID)
                    pe.wait_ge(sem("xT"), j + 1)
                    if j >= 2:
                        pe.wait_ge(sem("h1"), DENSE + j - 1)
                    pe.matmul(ps[:, j % 2, :], xT[:, j % 2, :], w["W1"][:, bass.ds(at_w[j], HID)], start=True,
                              stop=True).then_inc(sem("p1_ps"), 1)
                if 0 <= i - 1 < NBLK:
                    j = i - 1
                    pe.wait_ge(sem("h1"), DENSE + j + 1)
                    if j >= 2:
                        pe.wait_ge(sem("gsT"), j - 1)
                    for q in range(4):
                        mm = pe.transpose(ps[:, 4 + j % 2, q * P:(q + 1) * P], gs[:, j % 2, q * P:(q + 1) * P], ident)
                    mm.then_inc(sem("gsT_ps"), 1)
                if 0 <= i - 2 < NBLK:
                    j = i - 2
                    pe.wait_ge(sem("gsT"), j + 1)
                    if j >= 2:
                        pe.wait_ge(sem("pr"), DENSE + j - 1)
                    elif j == 0:
                        pe.wait_ge(sem("posu"), 1)
                    for q in range(4):
                        mm = pe.matmul(ps[:, 6 + j % 2, 0:D], gsT[:, j % 2, q * P:(q + 1) * P],
                                       w["W2"][:, bass.ds(at_w[j] + q * D, D)], start=(q == 0), stop=(q == 3))
                    mm.then_inc(sem("p2_ps"), 1)


def shape_constants():
    import numpy as np

    k = np.arange(P)
    pos = np.arange(S, dtype=np.float32)
    inv = np.float32(10000.0) ** (-np.arange(0, DK, 2, dtype=np.float32) / np.float32(DK))
    ang = (pos[:, None] * inv[None, :]).astype(np.float32)
    d = np.arange(P) % DK
    cos = np.cos(ang)[:, d // 2].T
    sin = np.sin(ang)[:, d // 2].T * np.where(d % 2 == 0, -1.0, 1.0)[:, None]
    mask = np.zeros((P, 4 * P), np.float32)
    mask[:, 3 * P:4 * P] = np.where(k[None, :] > k[:, None], NEG, 0.0)
    const = {
        "ident": np.eye(P), "tri": k[:, None] <= k[None, :], "after": k[:, None] > k[None, :],
        "cos": cos, "sin": sin, "iota": np.broadcast_to(8.0 - np.arange(8), (P, 8)), "mask": mask,
        "segment": np.broadcast_to(np.arange(NT * E1) % NT > 0, (P, NT * E1)),
        "full": np.broadcast_to(P * np.arange(NT), (P, NT)),
        "block": np.broadcast_to(np.arange(NBLK), (P, NBLK)),
    }
    sel0 = np.zeros((P, 8, P))
    for e in range(8):
        for piece in range(3):
            sel0[8 * piece + e, e, :] = 1.0
    sel1 = np.zeros((P, 8, P))
    for e in range(8):
        sel1[e, e, :] = 1.0
    bconst = {
        "identb": np.eye(P), "causal": np.where(k[:, None] > k[None, :], NEG, 0.0),
        "sel0": sel0.reshape(P, -1), "sel1": sel1.reshape(P, -1),
    }
    fc = np.concatenate([np.asarray(const[n], np.float32) for n, _ in PACKS["const"]], axis=1)
    bc = np.concatenate([np.asarray(bconst[n], np.float32) for n, _ in BPACK], axis=1).astype(np.dtype("bfloat16"))
    kones = np.zeros((6, NH, S), np.float32)
    kones[0:3, 0::2] = 1.0
    kones[3:6, 1::2] = 1.0
    return fc, bc, kones.astype(np.dtype("bfloat16"))


def lay_out(i):
    import numpy as np

    a = {k: np.asarray(v) for k, v in i.items()}

    def rows(v):
        return np.broadcast_to(v, (P, v.shape[-1]))

    def cols(v):
        return v.reshape(-1, P).T

    def experts(wt):
        return wt.transpose(2, 0, 1).reshape(P, -1)

    fields = {
        "cT": np.concatenate([a["L0_c"].T, a["L1_c"].T], axis=1),
        "wmod0": a["L0_wmod"], "wmod1": a["L1_wmod"],
        "norm_w": cols(a["L0_attn_norm_w"]), "norm_b": cols(a["L0_attn_norm_b"]),
        "in_proj": a["L0_attn_in_proj_w"].T,
        "conv_w": a["L0_attn_conv_w"].reshape(4, P, TAPS).transpose(1, 0, 2).reshape(P, -1),
        "conv_b": cols(a["L0_attn_conv_b"]),
        "dt_bias": rows(a["L0_attn_dt_bias"]), "A_log": rows(a["L0_attn_A_log"]), "D": rows(a["L0_attn_D"]),
        "rms_w": cols(a["L0_attn_rms_w"]),
        "out_proj": a["L0_attn_out_proj_w"].T.reshape(2, P, D).transpose(1, 0, 2).reshape(P, -1),
        "gate": a["L0_ffn_gate_w"].T,
        "w1": experts(a["L0_ffn_w1"]), "w2": experts(a["L0_ffn_w2"]), "w3": experts(a["L0_ffn_w3"]),
        "b1": a["L0_ffn_b1"].T, "b2": a["L0_ffn_b2"].T,
        "sw1": a["L0_ffn_sw1"].T, "sw2": a["L0_ffn_sw2"].T,
        "sw3": a["L0_ffn_sw3"].T.reshape(2, P, D).transpose(1, 0, 2).reshape(P, -1),
        "wr": a["L1_ffn_Wr"],
        "W1": a["L1_ffn_W1"].transpose(1, 0, 2).reshape(P, -1),
        "W2": a["L1_ffn_W2"].reshape(E1, 4, P, D).transpose(2, 0, 1, 3).reshape(P, -1),
    }
    swap = np.arange(P) ^ 1
    for n in "qkvo":
        wt = a[f"L1_attn_W_{n}"]
        fields["w" + n] = wt.T
        if n in "qk":
            fields["w" + n + "s"] = wt[swap].T
    packs = {
        f"{pack}_in": np.ascontiguousarray(np.concatenate([fields[n] for n, _ in PACKS[pack]], axis=1))
        for pack in ("mixw", "moe0", "attn", "moe1")
    }
    packs["x_in"] = np.ascontiguousarray(a["L0_attn_x"].reshape(NT, P, D).transpose(1, 0, 2))
    b3 = np.zeros((P, E0, D), np.float32)
    for piece in range(3):
        for e in range(E0):
            b3[32 + 32 * piece + e, e, :] = a["L0_ffn_b3"][e]
    packs["b3_in"] = b3
    packs["const_in"], packs["bconst_in"], packs["kones_in"] = shape_constants()
    return packs


def kernel(**inputs):
    import concourse.bacc as bacc
    import numpy as np
    from concourse.bass_utils import run_bass_kernel_spmd

    nc = bacc.Bacc("TRN2", target_bir_lowering=False, num_devices=1)
    arrays = lay_out(inputs)
    args = {n: nc.dram_tensor(n, v.shape, mybir.dt.from_np(v.dtype), kind="ExternalInput").ap()
            for n, v in arrays.items()}
    out = nc.dram_tensor("y_out", (P, NT, D), F32, kind="ExternalOutput").ap()
    adaln_kernel(nc, out=out, **args)
    got = run_bass_kernel_spmd(nc, [arrays], core_ids=[0]).results[0]["y_out"]
    return np.ascontiguousarray(np.asarray(got).transpose(1, 0, 2)).reshape(B, S, D)
```

```python
from contextlib import ExitStack

import concourse.bass as bass
from concourse import mybir

F32 = mybir.dt.float32
BF16 = mybir.dt.bfloat16
ALU = mybir.AluOpType
ACT = mybir.ActivationFunctionType
AX_X = mybir.AxisListType.X

P = 128
B, S, D = 4, 512, 128
TPB = S // P
NT = B * TPB
NTOK = B * S
EPS = 1e-5
DI, HEADS, HP = 256, 4, 64
TAPS = 4
E0, E1 = 8, 8
HID = 512
NH, DK = 16, 8
QG = NH // 4
PIECES = 6
KR = 2 * PIECES * DK
NBLK = NT + E1 - 1
KM = KR + 6
VW = DK + 1
ATT_SCALE = float(DK) ** -0.5
DENSE = B * E0
NEG = -1e30
MOD1_BANK = (5, 6, 7, 1)
Z_BANK = (4, 5, 6, 7)
Y0T_BANK = (0, 1, 6, 7)
ROUTE0, ROUTE1 = 21, 26
CHOSEN = 2.0 ** -120
SHARED_AT = (11, 14, 18, 21)
ROW = D + 4

PACKS = {
    "mod": [("cT", 8), ("wmod0", 768), ("wmod1", 768)],
    "mixw": [("norm_w", 1), ("norm_b", 1), ("in_proj", 772),
             ("conv_w", 16), ("conv_b", 4), ("dt_bias", 4), ("A_log", 4), ("D", 4), ("rms_w", 2),
             ("out_proj", 256)],
    "moe0": [("gate", 8), ("w1", 1024), ("w2", 1024), ("w3", 1024), ("b1", 8), ("b2", 8), ("b3", 8),
             ("sw1", 256), ("sw2", 256), ("sw3", 256)],
    "attn": [("wq", 128), ("wqs", 128), ("wk", 128), ("wks", 128), ("wv", 128), ("wo", 128)],
    "moe1": [("wr", 8), ("W1", 4096), ("W2", 4096)],
    "const": [("ident", 128), ("tri", 128), ("after", 128), ("cos", 512), ("sin", 512), ("iota", 8),
              ("mask", 512), ("segment", NT * E1), ("full", NT), ("block", NBLK), ("number", NT), ("spare", NBLK)],
}
BPACK = [("identb", 128), ("causal", 128), ("sel0", 1024)]


def offsets(fields):
    out, at = {}, 0
    for name, width in fields:
        out[name] = (at, at + width)
        at += width
    return out, at


def adaln_kernel(nc, x_in, mod_in, mixw_in, moe0_in, attn_in, moe1_in, const_in, bconst_in, kones_in, out):
    with ExitStack() as ctx:
        def sb(name, shape, dt=F32):
            return ctx.enter_context(nc.sbuf_tensor(name, shape, dt))

        sems = {}

        def sem(name):
            if name not in sems:
                sems[name] = ctx.enter_context(nc.semaphore(name))
            return sems[name]

        ps = ctx.enter_context(nc.psum_tensor("ps", [P, 8, 512], F32))

        w = {}
        packed = {}
        for pack, fields in PACKS.items():
            off, total = offsets(fields)
            if pack == "moe1":
                continue
            t = packed[pack] = sb(pack, [P, total])
            for name, (lo, hi) in off.items():
                w[name] = t[:, lo:hi]
        off, total = offsets(BPACK)
        bconst = sb("bconst", [P, total], BF16)
        for name, (lo, hi) in off.items():
            w[name] = bconst[:, lo:hi]
        ident, identb = w["ident"], w["identb"]

        x = sb("x", [P, NT, D])
        rows = sb("rows", [P, NT, ROW])
        xn = rows[:, :, 0:D]
        hT = sb("hT", [P, NTOK])
        siluc = sb("siluc", [P, 8])
        modT = sb("modT", [P, 6, 2, B])
        mod0 = sb("mod0", [P, B, 3 * D])
        mod1 = sb("mod1", [P, B, 4 * D])
        zeros = sb("zeros", [P, ROW])
        guard_tmp = sb("guard_tmp", [P, 2, 2, 2 * B])
        neghalf = sb("neghalf", [P, NT])
        ones = sb("ones", [P, P])
        LN = 5
        st = sb("st", [P, LN, NT, 6])
        mv = sb("mv", [P, LN, NT, 2])
        rs = sb("rs", [P, LN, NT])
        nmean = sb("nmean", [P, NT])
        ARENA = 31328
        KAUG = ARENA - NH * S
        VA = KAUG - 2 * TPB * NH * 32
        arena = sb("arena", [P, ARENA])

        class Area:
            def __init__(self, room, size):
                self.room, self.size, self.at = room, size, 0

            def take(self, n, dt=F32):
                words = n if dt == F32 else n // 2
                v = self.room[:, self.at:self.at + words]
                self.at += words
                assert self.at <= self.size, self.at
                return v if dt == F32 else v.bitcast(dt)

        ar = Area(arena, ARENA)
        xcT = ar.take(4 * NTOK).rearrange("p (c t) -> p c t", c=4)
        acc0 = ar.take(4 * S).rearrange("p (c t) -> p c t", c=4)
        h = ar.take(NT * D).rearrange("p (t d) -> p t d", d=D)
        sz = ar.take(NT * DI).rearrange("p (t d) -> p t d", d=DI)
        xs = ar.take(NT * DI).rearrange("p (t d) -> p t d", d=DI)
        Bt = ar.take(NT * D).rearrange("p (t d) -> p t d", d=D)
        wor = sb("wor", [P, 2, D])
        eA = sb("eA", [P, HEADS])
        ssq = sb("ssq", [P, NT])
        rr = sb("rr", [P, NT])

        def heads(v):
            return v.rearrange("p (k h s) -> p k h s", k=2, h=HEADS)

        dtv = ar.take(8 * NT * HEADS).rearrange("p (i t h) -> p i t h", i=8, h=HEADS)
        av = ar.take(NT * HEADS).rearrange("p (t h) -> p t h", h=HEADS)
        eact = ar.take(2 * NT * HEADS).rearrange("p (i t h) -> p i t h", i=2, h=HEADS)
        acc = [acc0, arena[:, ar.at:ar.at + 4 * S].rearrange("p (c t) -> p c t", c=4)]
        ua = heads(ar.take(2 * HEADS * P))
        L = heads(ar.take(2 * HEADS * P))
        M = heads(ar.take(2 * HEADS * P))
        Gm = ar.take(2 * P).rearrange("p (k s) -> p k s", k=2)
        X = heads(ar.take(2 * DI))
        Xd = heads(ar.take(2 * DI))
        Dx = heads(ar.take(2 * DI))
        prev = heads(ar.take(2 * DI))
        Yo = ar.take(DI).rearrange("p (h s) -> p h s", h=HEADS)
        y = ar.take(2 * DI).rearrange("p (k s) -> p k s", k=2)
        ysq = ar.take(DI)
        yT = ar.take(2 * DI).rearrange("p (k i s) -> p k i s", k=2, i=2)
        o = ar.take(2 * D).rearrange("p (k s) -> p k s", k=2)

        ar = Area(arena, ARENA)
        off, total = offsets(PACKS["moe1"])
        packed["moe1"] = ar.take(total)
        for name, (lo, hi) in off.items():
            w[name] = packed["moe1"][:, lo:hi]
        later = ar.at
        rt = ar.take(12 * NT * 8).rearrange("p (i t e) -> p i t e", i=12, e=8)
        wp = ar.take(NT * P, BF16).rearrange("p (t r) -> p t r", t=NT)
        wT = ar.take(NTOK, BF16)
        xm = ar.take(2 * S).rearrange("p (k t) -> p k t", k=2)
        gT = ar.take(4 * S).rearrange("p (k t) -> p k t", k=4)
        s3 = ar.take(2 * S).rearrange("p (k t) -> p k t", k=2)
        pr = ar.take(2 * S).rearrange("p (k t) -> p k t", k=2)
        yacc = ar.take(NTOK)
        assert ar.at <= VA
        wtop = sb("wtop", [P, NT])
        ar.at = later
        qaug = ar.take(2 * 8 * S, BF16).rearrange("p (k a t) -> p k a t", k=2, a=8)
        kaug = arena[:, KAUG:ARENA].bitcast(BF16).rearrange("p (k a t) -> p k a t", k=2, a=NH)
        va = arena[:, VA:KAUG].rearrange("p (k t h d) -> p k t h d", k=2, t=TPB, h=NH)
        used = Area(packed["moe0"], offsets(PACKS["moe0"])[1])
        ropet = used.take(4 * S).rearrange("p (k t) -> p k t", k=4)
        qk = used.take(2 * S).rearrange("p (k t) -> p k t", k=2)
        junk = used.take(2 * S, BF16).rearrange("p (k t) -> p k t", k=2)
        pc = ar.take(6 * S, BF16).rearrange("p (a i t) -> p a i t", a=2, i=3)
        pt = ar.take(3 * 2 * S).rearrange("p (k a t) -> p k a t", k=3, a=2)
        mx = ar.take(2 * 16).rearrange("p (k q j) -> p k q j", k=2, q=4)
        mres = ar.take(16).rearrange("p (q j) -> p q j", q=4)
        mpc = ar.take(2 * 48, BF16).rearrange("p (k q j i) -> p k q j i", k=2, q=4, j=4)
        mT = ar.take(2 * S, BF16).rearrange("p (k t) -> p k t", k=2)
        used = Area(packed["mod"], offsets(PACKS["mod"])[1])
        ot = used.take(S)
        rden = ar.take(16).rearrange("p (q j) -> p q j", q=4)
        at = ar.take(TPB * D).rearrange("p (q h d) -> p q h d", q=TPB, h=NH)
        aT = used.take(S)
        ao = used.take(S)
        assert ar.at <= VA
        ar.at = later
        ar.take(12 * NT * 8)
        xb = ar.take(NBLK * ROW).rearrange("p (j d) -> p j d", d=ROW)
        xT = ar.take(2 * P).rearrange("p (k s) -> p k s", k=2)
        gs = ar.take(2 * HID).rearrange("p (k h) -> p k h", k=2)
        w1 = ar.take(2 * HID).rearrange("p (k h) -> p k h", k=2)
        ys = ar.take(NBLK * D).rearrange("p (j d) -> p j d", d=D)
        yt = ar.take(NT * D).rearrange("p (t d) -> p t d", d=D)
        gw = ar.take(NT * D).rearrange("p (t d) -> p t d", d=D)
        dp = ar.take(6 * NT * E1).rearrange("p (i e t) -> p i e t", i=6, e=E1)
        nblk = ar.take(4 * E1).rearrange("p (i e) -> p i e", i=4)
        blk = ar.take(NBLK * E1).rearrange("p (j e) -> p j e", e=E1)
        blk1 = ar.take(NBLK).rearrange("p (j e) -> p j e", e=1)
        expert_at = sb("expert_at", [P, NBLK], mybir.dt.int32)
        pos = ar.take(NT).rearrange("p (t e) -> p t e", e=1)
        posu = sb("posu", [P, NT], mybir.dt.uint32)
        spare = ar.take(NBLK)
        token_at = sb("token_at", [P, NBLK], mybir.dt.uint32)
        slots_x = nc.dram_tensor("slots_x", (NBLK * P, ROW), F32, kind="Internal").ap()
        tokens_y = nc.dram_tensor("tokens_y", (1 + NTOK + NBLK * P, D), F32, kind="Internal").ap()
        qkd = nc.dram_tensor("qk_parts", (B, 2, NH // 2, 2, PIECES, DK, S), BF16, kind="Internal").ap()

        block = ctx.enter_context(nc.Block())

        BLOCK_GROUPS = [slice(j, min(j + 6, NBLK)) for j in range(0, NBLK, 6)]

        RING = 3
        FIRST_PASS = [
            [(3, [0])],
            [(3, [1])],
            [(2, [0]), (0, [0, 1, 2, 3])],
            [(2, [1])],
            [(1, [0, 1]), (2, [2])],
            [(2, [3])],
            [(3, [2]), (1, [2, 3])],
            [(3, [3])],
        ]
        ring = []

        units, at_slot, maxima_done = [], [], [0]
        for slot in FIRST_PASS:
            at_slot.append(range(len(units), len(units) + len(slot)))
            for qt, js in slot:
                units.append((qt, js))
                maxima_done.append(maxima_done[-1] + len(js))

        def ring_projection(b, j):
            ring.append(((("rope", b, j), ("rope", 4 * b + j + 1)) if j < 4 else (("va", b), ("va", b + 1))))

        for b in (0, 1):
            for j in range(5):
                ring_projection(b, j)
        for it in range(-2, 17):
            for i in range(8):
                if it + 2 < 16:
                    for n in at_slot[i]:
                        ring.append((("mx", it + 2, n), ("mx", 16 * (it + 2) + maxima_done[n + 1])))
                if i == 2 and 0 <= it + 1 < 16:
                    ring.append((("mT", it + 1), ("mT", it + 2)))
                if i == 3 and 0 <= it - 1:
                    ring.append((("oT", it - 1), ("at", it)))
                if i == 5 and it >= 4 and it % 4 == 0:
                    ring.append((("aT", it // 4 - 1), ("aT", it // 4)))
                if i == 7 and it >= 4 and it % 4 == 0:
                    ring.append((("ao", it // 4 - 1), ("ao", it // 4)))
                if it in (2, 6) and i % 2 == 0:
                    ring_projection((it + 6) // 4, i // 2)
                if it in (4, 8) and i == 6:
                    ring_projection((it + 4) // 4, 4)
        ring_at = {item: n for n, (item, _) in enumerate(ring)}

        def ring_read(engine, *item):
            engine.wait_ge(sem("ring_ps"), ring_at[item] + 1)
            return ring_at[item] % RING

        @block.sync
        def _(sp):
            sp.dma_start(x[:, :, :], x_in).then_inc(sem("ld_x"), 16)
            sp.dma_start(packed["mod"][:, :], mod_in).then_inc(sem("ld_mod"), 16)
            sp.dma_start(packed["const"][:, :], const_in).then_inc(sem("ld_const"), 16)
            sp.dma_start(packed["mixw"][:, :], mixw_in).then_inc(sem("ld_mixw"), 16)
            sp.dma_start(bconst[:, :], bconst_in).then_inc(sem("ld_bconst"), 16)
            sp.dma_start(packed["moe0"][:, :], moe0_in).then_inc(sem("ld_moe0"), 16)
            sp.dma_start(packed["attn"][:, :], attn_in).then_inc(sem("ld_attn"), 16)
            sp.wait_ge(sem("pool_const"), 3)
            sp.dma_start(slots_x.rearrange("(j p) d -> p j d", p=P), zeros[:, :].unsqueeze(1)
                         .to_broadcast([P, NBLK, ROW])).then_inc(sem("slots_clear"), 16)
            sp.wait_ge(sem("x1"), NT)
            sp.dma_start(packed["moe1"][:, :], moe1_in).then_inc(sem("ld_moe1"), 16)
            sp.wait_ge(sem("kaug_clear"), 1)
            for k in range(2):
                sp.dma_start(kaug[KR:KM, k, :, :], kones_in).then_inc(sem("k_ones"), 16)

            def parts_out(b, i):
                for a in range(2):
                    sp.wait_ge(sem(("part_hi", "part_mid", "parts")[i]), 2 * b + a + 1)
                    for c in range(PIECES):
                        if ((0, 0, 0, 1, 1, 2), (0, 1, 2, 0, 1, 0))[a][c] == i:
                            sp.dma_start(qkd[b, a, :, :, c].rearrange("r h d t -> (r h) d t"), pc[:, a, i, :])\
                                .then_inc(sem(f"parts_out{a}"), 16)

            def relayout(b):
                if b >= 2:
                    sp.wait_ge(sem("pv"), 8 * 4 * (b - 1))
                for name, r in (("aug_first", slice(0, 2)), ("aug", slice(2, 8))):
                    for a in range(2):
                        if r.start == 0:
                            sp.wait_ge(sem(f"parts_out{a}"), 16 * PIECES * (b + 1))
                        if a == 0:
                            sp.dma_start(qaug[0:KR, b % 2, r, :], qkd[b, a, r].rearrange("r h c d t -> (h c d) r t"))\
                                .then_inc(sem(f"{name}{b % 2}"), 16)
                        else:
                            for hh in range(2):
                                sp.dma_start(kaug[hh * KR // 2:(hh + 1) * KR // 2, b % 2, hh + 2 * r.start:2 * r.stop:2, :],
                                             qkd[b, a, r, hh].rearrange("r c d t -> (c d) r t"))\
                                    .then_inc(sem(f"{name}{b % 2}"), 16)

            for b in range(2):
                for i in range(3):
                    parts_out(b, i)
                relayout(b)
            for s in range(NT):
                sp.wait_ge(sem("mT"), s + 1)
                b, g = divmod(s, QG)
                if g == 0 and b >= 2:
                    sp.wait_ge(sem("pv"), 32 * (b - 1))
                for i in range(2):
                    sp.dma_start(qaug[KR:KM, b % 2, 2 * g + i, :], mT[6 * i:6 * i + 6, s % 2, :])\
                        .then_inc(sem(f"m_rows{s % 2}"), 16)
                if s in (4, 8):
                    for i in range(3):
                        parts_out(s // 4 + 1, i)
                    relayout(s // 4 + 1)
            sp.wait_ge(sem("scattered"), 16 * NT)
            slots = slots_x.rearrange("(j p) d -> p j d", p=P)
            for c, js in enumerate(BLOCK_GROUPS):
                sp.dma_start(xb[:, js, :], slots[:, js, :]).then_inc(sem(f"ld_moe1_{c}"), 16)
            sp.wait_ge(sem("returned"), 16 * NBLK)
            for b in range(B):
                sp.dma_start(yt[:, TPB * b:TPB * (b + 1), :], tokens_y[1 + b * S:1 + (b + 1) * S, :]
                             .rearrange("(t p) d -> p t d", p=P)).then_inc(sem(f"ld_moe1_{b}"), 16)
            for b in (1, 0, 2, 3):
                if b == 0:
                    sp.wait_ge(sem("x4_0"), 1)
                else:
                    sp.wait_ge(sem("x4"), b)
                ts = slice(TPB * b, TPB * (b + 1))
                sp.dma_start(out[:, ts, :], x[:, ts, :]).then_inc(sem("stored"), 16)
            sp.wait_ge(sem("stored"), 16 * B)

        def ln_stats(v, k, src, b):
            for t in range(TPB * b, TPB * (b + 1)):
                v.bn_stats(st[:, k, t, :], src[:, t, :]).then_inc(sem("ln_stats"), 1)

        def ln_moments(v, k, b):
            v.wait_ge(sem("ln_stats"), NT * k + TPB * (b + 1))
            for t in range(TPB * b, TPB * (b + 1)):
                v.bn_aggr(mv[:, k, t, :], st[:, k, t, :]).then_inc(sem("ln_moments"), 1)

        def ln_rstd(pool, k, b):
            ts = slice(TPB * b, TPB * (b + 1))
            pool.wait_ge(sem("ln_moments"), NT * k + TPB * (b + 1))
            if k == 0:
                pool.tensor_scalar(nmean[:, ts], mv[:, k, ts, 0], -1.0, None, ALU.mult)
            pool.tensor_scalar(rs[:, k, ts], mv[:, k, ts, 1], EPS, None, ALU.add).then_inc(sem("ln_var"), 1)
            pool.wait_ge(sem("ln_var"), B * k + b + 1)
            pool.tensor_tensor(rs[:, k, ts], rs[:, k, ts], neghalf[:, ts], ALU.pow).then_inc(sem("ln_rstd"), 1)

        def ln_apply(v, k, src, dst, b):
            v.wait_ge(sem("ln_rstd"), B * k + b + 1)
            for t in range(TPB * b, TPB * (b + 1)):
                v.tensor_scalar(dst[:, t, :], src[:, t, :], mv[:, k, t, 0:1], rs[:, k, t:t + 1],
                                ALU.subtract, ALU.mult).then_inc(sem("ln_out"), 1)

        def combine(engine, b, weighted, done, n):
            ts = slice(TPB * b, TPB * (b + 1))
            engine.wait_ge(sem(f"ld_moe1_{b}"), 32)
            engine.tensor_tensor(yt[:, ts, :], yt[:, ts, :], gw[:, ts, :], ALU.mult).then_inc(sem(weighted), 1)
            engine.wait_ge(sem(weighted), n)
            engine.tensor_tensor(x[:, ts, :], x[:, ts, :], yt[:, ts, :], ALU.add).then_inc(sem(done), 1)

        @block.gpsimd
        def _(pool):
            pool.memset(neghalf[:, :], -0.5).then_inc(sem("pool_const"), 1)
            pool.memset(ones[:, :], 1.0).then_inc(sem("pool_const"), 1)
            pool.memset(zeros[:, :], 0.0).then_inc(sem("pool_const"), 1)
            pool.wait_ge(sem("pool_const"), 2)
            for b in range(B):
                ln_rstd(pool, 0, b)
            for b in range(B):
                ln_rstd(pool, 1, b)
            pool.wait_ge(sem("ld_const"), 16)
            pool.wait_ge(sem("ld_mixw"), 16)
            pool.wait_ge(sem("decay_in"), 1)

            for i in range(NT + 3):
                if i < NT:
                    t, k = i, i % 2
                    if t >= 2:
                        pool.wait_ge(sem("y_ps"), t - 1)
                        pool.wait_ge(sem("y_gated"), t - 1)
                    x3 = xs[:, t, :].rearrange("p (h e) -> p h e", h=HEADS)
                    pool.wait_ge(sem("xs_tok"), 3 * (t // TPB + 1))
                    pool.tensor_tensor(X[:, k], x3, dtv[:, 7, t, :].unsqueeze(2).to_broadcast([P, HEADS, HP]),
                                       ALU.mult).then_inc(sem("X"), 1)
                    pool.tensor_tensor(Dx[:, k], x3, w["D"].unsqueeze(2).to_broadcast([P, HEADS, HP]),
                                       ALU.mult).then_inc(sem("Dx"), 1)
                    if t >= 2 and (t - 2) % TPB < 3:
                        pool.wait_ge(sem("state_ps"), ((t - 2) // TPB) * 3 + (t - 2) % TPB + 1)
                    pool.wait_ge(sem("L"), t + 1)
                    pool.wait_ge(sem("X"), t + 1)
                    pool.tensor_tensor(Xd[:, k], X[:, k], L[:, k, :, P - 1:P].to_broadcast([P, HEADS, HP]),
                                       ALU.mult).then_inc(sem("Xd"), 1)
                if 0 <= i - 2 < NT:
                    t = i - 2
                    pool.wait_ge(sem("ssq"), t + 1)
                    pool.tensor_scalar(rr[:, t:t + 1], ssq[:, t:t + 1], 1.0 / DI, EPS, ALU.mult,
                                       ALU.add).then_inc(sem("msq"), 1)
                    pool.wait_ge(sem("msq"), t + 1)
                    pool.tensor_tensor(rr[:, t:t + 1], rr[:, t:t + 1], neghalf[:, 0:1], ALU.pow)\
                        .then_inc(sem("rms"), 1)
                if 0 <= i - 3:
                    t = i - 3
                    pool.wait_ge(sem("o_gated"), t + 1)
                    pool.tensor_tensor(x[:, t, :], x[:, t, :], o[:, t % 2, :], ALU.add).then_inc(sem("x1"), 1)
                if i >= 9 and i % TPB == 1:
                    ln_rstd(pool, 2, i // TPB - 2)

            ln_rstd(pool, 2, B - 1)
            pool.memset(wp[:, :, :], 0.0).then_inc(sem("wp_clear"), 1)
            pool.memset(kaug[:, :, :, :], 0.0).then_inc(sem("kaug_clear"), 1)
            pool.memset(va[:, :, :, :, :], 0.0).then_inc(sem("va_clear"), 1)
            pool.wait_ge(sem("va_clear"), 1)
            pool.memset(va[:, :, :, :, DK:DK + 1], 1.0).then_inc(sem("va_clear"), 1)
            for i in range(32):
                n, e = divmod(i, E0)
                ts = slice(n * S, (n + 1) * S)
                pool.wait_ge(sem("pr"), i + 1)
                if i == 0 or i == E0:
                    pool.wait_ge(sem("z_sb"), n + 1)
                elif e > 0:
                    pool.wait_ge(sem("yacc"), i)
                if e == 0 and n >= 2:
                    pool.tensor_copy(yacc[:, ts], pr[:, i % 2, :]).then_inc(sem("yacc"), 1)
                else:
                    pool.tensor_tensor(yacc[:, ts], yacc[:, ts], pr[:, i % 2, :], ALU.add).then_inc(sem("yacc"), 1)

            def rotate(i):
                a = i % 2
                pool.wait_ge(sem("rope"), 2 * (i + 1))
                if i >= 2:
                    pool.wait_ge(sem("parts"), i - 1)
                pool.tensor_tensor(qk[:, a, :], ropet[:, 2 * a, :], ropet[:, 2 * a + 1, :], ALU.add)\
                    .then_inc(sem("qk"), 1)

            def rest(i):
                a = i % 2
                pool.wait_ge(sem("part_hi"), i + 1)
                pool.tensor_tensor(qk[:, a, :], qk[:, a, :], pc[:, a, 0, :], ALU.subtract).then_inc(sem("res"), 1)

            def last_part(i):
                a = i % 2
                pool.wait_ge(sem("part_mid"), i + 1)
                pool.tensor_tensor(pc[:, a, 2, :], qk[:, a, :], pc[:, a, 1, :], ALU.subtract).then_inc(sem("parts"), 1)

            ln_rstd(pool, 3, 0)
            ln_rstd(pool, 3, 1)
            rotate(0)
            rotate(1)
            rest(0)
            rest(1)
            last_part(0)
            last_part(1)
            ln_rstd(pool, 3, 2)
            ln_rstd(pool, 3, 3)
            for b in range(1, B):
                if b == 3:
                    ln_rstd(pool, 4, 0)
                for stage in (rotate, rest, last_part):
                    stage(2 * b)
                    stage(2 * b + 1)
            for b in range(1, B):
                ln_rstd(pool, 4, b)
            pool.wait_ge(sem("posu"), 1)
            pool.wait_ge(sem("numbers"), 2)
            pool.wait_ge(sem("h4"), B)
            pool.wait_ge(sem("slots_clear"), 16)
            for t in range(NT):
                pool.indirect_dma_start(out=slots_x[:, :], out_offset=bass.IndirectOffsetOnAxis(
                    ap=posu[:, t:t + 1], axis=0), in_=rows[:, t, :], in_offset=None).then_inc(sem("scattered"), 16)
            for j in range(NBLK):
                pool.wait_ge(sem("pr"), DENSE + j + 1)
                pool.wait_ge(sem("token_at"), j // 6 + 1)
                pool.indirect_dma_start(out=tokens_y[:, :], out_offset=bass.IndirectOffsetOnAxis(
                    ap=token_at[:, j:j + 1], axis=0), in_=ys[:, j, :], in_offset=None)\
                    .then_inc(sem("returned"), 16)
            pool.wait_ge(sem("gate_weights"), NT)
            combine(pool, 0, "y_weighted0", "x4_0", 1)

        @block.scalar
        def _(act):
            act.wait_ge(sem("ld_mod"), 16)
            act.activation(siluc[:, :], w["cT"], ACT.Silu).then_inc(sem("siluc"), 1)
            for b in range(2, B):
                act.wait_ge(sem("ln_rstd"), b + 1)
                for t in range(TPB * b, TPB * (b + 1)):
                    act.activation(h[:, t, :], x[:, t, :], ACT.Identity, bias=nmean[:, t:t + 1])\
                        .then_inc(sem("h_centered"), 1)
                for t in range(TPB * b, TPB * (b + 1)):
                    act.wait_ge(sem("h_centered"), t - 2 * TPB + 1)
                    act.activation(h[:, t, :], h[:, t, :], ACT.Identity, scale=rs[:, 0, t:t + 1])\
                        .then_inc(sem("h_normed"), 1)
            for b in range(B):
                act.wait_ge(sem("mod0_ps"), b + 1)
                act.activation(mod0[:, b, :], ps[:, 1 + b, 0:384], ACT.Identity).then_inc(sem("mod0"), 1)
            for b in range(B):
                act.wait_ge(sem("mod1_ps"), b + 1)
                act.activation(mod1[:, b, :], ps[:, MOD1_BANK[b], :], ACT.Identity).then_inc(sem("mod0"), 1)
            act.wait_ge(sem("ld_mixw"), 16)

            def mixer_in(b):
                act.wait_ge(sem("xnT_ps"), b + 1)
                act.activation(hT[:, b * S:(b + 1) * S], ps[:, 6 + b % 2, :], ACT.Identity,
                               scale=w["norm_w"], bias=w["norm_b"]).then_inc(sem("hT"), 1)

            mixer_in(0)
            mixer_in(1)

            def to_tokens(b):
                for c in range(3):
                    m = 3 * b + c
                    act.wait_ge(sem("xs_ps"), m + 1)
                    src = ps[:, 6 + m % 2, :].rearrange("p (t d) -> p t d", t=TPB)
                    ts = slice(TPB * b, TPB * (b + 1))
                    dst = xs[:, ts, c * P:(c + 1) * P] if c < 2 else Bt[:, ts, :]
                    act.activation(dst, src, ACT.Identity).then_inc(sem("xs_tok"), 1)

            def last_tap(b, c):
                act.wait_ge(sem("xbc_ps"), 4 * b + c + 1)
                if b >= 2:
                    act.wait_ge(sem("xbc_silu"), 4 * (b - 2) + c + 1)
                act.activation(acc[b % 2][:, c, :], ps[:, c, :], ACT.Identity,
                               scale=w["conv_w"][:, 4 * c + 3:4 * c + 4], bias=w["conv_b"][:, c:c + 1])\
                    .then_inc(sem("conv_last_tap"), 1)

            def silu(b, c):
                act.wait_ge(sem("conv"), 4 * b + c + 1)
                act.activation(xcT[:, c, b * S:(b + 1) * S], acc[b % 2][:, c, :], ACT.Silu).then_inc(sem("xbc_silu"), 1)

            for b in range(B + 1):
                for c0 in (0, 2):
                    for c in (c0, c0 + 1):
                        if b < B:
                            last_tap(b, c)
                    if b == 0 and c0 == 0:
                        mixer_in(2)
                        mixer_in(3)
                    for c in (c0, c0 + 1):
                        if b >= 1:
                            silu(b - 1, c)
                    if b == 2 and c0 == 0:
                        act.wait_ge(sem("dt_nabs"), 1)
                        act.activation(dtv[:, 2, :, :], dtv[:, 1, :, :], ACT.Exp).then_inc(sem("dt_exp"), 1)
                        act.activation(eA[:, :], w["A_log"], ACT.Exp).then_inc(sem("dt_exp"), 1)
                if b >= 1:
                    for i in range(2):
                        act.wait_ge(sem("z_ps"), 2 * (b - 1) + i + 1)
                        t = TPB * (b - 1) + 2 * i
                        act.activation(sz[:, t:t + 2, :], ps[:, 4 + i, :].rearrange("p (a d) -> p a d", a=2),
                                       ACT.Silu).then_inc(sem("sz"), 1)
                if 2 <= b < B:
                    to_tokens(b - 2)
            act.wait_ge(sem("decay_in"), 1)
            act.wait_ge(sem("xbc_silu"), 16)

            def decays(t):
                k = t % 2
                if t >= 2:
                    act.wait_ge(sem("seg_ps"), t - 1)
                for hh in range(HEADS):
                    act.activation(ua[:, k, hh, :], w["tri"], ACT.Identity, scale=av[:, t, hh:hh + 1])\
                        .then_inc(sem("ua"), 1)

            decays(0)
            act.wait_ge(sem("acum_ps"), 1)
            act.activation(eact[:, :, :, :].rearrange("p a t h -> p (a t h)"), ps[:, 3, 0:2 * NT * HEADS],
                           ACT.Exp).then_inc(sem("eact"), 1)
            for i in range(NT + 2):
                if i < NT:
                    t, k = i, i % 2
                    if t + 1 < NT:
                        decays(t + 1)
                    act.wait_ge(sem("seg_ps"), t + 1)
                    if t >= 2:
                        act.wait_ge(sem("M"), t - 1)
                        act.wait_ge(sem("Xd"), t - 1)
                    act.activation(L[:, k].rearrange("p h s -> p (h s)"), ps[:, k, :], ACT.Exp).then_inc(sem("L"), 1)
                if i < 2:
                    to_tokens(B - 2 + i)
                if 0 <= i - 2:
                    t, k = i - 2, i % 2
                    act.wait_ge(sem("yT_ps"), t + 1)
                    if t >= 2:
                        act.wait_ge(sem("o_ps"), t - 1)
                    act.activation(yT[:, k].rearrange("p a s -> p (a s)"), ps[:, 6, k * 256:(k + 1) * 256],
                                   ACT.Identity).then_inc(sem("yT"), 1)
                    if t >= 1:
                        act.wait_ge(sem("ssq"), t)
                    act.activation(ysq[:, :], y[:, k, :], ACT.Square, accum_out=ssq[:, t:t + 1])\
                        .then_inc(sem("ssq"), 1)

            def hT_evac(k, layer, scale, bias, bank=6, sequences=range(B)):
                for b in sequences:
                    act.wait_ge(sem("xnT_ps"), B * (k - 1) + b + 1)
                    act.activation(hT[:, b * S:(b + 1) * S], ps[:, bank + b % 2, :], ACT.Identity,
                                   scale=modT[:, scale, layer, b:b + 1], bias=modT[:, bias, layer, b:b + 1])\
                        .then_inc(sem("hT"), 1)

            hT_evac(2, 0, 4, 3)
            act.wait_ge(sem("gate_shifted"), 1)
            act.activation(rt[:, 1], rt[:, 0], ACT.Exp).then_inc(sem("gate_exp"), 1)

            def shared_silu(j):
                act.wait_ge(sem("sa_ps"), j + 1)
                if j >= 2:
                    act.wait_ge(sem("sg"), j - 1)
                if j in (4, 5):
                    act.wait_ge(sem("p2_ps"), DENSE - 5 + j)
                act.activation(gT[:, j % 2, :], ps[:, 2 + j % 2, :], ACT.Silu).then_inc(sem("sh"), 1)

            for j in range(4):
                shared_silu(j)
            for n in range(2):
                act.wait_ge(sem("z_acc"), 2 * (n + 1))
                act.activation(yacc[:, n * S:(n + 1) * S], ps[:, Z_BANK[n], :], ACT.Identity).then_inc(sem("z_sb"), 1)
            for i in range(32):
                n, e = divmod(i, E0)
                act.wait_ge(sem("p1_ps"), i + 1)
                if i >= 2:
                    act.wait_ge(sem("p2_ps"), i - 1)
                elif i == 0:
                    act.wait_ge(sem("sg"), 4)
                act.activation(gT[:, i % 2, :], ps[:, 2 + i % 2, :], ACT.Silu, bias=w["b1"][:, e:e + 1])\
                    .then_inc(sem("h1"), 1)
                act.wait_ge(sem("p3_ps"), i + 1)
                if i >= 2:
                    act.wait_ge(sem("pr"), i - 1)
                act.activation(s3[:, i % 2, :], ps[:, 4 + i % 2, :], ACT.Identity, bias=w["b3"][:, e:e + 1])\
                    .then_inc(sem("s3"), 1)
            for j in range(4, 8):
                shared_silu(j)


            def part_hi(b, a):
                act.wait_ge(sem("qk"), 2 * b + a + 1)
                if b >= 1:
                    act.wait_ge(sem(f"parts_out{a}"), 16 * PIECES * b)
                act.activation(pc[:, a, 0, :], qk[:, a, :], ACT.Identity).then_inc(sem("part_hi"), 1)

            def part_mid(b, a):
                act.wait_ge(sem("res"), 2 * b + a + 1)
                act.activation(pc[:, a, 1, :], qk[:, a, :], ACT.Identity).then_inc(sem("part_mid"), 1)

            def probs(u):
                kt = 3 - (u % 8) // 2
                n = S - kt * P
                k = u % 2
                act.wait_ge(sem("st_ps"), u + 1)
                if u >= 3:
                    act.wait_ge(sem("pv"), u - 2)
                act.activation(pt[:, u % 3, :, 0:n], ps[:, 4 + 2 * k:6 + 2 * k, 0:n], ACT.Exp,
                               scale=ATT_SCALE).then_inc(sem("probs"), 1)

            hT_evac(3, 1, 1, 0, bank=4, sequences=range(0, 1))
            part_hi(0, 0)
            part_hi(0, 1)
            part_mid(0, 0)
            part_mid(0, 1)
            hT_evac(3, 1, 1, 0, bank=4, sequences=range(1, 2))
            for a in range(2):
                part_hi(1, a)
            for a in range(2):
                part_mid(1, a)
            hT_evac(3, 1, 1, 0, bank=4, sequences=range(2, B))
            for it in range(-2, 17):
                for i in range(8):
                    if 0 <= it < 16:
                        probs(8 * it + i)
                    if i == 1 and it >= 1:
                        s = it - 1
                        act.wait_ge(sem("pv"), 8 * (s + 1))
                        if s >= 1:
                            act.wait_ge(sem("at"), s)
                        act.activation(ot[:, :], ps[:, 3, :], ACT.Identity).then_inc(sem("ot"), 1)
                    if i == 2 and 0 <= it + 1 < 16:
                        s = it + 1
                        k = ring_read(act, "mT", s)
                        if s >= 2:
                            act.wait_ge(sem(f"m_rows{s % 2}"), 32 * (s // 2))
                        act.activation(mT[0:12, s % 2, :], ps[0:12, k, 0:256].bitcast(BF16), ACT.Identity)\
                            .then_inc(sem("mT"), 1)
                    if i == 5 and it >= 4 and it % 4 == 0:
                        k = ring_read(act, "aT", it // 4 - 1)
                        act.activation(aT[:, :], ps[:, k, :], ACT.Identity).then_inc(sem("aT"), 1)
                    if it in (3, 7) and i in (1, 2):
                        part_hi((it + 5) // 4, i - 1)
                    if it in (3, 7) and i in (4, 5):
                        part_mid((it + 5) // 4, i - 4)
            for b in range(B):
                act.wait_ge(sem("xnT_ps"), B * 3 + b + 1)
                act.activation(hT[:, b * S:(b + 1) * S], ps[:, 6 + b % 2, :], ACT.Identity).then_inc(sem("hT"), 1)
            act.wait_ge(sem("top_diff"), 1)
            act.activation(rt[:, 10, :, 0], rt[:, 9, :, 0], ACT.Exp).then_inc(sem("top_exp"), 1)
            for j in range(NBLK):
                act.wait_ge(sem("p1_ps"), DENSE + j + 1)
                if j >= 2:
                    act.wait_ge(sem("p2_ps"), DENSE + j - 1)
                act.activation(gs[:, j % 2, :], ps[:, j % 2, :], ACT.Gelu).then_inc(sem("h1"), 1)

        @block.vector
        def _(v):
            v.wait_ge(sem("ld_x"), 16)
            for b in range(B + 1):
                if b < B:
                    ln_stats(v, 0, x, b)
                if b >= 1:
                    ln_moments(v, 0, b - 1)
            ln_apply(v, 0, x, h, 0)
            ln_apply(v, 0, x, h, 1)
            v.wait_ge(sem("modT_ps"), 1)
            n = [0]

            def step(ins):
                n[0] += 1
                ins.then_inc(sem("mod_step"), 1)
                v.wait_ge(sem("mod_step"), n[0])

            step(v.tensor_copy(modT[:, :, :, :].rearrange("p c l b -> p (c l b)"), ps[:, 0, 0:48]))
            g = modT[:, 2:6:3].rearrange("p i l b -> p i (l b)")
            step(v.tensor_scalar(guard_tmp[:, 0], g, 0.0, -0.5, ALU.is_ge, ALU.add))
            step(v.scalar_tensor_tensor(out=guard_tmp[:, 1], in0=g, scalar=-1.0, in1=g, op0=ALU.mult, op1=ALU.max))
            step(v.scalar_tensor_tensor(out=g, in0=guard_tmp[:, 1], scalar=0.25, in1=guard_tmp[:, 0], op0=ALU.max,
                                        op1=ALU.mult))
            v.tensor_scalar(g, g, 2.0, None, ALU.mult).then_inc(sem("modT"), 1)
            v.tensor_scalar(modT[:, 1:5:3], modT[:, 1:5:3], 1.0, None, ALU.add).then_inc(sem("modT"), 1)
            for i in range(B + 4):
                if i < B:
                    b, ts = i, slice(TPB * i, TPB * (i + 1))
                    if b < 2:
                        v.wait_ge(sem("ln_out"), TPB * (b + 1))
                    else:
                        v.wait_ge(sem("h_normed"), TPB * (b - 1))
                    v.wait_ge(sem("mod0"), b + 1)
                    v.tensor_tensor(h[:, ts, :], h[:, ts, :], mod0[:, b, D:2 * D].unsqueeze(1)
                                    .to_broadcast([P, TPB, D]), ALU.mult).then_inc(sem("h_scaled"), 1)
                if 0 <= i - 1 < B:
                    b, ts = i - 1, slice(TPB * (i - 1), TPB * i)
                    v.wait_ge(sem("h_scaled"), b + 1)
                    v.tensor_tensor(h[:, ts, :], h[:, ts, :], mod0[:, b, 0:D].unsqueeze(1)
                                    .to_broadcast([P, TPB, D]), ALU.add).then_inc(sem("h"), 1)
                if 0 <= i - 2 < B:
                    v.wait_ge(sem("h"), i - 1)
                    ln_stats(v, 1, h, i - 2)
                if 0 <= i - 3 < B:
                    ln_moments(v, 1, i - 3)
                if 0 <= i - 4:
                    ln_apply(v, 1, h, xn, i - 4)

            v.wait_ge(sem("ld_const"), 16)
            v.tensor_copy(rows[:, :, D], w["number"]).then_inc(sem("numbers"), 1)
            v.tensor_copy(rows[:, :, D + 1:ROW], zeros[:, 0:1].unsqueeze(1).to_broadcast([P, NT, ROW - D - 1]))\
                .then_inc(sem("numbers"), 1)

            d = [dtv[:, i, :, :] for i in range(8)]

            def softplus():
                m = 0
                v.wait_ge(sem("dt_ps"), 1)
                v.tensor_tensor(d[0], ps[:, 7, 0:NT * HEADS].rearrange("p (t h) -> p t h", t=NT),
                                w["dt_bias"].unsqueeze(1).to_broadcast([P, NT, HEADS]), ALU.add)\
                    .then_inc(sem("dt_step"), 1)
                yield
                v.wait_ge(sem("dt_step"), 1)
                v.scalar_tensor_tensor(out=d[1], in0=d[0], scalar=-1.0, in1=d[0], op0=ALU.mult,
                                       op1=ALU.min).then_inc(sem("dt_nabs"), 1)
                yield
                for _ in range(6):
                    yield
                v.wait_ge(sem("dt_exp"), 1)
                chain = [lambda: v.tensor_scalar(d[3], d[2], 2.0, None, ALU.add),
                         lambda: v.reciprocal(d[4], d[3]),
                         lambda: v.tensor_tensor(d[3], d[2], d[4], ALU.mult),
                         lambda: v.tensor_tensor(d[4], d[3], d[3], ALU.mult),
                         lambda: v.tensor_scalar(d[5], d[4], 1.0 / 15.0, None, ALU.mult)]
                for k in (13, 11, 9, 7, 5, 3):
                    chain.append(lambda k=k: v.scalar_tensor_tensor(out=d[5], in0=d[5], scalar=1.0 / k, in1=d[4],
                                                                    op0=ALU.add, op1=ALU.mult))
                chain += [lambda: v.scalar_tensor_tensor(out=d[6], in0=d[5], scalar=1.0, in1=d[3], op0=ALU.add,
                                                         op1=ALU.mult),
                          lambda: v.tensor_scalar(d[5], d[0], 0.0, None, ALU.max),
                          lambda: v.scalar_tensor_tensor(out=d[7], in0=d[6], scalar=2.0, in1=d[5], op0=ALU.mult,
                                                         op1=ALU.add)]
                for m, ins in enumerate(chain):
                    v.wait_ge(sem("dt_step"), m + 1)
                    ins().then_inc(sem("dt_step"), 1)
                    yield
                v.wait_ge(sem("dt_step"), len(chain) + 1)
                v.wait_ge(sem("dt_exp"), 2)
                v.scalar_tensor_tensor(out=av[:, :, :], in0=d[7], scalar=-1.0,
                                       in1=eA[:, :].unsqueeze(1).to_broadcast([P, NT, HEADS]),
                                       op0=ALU.mult, op1=ALU.mult).then_inc(sem("decay_in"), 1)
                yield

            steps = softplus()
            v.wait_ge(sem("ld_mixw"), 16)
            for b in range(B):
                for c0 in (0, 2):
                    for s in range(1, TAPS):
                        for c in (c0, c0 + 1):
                            if s == 1:
                                v.wait_ge(sem("conv_last_tap"), 4 * b + c + 1)
                            else:
                                v.wait_ge(sem("conv_tap"), 4 * (2 * b + c0 // 2) + 2 * (s - 2) + c - c0 + 1)
                            v.scalar_tensor_tensor(out=acc[b % 2][:, c, s:S], in0=ps[:, c, 0:S - s],
                                                   scalar=w["conv_w"][:, 4 * c + 3 - s:4 * c + 4 - s],
                                                   in1=acc[b % 2][:, c, s:S], op0=ALU.mult, op1=ALU.add)\
                                .then_inc(sem("conv_tap" if s < TAPS - 1 else "conv"), 1)
                            if b >= 2:
                                next(steps, None)
            for _ in steps:
                pass
            for i in range(2):
                v.tensor_scalar(wor[:, i, :], w["out_proj"][:, i * D:(i + 1) * D], w["rms_w"][:, i:i + 1], None,
                                ALU.mult).then_inc(sem("wor"), 1)

            def bc(a):
                return a.unsqueeze(2).to_broadcast([P, HEADS, HP])

            v.wait_ge(sem("eact"), 1)
            for i in range(NT + 3):
                if i < NT:
                    t, k = i, i % 2
                    v.wait_ge(sem("g_ps"), t + 1)
                    v.tensor_tensor(Gm[:, k, :], ps[:, 2, k * P:(k + 1) * P], w["tri"], ALU.mult).then_inc(sem("Gm"), 1)
                if 0 <= i - 1 < NT and (i - 1) % TPB < TPB - 1:
                    t, k = i - 1, (i - 1) % 2
                    c, b = t % TPB, t // TPB
                    stp = ps[:, 5, k * DI:(k + 1) * DI].rearrange("p (h e) -> p h e", h=HEADS)
                    if c == 0:
                        v.wait_ge(sem("state_ps"), 3 * b + c + 1)
                        if b >= 1:
                            v.wait_ge(sem("y_ps"), t)
                        v.tensor_copy(prev[:, k], stp).then_inc(sem("prev"), 1)
                    else:
                        v.wait_ge(sem("y_ps"), t)
                        v.tensor_tensor(prev[:, k], prev[:, 1 - k], bc(eact[:, 1, t, :]), ALU.mult)\
                            .then_inc(sem("prev_decayed"), 1)
                if i < NT:
                    t, k = i, i % 2
                    v.wait_ge(sem("Gm"), t + 1)
                    v.wait_ge(sem("L"), t + 1)
                    if t >= 2:
                        v.wait_ge(sem("y_ps"), t - 1)
                    v.tensor_tensor(M[:, k], L[:, k], Gm[:, k, :].unsqueeze(1).to_broadcast([P, HEADS, P]),
                                    ALU.mult).then_inc(sem("M"), 1)
                if 0 <= i - 1 < NT and 0 < (i - 1) % TPB < TPB - 1:
                    t, k = i - 1, (i - 1) % 2
                    c, b = t % TPB, t // TPB
                    stp = ps[:, 5, k * DI:(k + 1) * DI].rearrange("p (h e) -> p h e", h=HEADS)
                    v.wait_ge(sem("state_ps"), 3 * b + c + 1)
                    v.wait_ge(sem("prev_decayed"), 2 * b + c)
                    v.tensor_tensor(prev[:, k], prev[:, k], stp, ALU.add).then_inc(sem("prev"), 1)
                t, k = i - 1, (i - 1) % 2
                c, b = t % TPB, t // TPB
                u, l = i - 3, (i - 3) % 2
                y3 = y[:, k, :].rearrange("p (h e) -> p h e", h=HEADS)
                if 0 <= t < NT:
                    yd = ps[:, 3 + k, 0:DI].rearrange("p (h e) -> p h e", h=HEADS)
                    yo = ps[:, 3 + k, DI:2 * DI].rearrange("p (h e) -> p h e", h=HEADS)
                    v.wait_ge(sem("y_ps"), t + 1)
                    v.wait_ge(sem("Dx"), t + 1)
                    if t >= 2:
                        v.wait_ge(sem("yT_ps"), t - 1)
                        v.wait_ge(sem("ssq"), t - 1)
                    v.tensor_tensor(y3, yd, Dx[:, k], ALU.add).then_inc(sem("y_a"), 1)
                    if c > 0:
                        v.tensor_tensor(Yo[:, :, :], yo, bc(eact[:, 0, t, :]), ALU.mult).then_inc(sem("y_b"), 1)
                if u >= 0:
                    v.wait_ge(sem("o_ps"), u + 1)
                    v.wait_ge(sem("rms"), u + 1)
                    if u >= 2:
                        v.wait_ge(sem("x1"), u - 1)
                    v.scalar_tensor_tensor(out=o[:, l, :], in0=ps[:, 7, P * (1 + l):P * (2 + l)],
                                           scalar=rr[:, u:u + 1], in1=h[:, u, :], op0=ALU.mult,
                                           op1=ALU.add).then_inc(sem("o_sum"), 1)
                if 0 <= t < NT:
                    v.wait_ge(sem("y_a"), t + 1)
                    if c > 0:
                        v.wait_ge(sem("y_b"), 2 * (3 * b + c - 1) + 1)
                        v.tensor_tensor(y3, y3, Yo[:, :, :], ALU.add).then_inc(sem("y_b"), 1)
                if u >= 0:
                    v.wait_ge(sem("o_sum"), u + 1)
                    v.tensor_tensor(o[:, l, :], o[:, l, :], mod0[:, u // TPB, 2 * D:3 * D], ALU.mult)\
                        .then_inc(sem("o_gated"), 1)
                if 0 <= t < NT:
                    if c > 0:
                        v.wait_ge(sem("y_b"), 2 * (3 * b + c - 1) + 2)
                    v.wait_ge(sem("sz"), 2 * (b + 1))
                    v.tensor_tensor(y[:, k, :], y[:, k, :], sz[:, t, :], ALU.mult).then_inc(sem("y_gated"), 1)
                if i >= 8:
                    b = i // TPB - 2
                    if i % TPB == 0:
                        v.wait_ge(sem("x1"), TPB * (b + 1))
                        ln_stats(v, 2, x, b)
                    elif i % TPB == 1:
                        ln_moments(v, 2, b)
                    elif i % TPB == 2:
                        ln_apply(v, 2, x, xn, b)

            v.wait_ge(sem("x1"), NT)
            ln_stats(v, 2, x, B - 1)
            ln_moments(v, 2, B - 1)
            ln_apply(v, 2, x, xn, B - 1)
            q = [rt[:, i] for i in range(12)]
            one = [rt[:, i, :, 0:1] for i in range(12)]
            nr = [0]

            def shared_product(j, bank):
                v.wait_ge(sem("sh"), j + 1)
                v.wait_ge(sem("sb_ps"), j + 1)
                if j >= 2:
                    v.wait_ge(sem("z_acc"), j - 1)
                v.tensor_tensor(xm[:, j % 2, :], ps[:, bank + j % 2, :], gT[:, j % 2, :], ALU.mult)\
                    .then_inc(sem("sg"), 1)

            between_steps = dict(zip(SHARED_AT, range(4)))

            def rstep(ins):
                nr[0] += 1
                ins.then_inc(sem("route"), 1)
                if nr[0] in between_steps:
                    shared_product(between_steps[nr[0]], bank=0)
                v.wait_ge(sem("route"), nr[0])

            def bc8(a):
                return a.to_broadcast([P, NT, 8])

            iota = w["iota"].unsqueeze(1).to_broadcast([P, NT, 8])

            def first_of_largest(src, top, hot, tmp, tmp1):
                rstep(v.tensor_reduce(top, src, AX_X, ALU.max))
                rstep(v.tensor_tensor(tmp, src, bc8(top), ALU.is_ge))
                rstep(v.tensor_tensor(tmp, tmp, iota, ALU.mult))
                rstep(v.tensor_reduce(tmp1, tmp, AX_X, ALU.max))
                rstep(v.tensor_tensor(hot, tmp, bc8(tmp1), ALU.is_equal))

            logits = ps[:, 5, 0:NT * 8].rearrange("p (t e) -> p t e", e=8)
            v.wait_ge(sem("gate_ps"), 1)
            rstep(v.tensor_reduce(one[2], logits, AX_X, ALU.max))
            v.tensor_tensor(q[0], logits, bc8(one[2]), ALU.subtract).then_inc(sem("gate_shifted"), 1)
            v.wait_ge(sem("gate_exp"), 1)
            rstep(v.tensor_reduce(one[2], q[1], AX_X, ALU.add))
            rstep(v.reciprocal(one[3], one[2]))
            rstep(v.tensor_tensor(q[4], q[1], bc8(one[3]), ALU.mult))
            first_of_largest(q[4], one[2], q[5], q[7], one[3])
            rstep(v.scalar_tensor_tensor(out=q[6], in0=q[5], scalar=-2.0, in1=q[4], op0=ALU.mult, op1=ALU.add))
            first_of_largest(q[6], one[2], q[8], q[7], one[3])
            rstep(v.tensor_tensor(q[5], q[5], q[8], ALU.add))
            rstep(v.scalar_tensor_tensor(out=q[6], in0=q[4], scalar=CHOSEN, in1=q[5], op0=ALU.max, op1=ALU.mult))
            v.wait_ge(sem("wp_clear"), 1)
            rstep(v.tensor_copy(wp[:, :, 0:8], q[6]))
            rstep(v.tensor_tensor(q[7], q[6], wp[:, :, 0:8], ALU.subtract))
            rstep(v.tensor_copy(wp[:, :, 8:16], q[7]))
            rstep(v.tensor_tensor(wp[:, :, 16:24], q[7], wp[:, :, 8:16], ALU.subtract))

            def wT_evac(name):
                for b in range(B):
                    v.wait_ge(sem(f"{name}_ps"), b + 1)
                    v.tensor_copy(wT[:, b * S:(b + 1) * S], ps[:, 6 + b % 2, 0:256].bitcast(BF16))\
                        .then_inc(sem(name), 1)

            wT_evac("wT0")

            def weigh(i):
                n = i // E0
                v.wait_ge(sem("wbc_ps"), i + 1)
                if i >= 2:
                    v.wait_ge(sem("p3_ps"), i - 1)
                elif i == 0:
                    v.wait_ge(sem("z_acc"), 4)
                v.tensor_tensor(xm[:, i % 2, :], hT[:, n * S:(n + 1) * S], ps[:, i % 2, :], ALU.mult)\
                    .then_inc(sem("xm"), 1)

            def mask(i):
                v.wait_ge(sem("s3"), i + 1)
                v.scalar_tensor_tensor(out=s3[:, i % 2, :], in0=ps[:, i % 2, :], scalar=0.0, in1=s3[:, i % 2, :],
                                       op0=ALU.is_gt, op1=ALU.mult).then_inc(sem("s3_masked"), 1)

            def product(i):
                e = i % E0
                v.wait_ge(sem("p2_ps"), i + 1)
                v.wait_ge(sem("s3_masked"), i + 1)
                if i >= 2:
                    v.wait_ge(sem("yacc"), i - 1)
                v.scalar_tensor_tensor(out=pr[:, i % 2, :], in0=ps[:, 6 + i % 2, :], scalar=w["b2"][:, e:e + 1],
                                       in1=s3[:, i % 2, :], op0=ALU.add, op1=ALU.mult).then_inc(sem("pr"), 1)

            weigh(0)
            for i in range(33):
                if i + 1 < 32:
                    weigh(i + 1)
                if i < 32:
                    mask(i)
                if i >= 1:
                    product(i - 1)
            v.wait_ge(sem("p3_ps"), 32)
            def rope(b, j):
                k = ring_read(v, "rope", b, j)
                if b >= 1:
                    v.wait_ge(sem("qk"), 2 * (b - 1) + j // 2 + 1)
                v.tensor_tensor(ropet[:, j, :], ps[:, k, :], w[("cos", "sin")[j % 2]], ALU.mult)\
                    .then_inc(sem("rope"), 1)

            def gated(n):
                ts = slice(n * S, (n + 1) * S)
                v.wait_ge(sem("yacc"), 8 * (n + 1))
                if n >= 2:
                    v.wait_ge(sem("z_acc"), 2 * (n + 1))
                    v.tensor_tensor(yacc[:, ts], yacc[:, ts], ps[:, Z_BANK[n], :], ALU.add).then_inc(sem("y0_sum"), 1)
                    v.wait_ge(sem("y0_sum"), n - 1)
                v.tensor_scalar(yacc[:, ts], yacc[:, ts], modT[:, 5, 0, n:n + 1], None, ALU.mult)\
                    .then_inc(sem("y0"), 1)

            def residual(n):
                tt = slice(TPB * n, TPB * (n + 1))
                v.wait_ge(sem("y0T_ps"), n + 1)
                v.tensor_tensor(x[:, tt, :], x[:, tt, :], ps[:, Y0T_BANK[n], :].rearrange("p (t d) -> p t d", t=TPB),
                                ALU.add).then_inc(sem("x2"), 1)
                v.wait_ge(sem("x2"), n + 1)
                ln_stats(v, 3, x, n)
                ln_moments(v, 3, n)

            gated(0)
            shared_product(4, bank=4)
            gated(1)
            shared_product(5, bank=4)
            residual(0)
            shared_product(6, bank=4)
            residual(1)
            shared_product(7, bank=4)
            ln_apply(v, 3, x, xn, 0)
            for i in range(4):
                rope(0, i)
            gated(2)
            gated(3)
            residual(2)
            residual(3)
            ln_apply(v, 3, x, xn, 1)

            def router_input(b, step):
                ts = slice(TPB * b, TPB * (b + 1))
                if step == 0:
                    v.wait_ge(sem("x3"), b + 1)
                    ln_stats(v, 4, x, b)
                elif step == 1:
                    ln_moments(v, 4, b)
                elif step == 2:
                    ln_apply(v, 4, x, xn, b)
                elif step == 3:
                    v.wait_ge(sem("ln_out"), NT * 3 + TPB * (b + 3))
                    v.tensor_tensor(xn[:, ts, :], xn[:, ts, :],
                                    mod1[:, b, 2 * D:3 * D].unsqueeze(1).to_broadcast([P, TPB, D]), ALU.mult)\
                        .then_inc(sem("h4_scaled"), 1)
                else:
                    v.wait_ge(sem("h4_scaled"), b + 1)
                    v.tensor_tensor(xn[:, ts, :], xn[:, ts, :],
                                    mod1[:, b, D:2 * D].unsqueeze(1).to_broadcast([P, TPB, D]), ALU.add)\
                        .then_inc(sem("h4"), 1)

            def values(b):
                k = ring_read(v, "va", b)
                v.wait_ge(sem("va_clear"), 2)
                if b >= 2:
                    v.wait_ge(sem("pv"), 32 * (b - 1))
                v.tensor_copy(va[:, b % 2, :, :, 0:DK], ps[:, k, :].rearrange("p (t h d) -> p t h d", t=TPB, h=NH))\
                    .then_inc(sem("va"), 1)

            def maximum(s, u):
                qt, js = units[u]
                n = P * (qt + 1)
                k = ring_read(v, "mx", s, u)
                if u == 0 and s >= 2:
                    v.wait_ge(sem("m_parts"), 4 * (s - 1))
                for c, j in enumerate(js):
                    done = 16 * s + maxima_done[u] + c
                    if done >= 2:
                        v.wait_ge(sem("mx"), done - 1)
                    v.tensor_tensor_reduce(out=junk[:, done % 2, 0:n], in0=ps[:, k, c * n:(c + 1) * n],
                                           in1=w["mask"][:, (3 - qt) * P:4 * P], scale=1.0, scalar=3 * NEG,
                                           op0=ALU.add, op1=ALU.max, accum_out=mx[:, s % 2, qt, j:j + 1])\
                        .then_inc(sem("mx"), 1)

            def max_parts(s, step):
                k = s % 2
                if step == 0:
                    v.wait_ge(sem("mx"), 16 * (s + 1))
                else:
                    v.wait_ge(sem("m_parts"), 4 * s + step)
                if step == 0:
                    ins = v.tensor_scalar(mpc[:, k, :, :, 0], mx[:, k], -1.0, None, ALU.mult)
                elif step == 1:
                    ins = v.scalar_tensor_tensor(out=mres[:, :, :], in0=mx[:, k], scalar=-1.0, in1=mpc[:, k, :, :, 0],
                                                 op0=ALU.mult, op1=ALU.subtract)
                elif step == 2:
                    ins = v.tensor_copy(mpc[:, k, :, :, 1], mres[:, :, :])
                else:
                    ins = v.tensor_tensor(mpc[:, k, :, :, 2], mres[:, :, :], mpc[:, k, :, :, 1], ALU.subtract)
                ins.then_inc(sem("m_parts"), 1)

            def o_norm(s):
                b, g = divmod(s, QG)
                k = ring_read(v, "oT", s)
                o4 = ps[:, k, :].rearrange("p (q j d) -> p q j d", q=4, j=4)
                if s >= 1:
                    v.wait_ge(sem("at"), s)
                v.reciprocal(rden[:, :, :], o4[:, :, :, DK]).then_inc(sem("rden"), 1)
                v.wait_ge(sem("rden"), s + 1)
                if g == 0 and b >= 1:
                    v.wait_ge(sem("aT"), b)
                v.tensor_tensor(at[:, :, 4 * g:4 * g + 4, :], o4[:, :, :, 0:DK],
                                rden[:, :, :].unsqueeze(3).to_broadcast([P, 4, 4, DK]), ALU.mult).then_inc(sem("at"), 1)

            def attn_out(b):
                k = ring_read(v, "ao", b)
                tt = slice(TPB * b, TPB * (b + 1))
                v.tensor_tensor(ao[:, :].rearrange("p (t d) -> p t d", t=TPB),
                                ps[:, k, :].rearrange("p (t d) -> p t d", t=TPB),
                                mod1[:, b, 0:D].unsqueeze(1).to_broadcast([P, TPB, D]), ALU.mult).then_inc(sem("ao"), 1)
                v.wait_ge(sem("ao"), b + 1)
                v.tensor_tensor(x[:, tt, :], x[:, tt, :], ao[:, :].rearrange("p (t d) -> p t d", t=TPB), ALU.add)\
                    .then_inc(sem("x3"), 1)

            for b in range(2):
                for j in range(4):
                    if b > 0:
                        rope(b, j)
                values(b)
            ln_apply(v, 3, x, xn, 2)
            ln_apply(v, 3, x, xn, 3)
            for it in range(-2, 17):
                for i in range(8):
                    if i < 2 and 0 <= it + 1 < 16:
                        max_parts(it + 1, 2 * i)
                    if it + 2 < 16:
                        for u in at_slot[i]:
                            maximum(it + 2, u)
                    if i < 2 and 0 <= it + 1 < 16:
                        max_parts(it + 1, 2 * i + 1)
                    if i == 3 and 0 <= it - 1:
                        o_norm(it - 1)
                    if i == 7 and it >= 4 and it % 4 == 0:
                        attn_out(it // 4 - 1)
                    if it in (2, 6) and i % 2 == 0:
                        rope((it + 6) // 4, i // 2)
                    if it in (4, 8) and i == 6:
                        values((it + 4) // 4)
                    if it >= 5 and it % 4 == 1 and 2 <= i < 7:
                        router_input(it // 4 - 1, i - 2)

            for step in range(5):
                router_input(B - 1, step)
            v.wait_ge(sem("gate1_ps"), 1)
            q[4] = logits
            first_of_largest(q[4], one[2], q[5], q[7], one[3])
            v.wait_ge(sem("rank_ps"), 1)
            d = [dp[:, i] for i in range(6)]
            flat = [dp[:, i].rearrange("p e t -> p (e t)") for i in range(6)]
            rank = ps[:, 7, 0:NT * E1].rearrange("p (e t) -> p e t", e=E1)
            rstep(v.tensor_copy(flat[0], ps[:, 7, NT * E1:2 * NT * E1]))
            rstep(v.tensor_tensor_scan(flat[1], w["segment"], flat[0], 0.0, ALU.mult, ALU.add))
            rstep(v.tensor_tensor(d[2], d[1][:, :, NT - 1:NT].to_broadcast([P, E1, NT]),
                                  w["full"].unsqueeze(1).to_broadcast([P, E1, NT]), ALU.is_gt))
            rstep(v.tensor_reduce(nblk[:, 0, :].unsqueeze(2), d[2], AX_X, ALU.add))
            rstep(v.tensor_tensor_scan(nblk[:, 1, :], ones[:, 0:E1], nblk[:, 0, :], 0.0, ALU.mult, ALU.add))
            rstep(v.tensor_tensor(nblk[:, 2, :], nblk[:, 1, :], nblk[:, 0, :], ALU.subtract))
            rstep(v.tensor_tensor(d[3], d[1], d[0], ALU.subtract))
            rstep(v.scalar_tensor_tensor(out=d[4], in0=nblk[:, 2, :].unsqueeze(2).to_broadcast([P, E1, NT]),
                                         scalar=float(P), in1=d[3], op0=ALU.mult, op1=ALU.add))
            rstep(v.tensor_tensor(d[4], d[4], rank, ALU.add))
            rstep(v.tensor_tensor(d[5], d[4], q[5].rearrange("p t e -> p e t"), ALU.mult))
            rstep(v.tensor_reduce(pos, d[5].rearrange("p e t -> p t e"), AX_X, ALU.add))
            v.tensor_scalar(posu[:, :], pos[:, :, 0], -1.0, None, ALU.add).then_inc(sem("posu"), 1)
            rstep(v.tensor_tensor(blk[:, :, :], nblk[:, 1, :].unsqueeze(1).to_broadcast([P, NBLK, E1]),
                                  w["block"].unsqueeze(2).to_broadcast([P, NBLK, E1]), ALU.is_le))
            rstep(v.tensor_reduce(blk1, blk[:, :, :], AX_X, ALU.add))
            v.tensor_scalar(expert_at[:, :], blk1[:, :, 0], float(E1 - 1), float(HID), ALU.min, ALU.mult)\
                .then_inc(sem("expert_at"), 1)
            rstep(v.scalar_tensor_tensor(out=q[6], in0=q[5], scalar=NEG, in1=q[4], op0=ALU.mult, op1=ALU.add))
            rstep(v.tensor_reduce(one[8], q[6], AX_X, ALU.max))
            v.tensor_tensor(rt[:, 9, :, 0], rt[:, 8, :, 0], rt[:, 2, :, 0], ALU.subtract).then_inc(sem("top_diff"), 1)
            v.wait_ge(sem("top_exp"), 1)
            rstep(v.tensor_scalar(rt[:, 11, :, 0], rt[:, 10, :, 0], 1.0, None, ALU.add))
            v.reciprocal(wtop[:, :], rt[:, 11, :, 0]).then_inc(sem("wtop"), 1)

            v.wait_ge(sem("expert_at"), 1)
            for i in range(-1, NBLK + 1):
                for c, js in enumerate(BLOCK_GROUPS):
                    if i == js.start:
                        v.wait_ge(sem(f"ld_moe1_{c}"), 16)
                        v.scalar_tensor_tensor(out=spare[:, js], in0=xb[:, js, D], scalar=0.0, in1=w["spare"][:, js],
                                               op0=ALU.is_equal, op1=ALU.mult).then_inc(sem("spare"), 1)
                        v.wait_ge(sem("spare"), c + 1)
                        v.tensor_tensor(token_at[:, js], spare[:, js], xb[:, js, D], ALU.add)\
                            .then_inc(sem("token_at"), 1)
                if 0 <= i + 1 < NBLK:
                    j = i + 1
                    if j >= 2:
                        v.wait_ge(sem("p1_ps"), DENSE + j - 1)
                    at_w = v.value_load(expert_at[0:1, j:j + 1], min_val=0, max_val=(E1 - 1) * HID)
                    v.tensor_copy(w1[:, j % 2, :], w["W1"][:, bass.ds(at_w, HID)]).then_inc(sem("w1"), 1)
                    v.wait_ge(sem("xT_ps"), j + 1)
                    v.tensor_copy(xT[:, j % 2, :], ps[:, 2 + j % 2, 0:P]).then_inc(sem("xT"), 1)
                if 0 <= i - 1 < NBLK:
                    j = i - 1
                    v.wait_ge(sem("p2_ps"), DENSE + j + 1)
                    v.tensor_copy(ys[:, j, :], ps[:, 6 + j % 2, 0:D]).then_inc(sem("pr"), 1)
                if 0 <= i < NT:
                    v.wait_ge(sem("wtop"), 1)
                    v.tensor_scalar(gw[:, i, :], mod1[:, i // TPB, 3 * D:4 * D], wtop[:, i:i + 1], None, ALU.mult)\
                        .then_inc(sem("gate_weights"), 1)
            v.wait_ge(sem("gate_weights"), NT)
            for b in range(1, B):
                combine(v, b, "y_weighted", "x4", b)

        @block.tensor
        def _(pe):
            pe.wait_ge(sem("siluc"), 1)
            for c in range(6):
                for layer in range(2):
                    mm = pe.matmul(ps[:, 0, (2 * c + layer) * B:(2 * c + layer + 1) * B],
                                   w[f"wmod{layer}"][:, c * D:(c + 1) * D], siluc[:, layer * B:(layer + 1) * B],
                                   start=True, stop=True)
            mm.then_inc(sem("modT_ps"), 1)
            pe.wait_ge(sem("ld_const"), 16)
            pe.wait_ge(sem("modT"), 2)
            for b in range(B):
                for n, c in enumerate((0, 1, 2)):
                    mm = pe.matmul(ps[:, 1 + b, n * D:(n + 1) * D], modT[:, c, 0, b:b + 1].to_broadcast([P, P]), ident,
                                   start=True, stop=True)
                mm.then_inc(sem("mod0_ps"), 1)
            for b in range(B):
                if b == 3:
                    pe.wait_ge(sem("mod0"), 1)
                for n, c in enumerate((2, 3, 4, 5)):
                    mm = pe.matmul(ps[:, MOD1_BANK[b], n * D:(n + 1) * D], modT[:, c, 1, b:b + 1].to_broadcast([P, P]),
                                   ident, start=True, stop=True)
                mm.then_inc(sem("mod1_ps"), 1)

            def transposes(k, b, bank=6):
                pe.wait_ge(sem("ln_out"), NT * (k - 1) + TPB * (b + 3))
                if b >= 2:
                    pe.wait_ge(sem("hT"), B * (k - 1) + b - 1)
                for i in range(TPB):
                    mm = pe.transpose(ps[:, bank + b % 2, i * P:(i + 1) * P], xn[:, TPB * b + i, :], ident)
                mm.then_inc(sem("xnT_ps"), 1)

            pe.wait_ge(sem("mod0"), 2 * B)
            transposes(1, 0)
            transposes(1, 1)

            def to_tokens(b):
                for c in range(3):
                    m = 3 * b + c
                    pe.wait_ge(sem("xbc_silu"), 4 * b + c + 1)
                    if m >= 2:
                        pe.wait_ge(sem("xs_tok"), m - 1)
                    elif m == 1:
                        pe.wait_ge(sem("dt_step"), 1)
                    for i in range(TPB):
                        mm = pe.transpose(ps[:, 6 + m % 2, i * P:(i + 1) * P],
                                          xcT[:, c, b * S + i * P:b * S + (i + 1) * P], ident)
                    mm.then_inc(sem("xs_ps"), 1)

            def channels(b, c):
                pe.wait_ge(sem("hT"), b + 1)
                if b >= 1:
                    pe.wait_ge(sem("conv"), 4 * (b - 1) + c + 1)
                pe.matmul(ps[:, c, :], w["in_proj"][:, DI + c * P:DI + (c + 1) * P], hT[:, b * S:(b + 1) * S],
                          start=True, stop=True).then_inc(sem("xbc_ps"), 1)

            for b in range(B + 1):
                if b < B:
                    channels(b, 0)
                    channels(b, 1)
                if b == 0:
                    transposes(1, 2)
                    transposes(1, 3)
                if b >= 1:
                    for i in range(2):
                        if b >= 2:
                            pe.wait_ge(sem("sz"), 2 * (b - 2) + i + 1)
                        for j in range(2):
                            t = TPB * (b - 1) + 2 * i + j
                            mm = pe.matmul(ps[:, 4 + i, j * DI:(j + 1) * DI], hT[:, t * P:(t + 1) * P],
                                           w["in_proj"][:, 0:DI], start=True, stop=True)
                        mm.then_inc(sem("z_ps"), 1)
                if b < B:
                    channels(b, 2)
                    channels(b, 3)
                if b == 1:
                    pe.wait_ge(sem("hT"), B)
                    for t in range(NT):
                        mm = pe.matmul(ps[:, 7, t * HEADS:(t + 1) * HEADS], hT[:, t * P:(t + 1) * P],
                                       w["in_proj"][:, 768:772], start=True, stop=True)
                    mm.then_inc(sem("dt_ps"), 1)
                if 2 <= b < B:
                    to_tokens(b - 2)
            pe.wait_ge(sem("decay_in"), 1)
            pe.wait_ge(sem("pool_const"), 2)
            pe.wait_ge(sem("conv"), 16)
            a2 = av[:, :, :].rearrange("p t h -> p (t h)")
            pe.matmul(ps[:, 3, 0:64], w["tri"], a2, start=True, stop=True)
            pe.matmul(ps[:, 3, 64:128], ones[:, :], a2, start=True, stop=True).then_inc(sem("acum_ps"), 1)

            for i in range(NT + 3):
                if i < NT:
                    t, k = i, i % 2
                    tok = slice(t * P, (t + 1) * P)
                    pe.wait_ge(sem("ua"), HEADS * (t + 1))
                    if t >= 2:
                        pe.wait_ge(sem("L"), t - 1)
                    pe.matmul(ps[:, k, :], w["after"], ua[:, k].rearrange("p h s -> p (h s)"), start=True,
                              stop=True).then_inc(sem("seg_ps"), 1)
                    if t >= 1:
                        pe.wait_ge(sem("Gm"), t)
                    pe.wait_ge(sem("xbc_silu"), 4 * (t // TPB + 1))
                    pe.matmul(ps[:, 2, k * P:(k + 1) * P], xcT[:, 2, tok], xcT[:, 3, tok], start=True,
                              stop=True).then_inc(sem("g_ps"), 1)
                if i < 2:
                    to_tokens(B - 2 + i)
                if 0 <= i - 2 < NT:
                    t, k = i - 2, i % 2
                    pe.wait_ge(sem("y_gated"), t + 1)
                    if t == 0:
                        pe.wait_ge(sem("xs_tok"), 12)
                    if t >= 1:
                        pe.wait_ge(sem("yT"), t)
                    for q in range(2):
                        mm = pe.transpose(ps[:, 6, k * 256 + q * P:k * 256 + (q + 1) * P], y[:, k, q * P:(q + 1) * P],
                                          ident)
                    mm.then_inc(sem("yT_ps"), 1)
                if 0 <= i - 1 < NT:
                    t, k = i - 1, (i - 1) % 2
                    c, b = t % TPB, t // TPB
                    tok = slice(t * P, (t + 1) * P)
                    if c < TPB - 1:
                        pe.wait_ge(sem("Xd"), t + 1)
                        if t >= 1:
                            pe.wait_ge(sem("prev"), 3 * b + c)
                        pe.matmul(ps[:, 5, k * DI:(k + 1) * DI], Bt[:, t, :], Xd[:, k].rearrange("p h e -> p (h e)"),
                                  start=True, stop=True).then_inc(sem("state_ps"), 1)
                    pe.wait_ge(sem("M"), t + 1)
                    pe.wait_ge(sem("X"), t + 1)
                    if t == 0:
                        pe.wait_ge(sem("eact"), 1)
                        pe.wait_ge(sem("sz"), 8)
                    if t >= 2:
                        pe.wait_ge(sem("y_gated"), t - 1)
                    if c > 0:
                        pe.wait_ge(sem("prev"), 3 * b + c)
                        pe.matmul(ps[:, 3 + k, DI:2 * DI], xcT[:, 3, tok],
                                  prev[:, 1 - k].rearrange("p h e -> p (h e)"), start=True, stop=True)
                    for hh in range(HEADS):
                        mm = pe.matmul(ps[:, 3 + k, hh * HP:(hh + 1) * HP], M[:, k, hh, :], X[:, k, hh, :],
                                       start=True, stop=True)
                    mm.then_inc(sem("y_ps"), 1)
                if 0 <= i - 3:
                    t, k = i - 3, (i - 3) % 2
                    pe.wait_ge(sem("yT"), t + 1)
                    if t >= 1:
                        pe.wait_ge(sem("o_sum"), t)
                    else:
                        pe.wait_ge(sem("wor"), 2)
                        pe.wait_ge(sem("eact"), 1)
                    for q in range(2):
                        mm = pe.matmul(ps[:, 7, P * (1 + k):P * (2 + k)], yT[:, k, q, :], wor[:, q, :],
                                       start=(q == 0), stop=(q == 1))
                    mm.then_inc(sem("o_ps"), 1)

            def router(k, weights, name):
                for b in range(B + 1):
                    if b < B:
                        if k == 4:
                            pe.wait_ge(sem("h4"), b + 1)
                        transposes(k, b)
                    if b >= 1:
                        pe.wait_ge(sem("hT"), B * (k - 1) + b)
                        for t in range(TPB * (b - 1), TPB * b):
                            mm = pe.matmul(ps[:, 5, 8 * t:8 * t + 8], hT[:, t * P:(t + 1) * P], weights, start=True,
                                           stop=True)
                mm.then_inc(sem(name), 1)

            def shared_in(j, bank):
                n, i = divmod(j, 2)
                ts = slice(n * S, (n + 1) * S)
                pe.wait_ge(sem("hT"), B + n + 1)
                if j >= 2:
                    pe.wait_ge(sem("sh"), j - 1)
                    pe.wait_ge(sem("sg"), j - 1)
                pe.matmul(ps[:, 2 + j % 2, :], w["sw1"][:, i * P:(i + 1) * P], hT[:, ts], start=True,
                          stop=True).then_inc(sem("sa_ps"), 1)
                pe.matmul(ps[:, bank + j % 2, :], w["sw2"][:, i * P:(i + 1) * P], hT[:, ts], start=True,
                          stop=True).then_inc(sem("sb_ps"), 1)

            def shared_out(j):
                n, i = divmod(j, 2)
                pe.wait_ge(sem("sg"), j + 1)
                if j == 4:
                    pe.wait_ge(sem("pr"), DENSE)
                pe.matmul(ps[:, Z_BANK[n], :], w["sw3"][:, i * D:(i + 1) * D],
                          xm[:, j % 2, :], start=(i == 0), stop=(i == 1)).then_inc(sem("z_acc"), 1)

            def weights_T(ready, name):
                pe.wait_ge(sem("route"), ready)
                for b in range(B):
                    if b >= 2:
                        pe.wait_ge(sem(name), b - 1)
                    for i in range(TPB):
                        mm = pe.transpose(ps[:, 6 + b % 2, i * 64:(i + 1) * 64].bitcast(BF16), wp[:, TPB * b + i, :],
                                          identb)
                    mm.then_inc(sem(f"{name}_ps"), 1)

            pe.wait_ge(sem("yT"), NT)
            pe.wait_ge(sem("o_sum"), NT)
            pe.wait_ge(sem("prev"), 12)
            pe.wait_ge(sem("ld_moe0"), 16)
            router(2, w["gate"], "gate_ps")
            pe.wait_ge(sem("ld_bconst"), 16)
            pe.wait_ge(sem("gate_shifted"), 1)
            shared_in(0, bank=0)
            shared_in(1, bank=0)
            shared_out(0)
            shared_in(2, bank=0)
            shared_out(1)
            shared_in(3, bank=0)
            shared_out(2)
            shared_out(3)
            weights_T(ROUTE0, "wT0")

            def spread(i):
                n, e = divmod(i, E0)
                pe.wait_ge(sem("wT0"), n + 1)
                if i >= 2:
                    pe.wait_ge(sem("s3_masked"), i - 1)
                    pe.wait_ge(sem("xm"), i - 1)
                pe.matmul(ps[:, i % 2, :], w["sel0"][0:96, e * P:(e + 1) * P], wT[0:96, n * S:(n + 1) * S],
                          start=True, stop=True).then_inc(sem("wbc_ps"), 1)

            def expert_out(i):
                e = i % E0
                pe.wait_ge(sem("h1"), i + 1)
                if i >= 2:
                    pe.wait_ge(sem("pr"), i - 1)
                elif i == 0:
                    pe.wait_ge(sem("wT0"), B)
                pe.matmul(ps[:, 6 + i % 2, :], w["w2"][:, e * D:(e + 1) * D], gT[:, i % 2, :], start=True,
                          stop=True).then_inc(sem("p2_ps"), 1)

            spread(0)
            pe.wait_ge(sem("sh"), 4)
            pe.wait_ge(sem("z_sb"), 2)
            for i in range(32):
                e = i % E0
                pe.wait_ge(sem("xm"), i + 1)
                if i >= 2:
                    pe.wait_ge(sem("h1"), i - 1)
                    pe.wait_ge(sem("s3"), i - 1)
                pe.matmul(ps[:, 2 + i % 2, :], w["w1"][:, e * D:(e + 1) * D], xm[:, i % 2, :], start=True,
                          stop=True).then_inc(sem("p1_ps"), 1)
                if i + 1 < 32:
                    spread(i + 1)
                pe.matmul(ps[:, 4 + i % 2, :], w["w3"][:, e * D:(e + 1) * D], xm[:, i % 2, :], start=True,
                          stop=True).then_inc(sem("p3_ps"), 1)
                if i >= 1:
                    expert_out(i - 1)
            expert_out(31)
            pe.wait_ge(sem("h1"), 32)
            pe.wait_ge(sem("s3"), 32)
            pe.wait_ge(sem("s3_masked"), 32)

            def ring_bank(*item):
                n = ring_at[item]
                if n >= RING:
                    reader, count = ring[n - RING][1]
                    pe.wait_ge(sem(reader), count)
                return n % RING

            def project(b, j):
                k = ring_bank("rope", b, j)
                pe.wait_ge(sem("hT"), 2 * B + b + 1)
                pe.matmul(ps[:, k, :], w[("wq", "wqs", "wk", "wks")[j]], hT[:, b * S:(b + 1) * S], start=True,
                          stop=True).then_inc(sem("ring_ps"), 1)

            def y0_T(n):
                pe.wait_ge(sem("y0"), n + 1)
                for i in range(TPB):
                    mm = pe.transpose(ps[:, Y0T_BANK[n], i * P:(i + 1) * P],
                                      yacc[:, n * S + i * P:n * S + (i + 1) * P], ident)
                mm.then_inc(sem("y0T_ps"), 1)

            shared_in(4, bank=4)
            y0_T(0)
            shared_in(5, bank=4)
            shared_out(4)
            y0_T(1)
            shared_in(6, bank=4)
            shared_out(5)
            shared_in(7, bank=4)
            shared_out(6)
            shared_out(7)
            transposes(3, 0, bank=4)
            pe.wait_ge(sem("ld_attn"), 16)
            for i in range(4):
                project(0, i)
            y0_T(2)
            y0_T(3)
            transposes(3, 1, bank=4)

            def project_values(b):
                k = ring_bank("va", b)
                for i in range(TPB):
                    t = TPB * b + i
                    mm = pe.matmul(ps[:, k, i * P:(i + 1) * P], hT[:, t * P:(t + 1) * P], w["wv"], start=True,
                                   stop=True)
                mm.then_inc(sem("ring_ps"), 1)

            def scores(s, i):
                b, g = divmod(s, QG)
                qt, js = units[i]
                n = P * (qt + 1)
                if g == 0 and i == 0:
                    pe.wait_ge(sem(f"aug_first{b % 2}"), 16 * 3 * (b // 2 + 1))
                    pe.wait_ge(sem("k_ones"), 32)
                elif g == 1 and i == 0:
                    pe.wait_ge(sem(f"aug{b % 2}"), 16 * 3 * (b // 2 + 1))
                k = ring_bank("mx", s, i)
                for c, j in enumerate(js):
                    mm = pe.matmul(ps[:, k, c * n:(c + 1) * n], qaug[0:KR, b % 2, 2 * g + j // 2, qt * P:(qt + 1) * P],
                                   kaug[0:KR, b % 2, 4 * g + j, 0:n], start=True, stop=True)
                mm.then_inc(sem("ring_ps"), 1)

            def maxima_T(s):
                pe.wait_ge(sem("m_parts"), 4 * (s + 1))
                k = ring_bank("mT", s)
                for qt in range(4):
                    mm = pe.transpose(ps[0:12, k, 64 * qt:64 * (qt + 1)].bitcast(BF16),
                                      mpc[:, s % 2, qt].rearrange("p j i -> p (j i)"), identb)
                mm.then_inc(sem("ring_ps"), 1)

            def scores_T(u):
                s, i = divmod(u, 8)
                b, g = divmod(s, QG)
                kt, jp = 3 - i // 2, i % 2
                n = S - kt * P
                if i == 0:
                    pe.wait_ge(sem(f"m_rows{s % 2}"), 32 * (s // 2 + 1))
                if u >= 2:
                    pe.wait_ge(sem("probs"), u - 1)
                for hh in range(2):
                    bank = 4 + 2 * (u % 2) + hh
                    pe.matmul(ps[:, bank, 0:P], identb, w["causal"], start=True, stop=True)
                    mm = pe.matmul(ps[:, bank, 0:n], kaug[0:KM, b % 2, 4 * g + 2 * jp + hh, kt * P:(kt + 1) * P],
                                   qaug[0:KM, b % 2, 2 * g + jp, kt * P:S], start=False, stop=True,
                                   skip_group_check=True)
                mm.then_inc(sem("st_ps"), 1)

            def weighted_values(u):
                s, i = divmod(u, 8)
                b, g = divmod(s, QG)
                kt, jp = 3 - i // 2, i % 2
                n = S - kt * P
                if i == 0 and s >= 1:
                    pe.wait_ge(sem("ot"), s)
                pe.wait_ge(sem("probs"), u + 1)
                pe.wait_ge(sem("va"), b + 1)
                for hh in range(2):
                    j = 2 * jp + hh
                    mm = pe.matmul(ps[32 * j:32 * j + 32, 3, kt * P:S], va[:, b % 2, kt, 4 * g + j, :],
                                   pt[:, u % 3, hh, 0:n], start=(kt == 3), stop=True, skip_group_check=True)
                mm.then_inc(sem("pv"), 1)

            def o_T(s):
                pe.wait_ge(sem("ot"), s + 1)
                k = ring_bank("oT", s)
                for qt in range(4):
                    mm = pe.transpose(ps[:, k, qt * P:(qt + 1) * P], ot[:, qt * P:(qt + 1) * P], ident)
                mm.then_inc(sem("ring_ps"), 1)

            def a_T(b):
                pe.wait_ge(sem("at"), 4 * (b + 1))
                k = ring_bank("aT", b)
                for qt in range(4):
                    mm = pe.transpose(ps[:, k, qt * P:(qt + 1) * P], at[:, qt].rearrange("p h d -> p (h d)"), ident)
                mm.then_inc(sem("ring_ps"), 1)

            def attn_out(b):
                pe.wait_ge(sem("aT"), b + 1)
                k = ring_bank("ao", b)
                for qt in range(4):
                    mm = pe.matmul(ps[:, k, qt * P:(qt + 1) * P], aT[:, qt * P:(qt + 1) * P], w["wo"], start=True,
                                   stop=True)
                mm.then_inc(sem("ring_ps"), 1)

            for b in range(2):
                for j in range(4):
                    if b > 0:
                        project(b, j)
                project_values(b)
            for it in range(-2, 17):
                if it == -1:
                    transposes(3, 2, bank=4)
                    transposes(3, 3, bank=4)
                for i in range(8):
                    if it + 2 < 16:
                        for u in at_slot[i]:
                            scores(it + 2, u)
                    if 0 <= it < 16:
                        scores_T(8 * it + i)
                    if 0 <= 8 * it + i - 2 < 128:
                        weighted_values(8 * it + i - 2)
                    if i == 2 and 0 <= it + 1 < 16:
                        maxima_T(it + 1)
                    if i == 3 and 0 <= it - 1:
                        o_T(it - 1)
                    if i == 5 and it >= 4 and it % 4 == 0:
                        a_T(it // 4 - 1)
                    if i == 7 and it >= 4 and it % 4 == 0:
                        attn_out(it // 4 - 1)
                    if it in (2, 6) and i % 2 == 0:
                        project((it + 6) // 4, i // 2)
                    if it in (4, 8) and i == 6:
                        project_values((it + 4) // 4)

            pe.wait_ge(sem("probs"), 128)
            pe.wait_ge(sem("ld_moe1"), 16)
            router(4, w["wr"], "gate1_ps")
            pe.wait_ge(sem("route"), ROUTE1)
            hot = rt[:, 5].rearrange("p t e -> p e t")
            pe.matmul(ps[:, 7, 0:NT * E1], w["tri"], hot, start=True, stop=True)
            pe.matmul(ps[:, 7, NT * E1:2 * NT * E1], ones[:, :], hot, start=True, stop=True).then_inc(sem("rank_ps"), 1)
            pe.wait_ge(sem("expert_at"), 1)
            at_w = {}
            for i in range(-1, NBLK + 1):
                if 0 <= i + 1 < NBLK:
                    j = i + 1
                    for c, js in enumerate(BLOCK_GROUPS):
                        if js.start == j:
                            pe.wait_ge(sem(f"ld_moe1_{c}"), 16)
                    if j >= 2:
                        pe.wait_ge(sem("xT"), j - 1)
                    pe.transpose(ps[:, 2 + j % 2, 0:P], xb[:, j, 0:D], ident).then_inc(sem("xT_ps"), 1)
                if 0 <= i < NBLK:
                    j = i
                    at_w[j] = pe.value_load(expert_at[0:1, j:j + 1], min_val=0, max_val=(E1 - 1) * HID)
                    pe.wait_ge(sem("xT"), j + 1)
                    pe.wait_ge(sem("w1"), j + 1)
                    if j >= 2:
                        pe.wait_ge(sem("h1"), DENSE + j - 1)
                    for q in range(4):
                        mm = pe.matmul(ps[:, j % 2, q * P:(q + 1) * P], w1[:, j % 2, q * P:(q + 1) * P],
                                       xT[:, j % 2, :], start=True, stop=True)
                    mm.then_inc(sem("p1_ps"), 1)
                if 0 <= i - 1 < NBLK:
                    j = i - 1
                    pe.wait_ge(sem("h1"), DENSE + j + 1)
                    if j >= 2:
                        pe.wait_ge(sem("pr"), DENSE + j - 1)
                    elif j == 0:
                        pe.wait_ge(sem("posu"), 1)
                    for q in range(4):
                        mm = pe.matmul(ps[:, 6 + j % 2, 0:D], gs[:, j % 2, q * P:(q + 1) * P],
                                       w["W2"][:, bass.ds(at_w[j] + q * D, D)], start=(q == 0), stop=(q == 3))
                    mm.then_inc(sem("p2_ps"), 1)


def shape_constants():
    import numpy as np

    k = np.arange(P)
    pos = np.arange(S, dtype=np.float32)
    inv = np.float32(10000.0) ** (-np.arange(0, DK, 2, dtype=np.float32) / np.float32(DK))
    ang = (pos[:, None] * inv[None, :]).astype(np.float32)
    d = np.arange(P) % DK
    cos = np.cos(ang)[:, d // 2].T
    sin = np.sin(ang)[:, d // 2].T * np.where(d % 2 == 0, -1.0, 1.0)[:, None]
    mask = np.zeros((P, 4 * P), np.float32)
    mask[:, 3 * P:4 * P] = np.where(k[None, :] > k[:, None], NEG, 0.0)
    const = {
        "ident": np.eye(P), "tri": k[:, None] <= k[None, :], "after": k[:, None] > k[None, :],
        "cos": cos, "sin": sin, "iota": np.broadcast_to(8.0 - np.arange(8), (P, 8)), "mask": mask,
        "segment": np.broadcast_to(np.arange(NT * E1) % NT > 0, (P, NT * E1)),
        "full": np.broadcast_to(P * np.arange(NT), (P, NT)),
        "block": np.broadcast_to(np.arange(NBLK), (P, NBLK)),
        "number": 1 + k[:, None] + P * np.arange(NT)[None, :],
        "spare": 1 + NTOK + k[:, None] + P * np.arange(NBLK)[None, :],
    }
    sel0 = np.zeros((P, 8, P))
    for e in range(8):
        for piece in range(3):
            sel0[8 * piece + e, e, :] = 1.0
    bconst = {
        "identb": np.eye(P), "causal": np.where(k[:, None] > k[None, :], NEG, 0.0),
        "sel0": sel0.reshape(P, -1),
    }
    fc = np.concatenate([np.asarray(const[n], np.float32) for n, _ in PACKS["const"]], axis=1)
    bc = np.concatenate([np.asarray(bconst[n], np.float32) for n, _ in BPACK], axis=1).astype(np.dtype("bfloat16"))
    kones = np.zeros((6, NH, S), np.float32)
    kones[0:3, 0::2] = 1.0
    kones[3:6, 1::2] = 1.0
    return fc, bc, kones.astype(np.dtype("bfloat16"))


def lay_out(i):
    import numpy as np

    a = {k: np.asarray(v) for k, v in i.items()}

    def rows(v):
        return np.broadcast_to(v, (P, v.shape[-1]))

    def cols(v):
        return v.reshape(-1, P).T

    def experts(wt):
        return wt.transpose(2, 0, 1).reshape(P, -1)

    fields = {
        "cT": np.concatenate([a["L0_c"].T, a["L1_c"].T], axis=1),
        "wmod0": a["L0_wmod"], "wmod1": a["L1_wmod"],
        "norm_w": cols(a["L0_attn_norm_w"]), "norm_b": cols(a["L0_attn_norm_b"]),
        "in_proj": a["L0_attn_in_proj_w"].T,
        "conv_w": a["L0_attn_conv_w"].reshape(4, P, TAPS).transpose(1, 0, 2).reshape(P, -1),
        "conv_b": cols(a["L0_attn_conv_b"]),
        "dt_bias": rows(a["L0_attn_dt_bias"]), "A_log": rows(a["L0_attn_A_log"]), "D": rows(a["L0_attn_D"]),
        "rms_w": cols(a["L0_attn_rms_w"]),
        "out_proj": a["L0_attn_out_proj_w"].T.reshape(2, P, D).transpose(1, 0, 2).reshape(P, -1),
        "gate": a["L0_ffn_gate_w"].T,
        "w1": experts(a["L0_ffn_w1"]), "w2": experts(a["L0_ffn_w2"]), "w3": experts(a["L0_ffn_w3"]),
        "b1": a["L0_ffn_b1"].T, "b2": a["L0_ffn_b2"].T, "b3": a["L0_ffn_b3"].T,
        "sw1": a["L0_ffn_sw1"].T, "sw2": a["L0_ffn_sw2"].T,
        "sw3": a["L0_ffn_sw3"].T.reshape(2, P, D).transpose(1, 0, 2).reshape(P, -1),
        "wr": a["L1_ffn_Wr"],
        "W1": a["L1_ffn_W1"].transpose(1, 0, 2).reshape(P, -1),
        "W2": a["L1_ffn_W2"].reshape(E1, 4, P, D).transpose(2, 0, 1, 3).reshape(P, -1),
    }
    swap = np.arange(P) ^ 1
    for n in "qkvo":
        wt = a[f"L1_attn_W_{n}"]
        fields["w" + n] = wt.T
        if n in "qk":
            fields["w" + n + "s"] = wt[swap].T
    packs = {
        f"{pack}_in": np.ascontiguousarray(np.concatenate([fields[n] for n, _ in PACKS[pack]], axis=1))
        for pack in ("mod", "mixw", "moe0", "attn", "moe1")
    }
    packs["x_in"] = np.ascontiguousarray(a["L0_attn_x"].reshape(NT, P, D).transpose(1, 0, 2))
    packs["const_in"], packs["bconst_in"], packs["kones_in"] = shape_constants()
    return packs


def kernel(**inputs):
    import concourse.bacc as bacc
    import numpy as np
    from concourse.bass_utils import run_bass_kernel_spmd

    nc = bacc.Bacc("TRN2", target_bir_lowering=False, num_devices=1)
    arrays = lay_out(inputs)
    args = {n: nc.dram_tensor(n, v.shape, mybir.dt.from_np(v.dtype), kind="ExternalInput").ap()
            for n, v in arrays.items()}
    out = nc.dram_tensor("y_out", (P, NT, D), F32, kind="ExternalOutput").ap()
    adaln_kernel(nc, out=out, **args)
    got = run_bass_kernel_spmd(nc, [arrays], core_ids=[0]).results[0]["y_out"]
    return np.ascontiguousarray(np.asarray(got).transpose(1, 0, 2)).reshape(B, S, D)
```
